# Optimizing a Trainium2 kernel written in Bass

```python
import numpy as np
import jax
import jax.numpy as jnp

def _softmax(x, axis=-1):
    return jax.nn.softmax(x, axis=axis)

def _gelu(x):
    return jax.nn.gelu(x, approximate=True)

def _silu(x):
    return jax.nn.silu(x)

def _sigmoid(x):
    return jax.nn.sigmoid(x)

def _layernorm(x, axis=-1, eps=1e-05):
    m = jnp.mean(x, axis=axis, keepdims=True)
    v = jnp.var(x, axis=axis, keepdims=True)
    return (x - m) / jnp.sqrt(v + eps)

def _scatter_add(tgt, idx, src, axis=0):
    return tgt.at[idx].add(src)

def _segment_sum(src, seg, n):
    return jax.ops.segment_sum(src, seg, n)
kernel_name = 'mk_recurrent_d2_jaxref_r8_dbd04b'

def setup_inputs(seed: int=0):
    np.random.seed(seed)
    _w = jnp.asarray

    def _L0_attn_setup():
        import jax, jax.numpy as jnp
        import numpy as np
        EMBED_DIM = 128
        NUM_HEADS = 16
        HEAD_DIM = EMBED_DIM // NUM_HEADS
        NUM_DECAYS = 2
        BATCH = 2
        SEQ = 256
        W_SCALE = 0.02
        key = jax.random.key(seed)
        ks = jax.random.split(key, 12)
        d = EMBED_DIM
        inp = {'x': jax.random.normal(ks[0], (BATCH, SEQ, d), dtype=jnp.float32), 'Wq': jax.random.normal(ks[1], (d, d), dtype=jnp.float32) * W_SCALE, 'bq': jnp.zeros((d,), dtype=jnp.float32), 'Wk': jax.random.normal(ks[2], (d, d), dtype=jnp.float32) * W_SCALE, 'bk': jnp.zeros((d,), dtype=jnp.float32), 'Wv': jax.random.normal(ks[3], (d, d), dtype=jnp.float32) * W_SCALE, 'bv': jnp.zeros((d,), dtype=jnp.float32), 'Wo': jax.random.normal(ks[4], (d, d), dtype=jnp.float32) * W_SCALE, 'bo': jnp.zeros((d,), dtype=jnp.float32), 'decay_params': jax.random.uniform(ks[5], (NUM_HEADS, NUM_DECAYS), dtype=jnp.float32), 'mix_weights': jax.random.normal(ks[6], (NUM_HEADS, NUM_DECAYS), dtype=jnp.float32)}
        return inp
    _L0_attn_in = _L0_attn_setup()

    def _L0_ffn_setup():
        import jax, jax.numpy as jnp
        import numpy as np
        D_MODEL = 128
        NUM_HEADS = 4
        NUM_EXPERTS = 8
        TOP_K = 2
        D_FF = 128
        EPS = 1e-06

        def _rmsnorm(x, g):
            return x * jax.lax.rsqrt(jnp.mean(x * x, axis=-1, keepdims=True) + EPS) * g

        def _swiglu(x, w1, w2, w3):
            return jax.nn.silu(x @ w1.T) * (x @ w3.T) @ w2.T
        key = jax.random.key(seed)
        ks = jax.random.split(key, 16)
        d, e, f = (D_MODEL, NUM_EXPERTS, D_FF)
        dc = d // 4
        s = 0.02
        return {'X': jax.random.normal(ks[0], (2, 128, d), dtype=jnp.float32), 'g1': jnp.ones((d,), jnp.float32), 'g2': jnp.ones((d,), jnp.float32), 'Wq': jax.random.normal(ks[1], (d, d), jnp.float32) * s, 'Wkc': jax.random.normal(ks[2], (dc, d), jnp.float32) * s, 'Wvc': jax.random.normal(ks[3], (dc, d), jnp.float32) * s, 'Wo': jax.random.normal(ks[4], (d, d), jnp.float32) * s, 'Wr': jax.random.normal(ks[5], (e, d), jnp.float32) * s, 'expert_bias': jnp.zeros((e,), jnp.float32), 'sW1': jax.random.normal(ks[6], (f, d), jnp.float32) * s, 'sW2': jax.random.normal(ks[7], (d, f), jnp.float32) * s, 'sW3': jax.random.normal(ks[8], (f, d), jnp.float32) * s, 'eW1': jax.random.normal(ks[9], (e, f, d), jnp.float32) * s, 'eW2': jax.random.normal(ks[10], (e, d, f), jnp.float32) * s, 'eW3': jax.random.normal(ks[11], (e, f, d), jnp.float32) * s}
    _L0_ffn_in = _L0_ffn_setup()

    def _L1_attn_setup():
        import jax, jax.numpy as jnp
        import numpy as np
        B, T, D = (8, 256, 128)
        H, N = (8, 32)

        def _xavier(key, shape, fan_in, fan_out):
            lim = float(np.sqrt(6.0 / (fan_in + fan_out)))
            return jax.random.uniform(key, shape, jnp.float32, -lim, lim)

        def _reference_tuple_inner(x, W_in, W_k, W_v, W_q, W_beta, b_beta, W_out):
            b, t, d = x.shape
            h, n = b_beta.shape
            xp = jax.nn.silu(jnp.einsum('btd,ed->bte', x, W_in))

            def proj(W):
                return jnp.einsum('btd,md->btm', xp, W).reshape(b, t, h, n).transpose(1, 0, 2, 3)
            k_all = proj(W_k)
            v_all = proj(W_v)
            q_all = proj(W_q)
            beta_all = jax.nn.sigmoid(proj(W_beta) + b_beta)
            S0 = jnp.zeros((b, h, n, n), x.dtype)

            def step(S, inp):
                k, v, q, beta = inp
                kn = k / (jnp.linalg.norm(k, axis=-1, keepdims=True) + 1e-06)
                retrieved = jnp.einsum('bhij,bhj->bhi', S, kn)
                delta = v - retrieved
                S = jnp.tanh(beta[..., None] * S + delta[..., None] * kn[..., None, :])
                Sq = jnp.einsum('bhij,bhj->bhi', S, q)
                out = Sq * jax.nn.silu(Sq)
                return (S, out)
            S_final, outs = jax.lax.scan(step, S0, (k_all, v_all, q_all, beta_all))
            cell_out = outs.transpose(1, 0, 2, 3).reshape(b, t, h * n)
            y = jnp.einsum('btm,dm->btd', cell_out, W_out)
            return (y, S_final)
        key = jax.random.key(seed)
        ks = jax.random.split(key, 8)
        x = jax.random.normal(ks[0], (B, T, D), jnp.float32)
        W_in = _xavier(ks[1], (D, D), D, D)
        W_k = _xavier(ks[2], (H * N, D), N, D)
        W_v = _xavier(ks[3], (H * N, D), N, D)
        W_q = _xavier(ks[4], (H * N, D), N, D)
        W_beta = _xavier(ks[5], (H * N, D), N, D)
        b_beta = jnp.full((H, N), 2.0, jnp.float32)
        W_out = _xavier(ks[6], (D, H * N), H * N, D)
        return {'x': x, 'W_in': W_in, 'W_k': W_k, 'W_v': W_v, 'W_q': W_q, 'W_beta': W_beta, 'b_beta': b_beta, 'W_out': W_out}
    _L1_attn_in = _L1_attn_setup()

    def _L1_ffn_setup():
        import jax, jax.numpy as jnp
        import numpy as np
        H = 128
        I = 64
        E = 64
        K = 2
        EPS = 1e-06
        CAP = 128

        def _rmsnorm(x, w, eps=EPS):
            v = jnp.mean(x.astype(jnp.float32) ** 2, axis=-1, keepdims=True)
            return (x.astype(jnp.float32) * jax.lax.rsqrt(v + eps)).astype(x.dtype) * w
        key = jax.random.key(seed)
        ks = jax.random.split(key, 8)
        B, S = (2, 512)
        s_h = 1.0 / np.sqrt(H)
        s_i = 1.0 / np.sqrt(I)
        return {'hidden_states': jax.random.normal(ks[0], (B, S, H), jnp.float32), 'rms_w': jnp.ones((H,), jnp.float32), 'gate_w': jax.random.normal(ks[1], (E, H), jnp.float32) * s_h, 'w13': jax.random.normal(ks[2], (E, H, 2 * I), jnp.float32) * s_h, 'w2': jax.random.normal(ks[3], (E, I, H), jnp.float32) * s_i, 'sw_gate': jax.random.normal(ks[4], (H, I), jnp.float32) * s_h, 'sw_up': jax.random.normal(ks[5], (H, I), jnp.float32) * s_h, 'sw_down': jax.random.normal(ks[6], (I, H), jnp.float32) * s_i}
    _L1_ffn_in = _L1_ffn_setup()
    _d = {'L0_attn_x': _L0_attn_in['x'], 'L0_attn_Wq': _L0_attn_in['Wq'], 'L0_attn_bq': _L0_attn_in['bq'], 'L0_attn_Wk': _L0_attn_in['Wk'], 'L0_attn_bk': _L0_attn_in['bk'], 'L0_attn_Wv': _L0_attn_in['Wv'], 'L0_attn_bv': _L0_attn_in['bv'], 'L0_attn_Wo': _L0_attn_in['Wo'], 'L0_attn_bo': _L0_attn_in['bo'], 'L0_attn_decay_params': _L0_attn_in['decay_params'], 'L0_attn_mix_weights': _L0_attn_in['mix_weights'], 'L0_ffn_g1': _L0_ffn_in['g1'], 'L0_ffn_g2': _L0_ffn_in['g2'], 'L0_ffn_Wq': _L0_ffn_in['Wq'], 'L0_ffn_Wkc': _L0_ffn_in['Wkc'], 'L0_ffn_Wvc': _L0_ffn_in['Wvc'], 'L0_ffn_Wo': _L0_ffn_in['Wo'], 'L0_ffn_Wr': _L0_ffn_in['Wr'], 'L0_ffn_expert_bias': _L0_ffn_in['expert_bias'], 'L0_ffn_sW1': _L0_ffn_in['sW1'], 'L0_ffn_sW2': _L0_ffn_in['sW2'], 'L0_ffn_sW3': _L0_ffn_in['sW3'], 'L0_ffn_eW1': _L0_ffn_in['eW1'], 'L0_ffn_eW2': _L0_ffn_in['eW2'], 'L0_ffn_eW3': _L0_ffn_in['eW3'], 'L1_attn_W_in': _L1_attn_in['W_in'], 'L1_attn_W_k': _L1_attn_in['W_k'], 'L1_attn_W_v': _L1_attn_in['W_v'], 'L1_attn_W_q': _L1_attn_in['W_q'], 'L1_attn_W_beta': _L1_attn_in['W_beta'], 'L1_attn_b_beta': _L1_attn_in['b_beta'], 'L1_attn_W_out': _L1_attn_in['W_out'], 'L1_ffn_rms_w': _L1_ffn_in['rms_w'], 'L1_ffn_gate_w': _L1_ffn_in['gate_w'], 'L1_ffn_w13': _L1_ffn_in['w13'], 'L1_ffn_w2': _L1_ffn_in['w2'], 'L1_ffn_sw_gate': _L1_ffn_in['sw_gate'], 'L1_ffn_sw_up': _L1_ffn_in['sw_up'], 'L1_ffn_sw_down': _L1_ffn_in['sw_down']}
    _x0 = _d['L0_attn_x']
    _d['L0_attn_x'] = jax.random.normal(jax.random.fold_in(jax.random.key(seed), 1), (1, 2048, 128), dtype=_x0.dtype)
    del _x0
    return _d

def reference(L0_attn_x, L0_attn_Wq, L0_attn_bq, L0_attn_Wk, L0_attn_bk, L0_attn_Wv, L0_attn_bv, L0_attn_Wo, L0_attn_bo, L0_attn_decay_params, L0_attn_mix_weights, L0_ffn_g1, L0_ffn_g2, L0_ffn_Wq, L0_ffn_Wkc, L0_ffn_Wvc, L0_ffn_Wo, L0_ffn_Wr, L0_ffn_expert_bias, L0_ffn_sW1, L0_ffn_sW2, L0_ffn_sW3, L0_ffn_eW1, L0_ffn_eW2, L0_ffn_eW3, L1_attn_W_in, L1_attn_W_k, L1_attn_W_v, L1_attn_W_q, L1_attn_W_beta, L1_attn_b_beta, L1_attn_W_out, L1_ffn_rms_w, L1_ffn_gate_w, L1_ffn_w13, L1_ffn_w2, L1_ffn_sw_gate, L1_ffn_sw_up, L1_ffn_sw_down):

    def _L0_attn_ref(x, Wq, bq, Wk, bk, Wv, bv, Wo, bo, decay_params, mix_weights):
        import jax, jax.numpy as jnp
        import numpy as np
        EMBED_DIM = 128
        NUM_HEADS = 16
        HEAD_DIM = EMBED_DIM // NUM_HEADS
        NUM_DECAYS = 2
        BATCH = 2
        SEQ = 256
        W_SCALE = 0.02
        B, S, _ = x.shape
        H, D = (NUM_HEADS, HEAD_DIM)

        def proj(W, b):
            return (jnp.einsum('bse,fe->bsf', x, W) + b).reshape(B, S, H, D).transpose(0, 2, 1, 3)
        q = proj(Wq, bq)
        k = proj(Wk, bk)
        v = proj(Wv, bv)
        attn_scores = jnp.einsum('bhqd,bhkd->bhqk', q, k) / jnp.sqrt(jnp.float32(D))
        t = jnp.arange(S, dtype=jnp.float32)
        time_diffs = jnp.abs(t[:, None] - t[None, :])
        dp = jnp.clip(decay_params, 0.01, 0.9999)
        decay_masks = dp[:, :, None, None] ** time_diffs[None, None, :, :]
        mix = jax.nn.softmax(mix_weights, axis=-1)
        decay_mask = jnp.einsum('hnqk,hn->hqk', decay_masks, mix)
        attn_scores = attn_scores * decay_mask[None]
        attn_probs = jax.nn.softmax(attn_scores, axis=-1)
        out = jnp.einsum('bhqk,bhkd->bhqd', attn_probs, v)
        out = out.transpose(0, 2, 1, 3).reshape(B, S, H * D)
        return jnp.einsum('bse,fe->bsf', out, Wo) + bo

    def _L0_ffn_ref(X, g1, g2, Wq, Wkc, Wvc, Wo, Wr, expert_bias, sW1, sW2, sW3, eW1, eW2, eW3):
        import jax, jax.numpy as jnp
        import numpy as np
        D_MODEL = 128
        NUM_HEADS = 4
        NUM_EXPERTS = 8
        TOP_K = 2
        D_FF = 128
        EPS = 1e-06

        def _rmsnorm(x, g):
            return x * jax.lax.rsqrt(jnp.mean(x * x, axis=-1, keepdims=True) + EPS) * g

        def _swiglu(x, w1, w2, w3):
            return jax.nn.silu(x @ w1.T) * (x @ w3.T) @ w2.T
        B, S, d = X.shape
        H = NUM_HEADS
        dk = d // H
        scale = 1.0 / jnp.sqrt(jnp.float32(dk))
        nx = _rmsnorm(X, g1)
        Q = (nx @ Wq.T).reshape(B, S, H, dk).transpose(0, 2, 1, 3)
        Kc = nx @ Wkc.T
        Vc = nx @ Wvc.T
        scores = jnp.einsum('bhsd,btd->bhst', Q, Kc) * scale
        attn = jax.nn.softmax(scores, axis=-1)
        out = jnp.einsum('bhst,btd->bhsd', attn, Vc)
        out = out.transpose(0, 2, 1, 3).reshape(B, S, d) @ Wo.T
        X = X + out
        nx = _rmsnorm(X, g2)
        xf = nx.reshape(-1, d)
        logits = xf @ Wr.T + expert_bias
        rw = jax.nn.softmax(logits, axis=-1)
        topw, topi = jax.lax.top_k(rw, TOP_K)
        topw = jax.nn.softmax(topw, axis=-1)
        combine = jnp.sum(jax.nn.one_hot(topi, NUM_EXPERTS, dtype=xf.dtype) * topw[..., None], axis=1)
        shared = _swiglu(xf, sW1, sW2, sW3)
        h = jax.nn.silu(jnp.einsum('td,efd->etf', xf, eW1)) * jnp.einsum('td,efd->etf', xf, eW3)
        eo = jnp.einsum('etf,edf->etd', h, eW2)
        specialist = jnp.einsum('te,etd->td', combine, eo)
        moe_out = (shared + specialist).reshape(B, S, d)
        return X + moe_out

    def _L1_attn_ref(x, W_in, W_k, W_v, W_q, W_beta, b_beta, W_out):
        import jax, jax.numpy as jnp
        import numpy as np
        B, T, D = (8, 256, 128)
        H, N = (8, 32)

        def _xavier(key, shape, fan_in, fan_out):
            lim = float(np.sqrt(6.0 / (fan_in + fan_out)))
            return jax.random.uniform(key, shape, jnp.float32, -lim, lim)

        def _reference_tuple_inner(x, W_in, W_k, W_v, W_q, W_beta, b_beta, W_out):
            b, t, d = x.shape
            h, n = b_beta.shape
            xp = jax.nn.silu(jnp.einsum('btd,ed->bte', x, W_in))

            def proj(W):
                return jnp.einsum('btd,md->btm', xp, W).reshape(b, t, h, n).transpose(1, 0, 2, 3)
            k_all = proj(W_k)
            v_all = proj(W_v)
            q_all = proj(W_q)
            beta_all = jax.nn.sigmoid(proj(W_beta) + b_beta)
            S0 = jnp.zeros((b, h, n, n), x.dtype)

            def step(S, inp):
                k, v, q, beta = inp
                kn = k / (jnp.linalg.norm(k, axis=-1, keepdims=True) + 1e-06)
                retrieved = jnp.einsum('bhij,bhj->bhi', S, kn)
                delta = v - retrieved
                S = jnp.tanh(beta[..., None] * S + delta[..., None] * kn[..., None, :])
                Sq = jnp.einsum('bhij,bhj->bhi', S, q)
                out = Sq * jax.nn.silu(Sq)
                return (S, out)
            S_final, outs = jax.lax.scan(step, S0, (k_all, v_all, q_all, beta_all))
            cell_out = outs.transpose(1, 0, 2, 3).reshape(b, t, h * n)
            y = jnp.einsum('btm,dm->btd', cell_out, W_out)
            return (y, S_final)
        return _reference_tuple_inner(x, W_in, W_k, W_v, W_q, W_beta, b_beta, W_out)[0]

    def _L1_ffn_ref(hidden_states, rms_w, gate_w, w13, w2, sw_gate, sw_up, sw_down):
        import jax, jax.numpy as jnp
        import numpy as np
        H = 128
        I = 64
        E = 64
        K = 2
        EPS = 1e-06
        CAP = 128

        def _rmsnorm(x, w, eps=EPS):
            v = jnp.mean(x.astype(jnp.float32) ** 2, axis=-1, keepdims=True)
            return (x.astype(jnp.float32) * jax.lax.rsqrt(v + eps)).astype(x.dtype) * w
        B, S, Hh = hidden_states.shape
        residual = hidden_states
        x = _rmsnorm(hidden_states, rms_w).reshape(-1, Hh)
        T = x.shape[0]
        logits = x.astype(jnp.float32) @ gate_w.astype(jnp.float32).T
        probs = jax.nn.softmax(logits, axis=-1)
        topk_w, topk_ids = jax.lax.top_k(probs, K)
        topk_w = (topk_w / jnp.sum(topk_w, axis=-1, keepdims=True)).astype(x.dtype)
        flat_e = topk_ids.reshape(-1)
        order = jnp.argsort(flat_e)
        se = flat_e[order]
        tok = order // K
        counts = jax.ops.segment_sum(jnp.ones_like(se, jnp.int32), se, num_segments=E)
        starts = jnp.cumsum(counts) - counts
        pos = jnp.arange(se.shape[0]) - starts[se]
        pos_c = jnp.minimum(pos, CAP)
        buf = jnp.zeros((E, CAP + 1, Hh), x.dtype).at[se, pos_c].set(x[tok])
        xb = buf[:, :CAP]
        gu = jnp.einsum('ech,ehf->ecf', xb, w13)
        g, u = jnp.split(gu, 2, axis=-1)
        hact = jax.nn.silu(g) * u
        yb = jnp.einsum('eci,eih->ech', hact, w2)
        yb = jnp.concatenate([yb, jnp.zeros((E, 1, Hh), yb.dtype)], axis=1)
        y_slot = yb[se, pos_c]
        w_slot = topk_w.reshape(-1)[order]
        moe_out = jnp.zeros((T, Hh), x.dtype).at[tok].add(w_slot[:, None] * y_slot)
        shared = jax.nn.silu(x @ sw_gate) * (x @ sw_up) @ sw_down
        out = (moe_out + shared).reshape(B, S, Hh) + residual
        return out
    x = L0_attn_x
    xn = _layernorm(x, axis=-1)
    s = _L0_attn_ref(xn, L0_attn_Wq, L0_attn_bq, L0_attn_Wk, L0_attn_bk, L0_attn_Wv, L0_attn_bv, L0_attn_Wo, L0_attn_bo, L0_attn_decay_params, L0_attn_mix_weights)
    g = _silu(_L0_ffn_ref(xn, L0_ffn_g1, L0_ffn_g2, L0_ffn_Wq, L0_ffn_Wkc, L0_ffn_Wvc, L0_ffn_Wo, L0_ffn_Wr, L0_ffn_expert_bias, L0_ffn_sW1, L0_ffn_sW2, L0_ffn_sW3, L0_ffn_eW1, L0_ffn_eW2, L0_ffn_eW3))
    x = x + s * g
    xn = _layernorm(x, axis=-1)
    s = _L1_attn_ref(xn, L1_attn_W_in, L1_attn_W_k, L1_attn_W_v, L1_attn_W_q, L1_attn_W_beta, L1_attn_b_beta, L1_attn_W_out)
    g = _silu(_L1_ffn_ref(xn, L1_ffn_rms_w, L1_ffn_gate_w, L1_ffn_w13, L1_ffn_w2, L1_ffn_sw_gate, L1_ffn_sw_up, L1_ffn_sw_down))
    x = x + s * g
    return x

_drawn_inputs = setup_inputs


def setup_inputs(seed=0):
    import zlib

    import numpy as np

    out = dict(_drawn_inputs(seed))
    spreads = {'L0_attn_bq': (0.0, 0.8),
     'L0_attn_bk': (0.0, 0.8),
     'L0_attn_bv': (0.0, 0.1),
     'L0_attn_bo': (0.0, 0.1),
     'L0_ffn_g1': (1.0, 0.6),
     'L0_ffn_g2': (1.0, 0.6),
     'L0_ffn_expert_bias': (0.0, 0.8),
     'L1_attn_b_beta': (2.0, 0.2),
     'L1_ffn_rms_w': (1.0, 0.2)}
    factors = {'L0_attn_Wq': 8.0,
     'L0_attn_Wk': 8.0,
     'L0_attn_Wv': 8.0,
     'L0_attn_decay_params': 8.0,
     'L0_attn_mix_weights': 8.0,
     'L0_ffn_Wq': 8.0,
     'L0_ffn_Wkc': 8.0,
     'L0_ffn_Wvc': 8.0,
     'L0_ffn_Wo': 8.0,
     'L0_ffn_Wr': 8.0,
     'L0_ffn_sW1': 8.0,
     'L0_ffn_sW2': 8.0,
     'L0_ffn_sW3': 8.0,
     'L0_ffn_eW1': 8.0,
     'L0_ffn_eW2': 8.0,
     'L0_ffn_eW3': 8.0}
    for name, (base, spread) in spreads.items():
        noise = np.random.default_rng([zlib.crc32(name.encode()), seed]).standard_normal(out[name].shape)
        drawn = base * np.exp(spread * noise) if base else spread * noise
        out[name] = jnp.asarray(drawn.astype(out[name].dtype))
    for name, factor in factors.items():
        out[name] = (out[name] * factor).astype(out[name].dtype)
    return out
```

```python
from contextlib import ExitStack

import numpy as np
import concourse.bass as bass
from concourse import mybir

F32 = mybir.dt.float32
BF16 = mybir.dt.bfloat16
ALU = mybir.AluOpType
ACT = mybir.ActivationFunctionType
AX = mybir.AxisListType

P = 128
D = 128
T = 2048
NT = T // P
QT = 512
NQ = T // QT
GW = 2 * QT - P
LEAST = -3.0e38
SPLIT_K = (0, 0, 0, 1, 1, 2)
SPLIT_Q = (0, 1, 2, 0, 1, 0)


class Links:

    def __init__(self, engine, sem):
        self.engine, self.sem, self.n = engine, sem, 0

    def __call__(self, ins):
        ins.then_inc(self.sem, 1)
        self.n += 1
        self.engine.wait_ge(self.sem, self.n)


class Shared:
    pass


class Room:

    def __init__(self, nc, ctx, tag):
        self.nc, self.ctx, self.tag = nc, ctx, tag
        ctx.enter_context(nc.cleanup_on_exit())

    def sb(self, name, shape, dt=F32):
        return self.ctx.enter_context(self.nc.sbuf_tensor(f"{self.tag}_{name}", shape, dt))

    def psum(self):
        return self.ctx.enter_context(self.nc.psum_tensor(f"{self.tag}_ps", [P, 8, QT], F32))

    def sem(self, name):
        return self.nc.alloc_semaphore(name=f"{self.tag}_{name}")


def normalise(nc, dve, link, src, dst, tmp, st, center, eps, squares_ready, roots_ready, n):
    if center:
        link(nc.vector.tensor_reduce(st[:, 0, :], src[:, :, :], AX.X, ALU.add))
        link(nc.vector.tensor_scalar(st[:, 0, :], st[:, 0, :], 1.0 / D, None, ALU.mult))
        link(nc.vector.tensor_tensor(dst[:, :, :], src[:, :, :],
                                     st[:, 0, :].unsqueeze(2).to_broadcast([P, NT, D]), ALU.subtract))
        src = dst
    link(nc.vector.tensor_tensor(tmp[:, :, :], src[:, :, :], src[:, :, :], ALU.mult))
    link(nc.vector.tensor_reduce(st[:, 1, :], tmp[:, :, :], AX.X, ALU.add))
    nc.vector.tensor_scalar(st[:, 1, :], st[:, 1, :], 1.0 / D, eps, ALU.mult, ALU.add).then_inc(squares_ready, 1)
    dve.wait_ge(roots_ready, n + 1)
    link(nc.vector.reciprocal(st[:, 3, :], st[:, 2, :]))
    return nc.vector.tensor_tensor(dst[:, :, :], src[:, :, :],
                                   st[:, 3, :].unsqueeze(2).to_broadcast([P, NT, D]), ALU.mult)


def constants(nc, S, dram):
    with ExitStack() as ctx:
        R = Room(nc, ctx, "c")
        zeroed, placed, loaded = R.sem("zeroed"), R.sem("placed"), R.sem("loaded")
        block = ctx.enter_context(nc.Block())

        @block.sync
        def _(sp):
            for n, dst in (("bv", S.bv), ("bo", S.bo), ("rb", S.rbias)):
                sp.dma_start(dst[:, :], dram[n].partition_broadcast(P)).then_inc(loaded, 16)
            sp.wait_ge(loaded, 48)

        @block.gpsimd
        def _(pool):
            nc.gpsimd.memset(S.ident[:, :], 0.0).then_inc(zeroed, 1)
            nc.gpsimd.memset(S.selo[:, :], 0.0).then_inc(zeroed, 1)
            nc.gpsimd.memset(S.selo2[:, :], 0.0).then_inc(zeroed, 1)
            nc.gpsimd.memset(S.spread[:, :], 0.0).then_inc(zeroed, 1)
            nc.gpsimd.memset(S.low_row[:, :], -1.0).then_inc(zeroed, 1)
            pool.wait_ge(zeroed, 5)
            nc.gpsimd.affine_select(out=S.ident[:, :], in_=S.ident[:, :], compare_op=ALU.not_equal, fill=1.0,
                                    base=0, pattern=[[-1, P]], channel_multiplier=1).then_inc(placed, 1)
            for t, w in ((S.selo, 32), (S.selo2, 64)):
                for g in range(P // w):
                    nc.gpsimd.affine_select(out=t[:, :], in_=t[:, :], compare_op=ALU.not_equal, fill=1.0,
                                            base=-w * g, pattern=[[-1, w]], channel_multiplier=1).then_inc(placed, 1)
                    pool.wait_ge(placed, 1 + g + 1 + (4 if w == 64 else 0))
            nc.gpsimd.memset(S.spread[96:98, :], 1.0).then_inc(placed, 1)
            nc.gpsimd.affine_select(out=S.low_row[:, :], in_=S.low_row[:, :], compare_op=ALU.is_gt, fill=0.0,
                                    base=0, pattern=[[0, 1]], channel_multiplier=1).then_inc(placed, 1)
            pool.wait_ge(placed, 9)


def prepare(nc, S, dram):
    with ExitStack() as ctx:
        R = Room(nc, ctx, "p")
        x, nx = R.sb("x", [P, NT, D]), R.sb("nx", [P, NT, D])
        tmp, st = R.sb("tmp", [P, NT, D]), R.sb("st", [P, 4, NT])
        n1T = R.sb("n1T", [P, T])
        W = R.sb("W", [P, 6, D])
        Wd = R.sb("Wd", [P, 4, D])
        prow = R.sb("prow", [1, 2, D])
        pdup = R.sb("pdup", [1, 9, D])
        dec = R.sb("dec", [1, 12, 32])
        one = R.sb("one", [1, P])
        cols = S.cols
        ps = R.psum()
        x_loaded, w_loaded, par_loaded = R.sem("x_loaded"), R.sem("w_loaded"), R.sem("par_loaded")
        squares, roots = R.sem("squares"), R.sem("roots")
        linked, xn_ready, nx_ready = R.sem("linked"), R.sem("xn_ready"), R.sem("nx_ready")
        wd_ready, clipped, logged = R.sem("wd_ready"), R.sem("clipped"), R.sem("logged")
        shifted, expd, rows_ready, cols_done, cols_kept = (R.sem(n) for n in ("shifted", "expd", "rows", "cols", "colk"))
        a_filled, a_kept, v_filled, v_kept = (R.sem(n) for n in ("a_filled", "a_kept", "v_filled", "v_kept"))
        block = ctx.enter_context(nc.Block())
        NA = 32

        @block.sync
        def _(sp):
            for t in range(NT):
                sp.dma_start(x[:, t, :], dram["x"][t * P:(t + 1) * P, :]).then_inc(x_loaded, 16)
            for n, name in enumerate(("WqT", "WkT", "WvT", "fWqT")):
                sp.dma_start(W[:, n, :], dram[name]).then_inc(w_loaded, 16)
            sp.dma_start(W[:, 4, 0:32], dram["WkcT"]).then_inc(w_loaded, 16)
            sp.dma_start(W[:, 5, 0:32], dram["WvcT"]).then_inc(w_loaded, 16)
            sp.dma_start(S.g[:, :], dram["g"]).then_inc(w_loaded, 16)
            sp.dma_start(prow[0:1, 0, :], dram["bq"].unsqueeze(0)).then_inc(par_loaded, 16)
            sp.dma_start(prow[0:1, 1, :], dram["bk"].unsqueeze(0)).then_inc(par_loaded, 16)
            sp.dma_start(dec[0:1, 0, :], dram["decay"].unsqueeze(0)).then_inc(par_loaded, 16)
            sp.dma_start(dec[0:1, 1, :], dram["mix"].unsqueeze(0)).then_inc(par_loaded, 16)
            sp.wait_ge(w_loaded, 16 * 7)
            sp.wait_ge(par_loaded, 16 * 4)

        @block.scalar
        def _(act):
            act.wait_ge(clipped, 1)
            nc.scalar.activation(dec[0:1, 3, :], dec[0:1, 2, :], ACT.Ln).then_inc(logged, 1)
            act.wait_ge(shifted, 1)
            nc.scalar.activation(dec[0:1, 5, :], dec[0:1, 4, :], ACT.Exp).then_inc(expd, 1)
            for n in range(2):
                act.wait_ge(squares, n + 1)
                nc.scalar.activation(st[:, 2, :], st[:, 1, :], ACT.Sqrt).then_inc(roots, 1)
            act.wait_ge(cols_done, 1)
            nc.scalar.activation(cols[:, :], ps[:, 7, 0:10], ACT.Copy).then_inc(cols_kept, 1)
            act.wait_ge(cols_kept, 1)
            dst = ([(S.xnT[:, :], None)] + [(n1T[:, :], S.g[:, 0:1])]
                   + [(S.Q2[:, i, :], cols[:, i:i + 1]) for i in range(2)]
                   + [(S.K2[:, i, :], cols[:, 2 + i:3 + i]) for i in range(2)] + [(S.QF[:, :], None), (S.KF[0:32, :], None)])
            for n in range(NA):
                out, par = dst[n // 4]
                rows = out.shape[0]
                out = out[:, (n % 4) * QT:(n % 4 + 1) * QT]
                act.wait_ge(a_filled, n + 1)
                src = ps[0:rows, n % 4, :]
                if par is None:
                    ins = nc.scalar.activation(out, src, ACT.Copy)
                elif n // 4 == 1:
                    ins = nc.scalar.activation(out, src, ACT.Copy, scale=par)
                else:
                    ins = nc.scalar.activation(out, src, ACT.Identity, bias=par)
                ins.then_inc(a_kept, 1)

        @block.tensor
        def _(pe):
            pe.wait_ge(rows_ready, 1)
            for c in range(9):
                nc.tensor.matmul(ps[:, 7, c:c + 1], pdup[0:1, c, :], one[0:1, 0:1], start=True, stop=True)
            last = nc.tensor.matmul(ps[:, 7, 9:10], one[0:1, :], one[0:1, 0:1], start=True, stop=True)
            last.then_inc(cols_done, 1)
            last = nc.tensor.matmul(ps[:, 6, 0:64], one[0:1, :], dec[0:1, 10:12, :], start=True, stop=True)
            last.then_inc(cols_done, 1)
            pe.wait_ge(w_loaded, 16 * 7)
            for n in range(NA):
                if n >= 4:
                    pe.wait_ge(a_kept, n - 3)
                kind, c = n // 4, n % 4
                if kind < 2:
                    pe.wait_ge((xn_ready, nx_ready)[kind], 1)
                    for j in range(4):
                        last = nc.tensor.transpose(ps[:, c, j * P:(j + 1) * P],
                                                   (S.xn, nx)[kind][:, 4 * c + j, :], S.ident[:, :])
                    last.then_inc(a_filled, 1)
                    continue
                if kind == 2 and c == 0:
                    pe.wait_ge(wd_ready, 1)
                if kind < 6:
                    w, r = Wd[:, kind - 2, :], S.xnT
                else:
                    w, r = (W[:, 3, :], W[:, 4, 0:32])[kind - 6], n1T
                rows = w.shape[1]
                nc.tensor.matmul(ps[0:rows, c, :], w, r[:, c * QT:(c + 1) * QT], start=True, stop=True).then_inc(a_filled, 1)
            for c in range(4):
                if c >= 2:
                    pe.wait_ge(v_kept, c - 1)
                for j in range(4):
                    t = 4 * c + j
                    last = nc.tensor.matmul(ps[:, 4 + c % 2, j * P:(j + 1) * P], S.xnT[:, t * P:(t + 1) * P], W[:, 2, :],
                                            start=True, stop=True)
                last.then_inc(v_filled, 1)
            pe.wait_ge(v_kept, 3)
            for t in range(NT):
                last = nc.tensor.matmul(ps[:, 4, t * 32:(t + 1) * 32], n1T[:, t * P:(t + 1) * P], W[:, 5, 0:32],
                                        start=True, stop=True)
            last.then_inc(v_filled, 1)

        @block.vector
        def _(dve):
            link = Links(dve, linked)
            link(nc.vector.memset(one[:, :], 1.0))
            link(nc.vector.memset(S.Vp[:, :, :, :], 0.0))
            link(nc.vector.memset(S.Vp[:, :, :, 8:9], 1.0))
            link(nc.vector.memset(S.Vcp[:, :, :], 0.0))
            link(nc.vector.memset(S.Vcp[:, :, 32:33], 1.0))
            dve.wait_ge(par_loaded, 64)
            nc.vector.tensor_scalar(dec[0:1, 2, :], dec[0:1, 0, :], 0.01, 0.9999, ALU.max, ALU.min).then_inc(clipped, 1)
            mix = dec[0:1, 1, :].rearrange("p (h n) -> p h n", n=2)
            link(nc.vector.tensor_reduce(dec[0:1, 6, 0:16], mix, AX.X, ALU.max))
            nc.vector.tensor_tensor(dec[0:1, 4, :].rearrange("p (h n) -> p h n", n=2), mix,
                                    dec[0:1, 6, 0:16].unsqueeze(2).to_broadcast([1, 16, 2]), ALU.subtract).then_inc(shifted, 1)
            dve.wait_ge(expd, 1)
            ex = dec[0:1, 5, :].rearrange("p (h n) -> p h n", n=2)
            link(nc.vector.tensor_reduce(dec[0:1, 7, 0:16], ex, AX.X, ALU.add))
            link(nc.vector.reciprocal(dec[0:1, 8, 0:16], dec[0:1, 7, 0:16]))
            link(nc.vector.tensor_tensor(dec[0:1, 11, :].rearrange("p (h n) -> p h n", n=2), ex,
                                         dec[0:1, 8, 0:16].unsqueeze(2).to_broadcast([1, 16, 2]), ALU.mult))
            dve.wait_ge(logged, 1)
            link(nc.vector.tensor_copy(dec[0:1, 10, :], dec[0:1, 3, :]))
            link(nc.vector.tensor_scalar(dec[0:1, 9, :], dec[0:1, 11, :], S.scale, None, ALU.mult))
            for i in range(2):
                for n in range(2):
                    def dup(c):
                        return pdup[0:1, c, :].rearrange("p (h n d) -> p h n d", n=2, d=8)[:, :, n, :]
                    for c in range(2):
                        link(nc.vector.tensor_copy(dup(2 * c + i), prow[0:1, c, 64 * i:64 * i + 64].rearrange("p (h d) -> p h d", d=8)))
                    for c, r in ((4, 10), (6, 9)):
                        v = dec[0:1, r, 16 * i:16 * i + 16].rearrange("p (h n) -> p h n", n=2)[:, :, n:n + 1]
                        link(nc.vector.tensor_copy(dup(c + i), v.to_broadcast([1, 8, 8])))
            link(nc.vector.memset(pdup[0:1, 8, :], 0.0))
            nc.vector.memset(pdup[0:1, 8, :].rearrange("p (h n d) -> p h n d", n=2, d=8)[:, :, 0, :], S.scale).then_inc(rows_ready, 1)
            dve.wait_ge(x_loaded, 16 * NT)
            normalise(nc, dve, link, x, S.xn, tmp, st, True, 1e-5, squares, roots, 0).then_inc(xn_ready, 1)
            dve.wait_ge(xn_ready, 1)
            normalise(nc, dve, link, S.xn, nx, tmp, st, False, 1e-6, squares, roots, 1).then_inc(nx_ready, 1)
            dve.wait_ge(w_loaded, 16 * 7)
            for c in range(4):
                for n in range(2):
                    link(nc.vector.tensor_copy(Wd[:, c, :].rearrange("p (h n d) -> p h n d", n=2, d=8)[:, :, n, :],
                                               W[:, c // 2, 64 * (c % 2):64 * (c % 2) + 64].rearrange("p (h d) -> p h d", d=8)))
            nc.vector.tensor_copy(Wd[0:1, 0, 0:1], Wd[0:1, 0, 0:1]).then_inc(wd_ready, 1)
            dve.wait_ge(cols_done, 2)
            link(nc.vector.tensor_copy(S.dwb[:, :, :], ps[:, 6, 0:64].rearrange("p (c n) -> p c n", c=2)))
            for c in range(4):
                dve.wait_ge(v_filled, c + 1)
                nc.vector.tensor_tensor(S.Vp[:, 4 * c:4 * c + 4, :, 0:8],
                                        ps[:, 4 + c % 2, :].rearrange("p (j h d) -> p j h d", j=4, d=8),
                                        S.bv[:, :].rearrange("p (h d) -> p h d", d=8).unsqueeze(1).to_broadcast([P, 4, 16, 8]),
                                        ALU.add).then_inc(v_kept, 1)
            dve.wait_ge(v_filled, 5)
            link(nc.vector.tensor_copy(S.Vcp[:, :, 0:32], ps[:, 4, :].rearrange("p (t c) -> p t c", c=32)))



def pieces(nc, S):
    with ExitStack() as ctx:
        R = Room(nc, ctx, "d")
        fw, rv = R.sb("fw", [P, 2, T]), R.sb("rv", [P, 2, T])
        full = R.sb("full", [P, 2, T])
        rest = R.sb("rest", [P, 2, T])
        up, down = rest[:, 0, :], rest[:, 1, :]
        cut = R.sb("cut", [P, 2, 3, T], BF16)
        dist = R.sb("dist", [P, GW])
        def ge(h, n):
            return full[:, h % 2, n * GW:(n + 1) * GW]
        g = R.sb("g", [P, 2, GW])
        iotas, fw_ready, rv_ready, made, high, rested, middle, low, written = (
            R.sem(n) for n in ("iotas", "fw_ready", "rv_ready", "made", "high", "rested", "middle", "low", "written"))
        linked, ge_ready, g_ready, g_written, near_ready = (R.sem(n) for n in ("linked", "ge_ready", "g_ready", "g_written", "near_ready"))
        slot_written = [R.sem("slot_written0"), R.sem("slot_written1")]
        g_slot_written = [R.sem("gsw0"), R.sem("gsw1")]
        block = ctx.enter_context(nc.Block())
        jobs = [(i, k, v) for i in range(2) for k, vs in (("k", range(4)), ("q", range(3))) for v in vs] + [(2, "k", 0), (2, "q", 0)]

        def rows(n):
            return 32 if jobs[n][:2] == (2, "k") else P

        @block.gpsimd
        def _(pool):
            nc.gpsimd.iota(up, [[1, T]], base=0, channel_multiplier=0, allow_small_or_imprecise_dtypes=True).then_inc(iotas, 1)
            nc.gpsimd.iota(down, [[-1, T]], base=T - 1, channel_multiplier=0, allow_small_or_imprecise_dtypes=True).then_inc(iotas, 1)
            nc.gpsimd.iota(dist[:, :], [[1, GW]], base=-(QT - P), channel_multiplier=-1, allow_small_or_imprecise_dtypes=True).then_inc(iotas, 1)
            for n in range(len(jobs)):
                r = rows(n)
                pool.wait_ge(high, n + 1)
                if n >= 2:
                    pool.wait_ge(low, n - 1)
                nc.gpsimd.tensor_tensor(rest[0:r, n % 2, :], full[0:r, n % 2, :], cut[0:r, n % 2, 0, :], ALU.subtract).then_inc(rested, 1)

        @block.scalar
        def _(act):
            act.wait_ge(iotas, 3)
            for i in range(2):
                nc.scalar.activation(fw[:, i, :], up, ACT.Exp, scale=S.cols[:, 4 + i:5 + i]).then_inc(fw_ready, 1)
                nc.scalar.activation(rv[:, i, :], down, ACT.Exp, scale=S.cols[:, 4 + i:5 + i]).then_inc(rv_ready, 1)
            act.wait_ge(near_ready, 2)
            for h in range(16):
                if h >= 2:
                    act.wait_ge(g_ready, h - 1)
                for n in range(2):
                    nc.scalar.activation(ge(h, n), dist[:, :], ACT.Exp, scale=S.dwb[:, 0, 2 * h + n:2 * h + n + 1]).then_inc(ge_ready, 1)
            for n in range(len(jobs)):
                r = rows(n)
                act.wait_ge(made, n + 1)
                if n >= 2:
                    act.wait_ge(slot_written[n % 2], 48 * (n // 2))
                nc.scalar.activation(cut[0:r, n % 2, 0, :], full[0:r, n % 2, :], ACT.Copy).then_inc(high, 1)
                act.wait_ge(rested, n + 1)
                nc.scalar.activation(cut[0:r, n % 2, 1, :], rest[0:r, n % 2, :], ACT.Copy).then_inc(middle, 1)

        @block.vector
        def _(dve):
            link = Links(dve, linked)
            dve.wait_ge(iotas, 3)
            nc.vector.tensor_scalar(ge(0, 0), dist[:, :], -1.0, None, ALU.mult).then_inc(near_ready, 1)
            dve.wait_ge(near_ready, 1)
            nc.vector.tensor_tensor(dist[:, :], dist[:, :], ge(0, 0), ALU.max).then_inc(near_ready, 1)
            for h in range(16):
                dve.wait_ge(ge_ready, 2 * h + 2)
                if h >= 2:
                    dve.wait_ge(g_slot_written[h % 2], 16 * (h // 2))
                link(nc.vector.tensor_scalar(ge(h, 0), ge(h, 0), S.dwb[:, 1, 2 * h:2 * h + 1], None, ALU.mult))
                nc.vector.scalar_tensor_tensor(g[:, h % 2, :], ge(h, 1), S.dwb[:, 1, 2 * h + 1:2 * h + 2], ge(h, 0),
                                               ALU.mult, ALU.add).then_inc(g_ready, 1)

            def finish(n):
                dve.wait_ge(middle, n + 1)
                r = rows(n)
                nc.vector.tensor_tensor(cut[0:r, n % 2, 2, :], rest[0:r, n % 2, :], cut[0:r, n % 2, 1, :], ALU.subtract).then_inc(low, 1)

            for n, (i, kind, v) in enumerate(jobs):
                if n >= 2:
                    dve.wait_ge(rested, n - 1)
                else:
                    dve.wait_ge(g_ready, 16)
                f = full[:, n % 2, :]
                ins = []
                if i == 2:
                    r = rows(n)
                    ins = [nc.vector.tensor_scalar(f[0:r], (S.KF if kind == "k" else S.QF)[0:r, :],
                                                   1.0 if kind == "k" else S.scale_f, None, ALU.mult)]
                elif kind == "k":
                    q0, q1 = QT * v, QT * v + QT
                    if v == 0:
                        dve.wait_ge(fw_ready, i + 1)
                        dve.wait_ge(rv_ready, i + 1)
                    if q0:
                        ins.append(nc.vector.tensor_tensor(f[:, 0:q0], S.K2[:, i, 0:q0], rv[:, i, T - 1 - q0:T - 1], ALU.mult))
                    ins.append(nc.vector.tensor_copy(f[:, q0:q1], S.K2[:, i, q0:q1]))
                    if q1 < T:
                        ins.append(nc.vector.tensor_tensor(f[:, q1:T], S.K2[:, i, q1:T], fw[:, i, 1:T - q1 + 1], ALU.mult))
                elif v == 1:
                    ins = [nc.vector.tensor_scalar(f, S.Q2[:, i, :], S.cols[:, 8:9], None, ALU.mult)]
                else:
                    part = fw[:, i, 0:QT] if v == 0 else rv[:, i, T - QT:T]
                    ins = [nc.vector.scalar_tensor_tensor(f.rearrange("p (a b) -> p a b", b=QT), S.Q2[:, i, :].rearrange("p (a b) -> p a b", b=QT),
                                                          S.cols[:, 6 + i:7 + i], part.unsqueeze(1).to_broadcast([P, NQ, QT]),
                                                          ALU.mult, ALU.mult)]
                ins[-1].then_inc(made, 1)
                if n >= 1:
                    finish(n - 1)
            finish(len(jobs) - 1)

        @block.sync
        def _(sp):
            for h in range(16):
                sp.wait_ge(g_ready, h + 1)
                sp.dma_start(S.GD[h, :, :], g[:, h % 2, :]).then_inc(g_slot_written[h % 2], 16)
            for n, (i, kind, v) in enumerate(jobs):
                sp.wait_ge(low, n + 1)
                r = rows(n)
                for c in range(3):
                    if i == 2:
                        dst = (S.KDF if kind == "k" else S.QDF)[c, :, :]
                    else:
                        dst = (S.KD if kind == "k" else S.QD)[v, c, P * i:P * i + P, :]
                    sp.dma_start(dst, cut[0:r, n % 2, c, :]).then_inc(slot_written[n % 2], 16)
            for m in range(2):
                sp.wait_ge(g_slot_written[m], 16 * 8)
                sp.wait_ge(slot_written[m], 48 * len(jobs[m::2]))


class Attention:
    LEAD, LAG, PSLOTS, NEAR_LATE = 20, 5, 8, 3

    def __init__(self, heads, dv, width, decayed):
        self.heads, self.dv, self.W, self.decayed = heads, dv, width, decayed
        self.rows = [96] if decayed else [96, 96]
        self.near_steps = (1, 4, 7, 10) if decayed else ()
        self.groups = P // width
        self.pairs = heads // 2

    def key_blocks(self, i):
        if not self.decayed:
            return [(kb, False) for kb in range(NT)]
        near = list(range(4 * i, 4 * i + 4))
        far = [kb for kb in range(NT) if kb not in near]
        return [(near.pop(0), True) if s in self.near_steps else (far.pop(0), False) for s in range(NT)]

    def variant(self, i, t):
        return 0 if not self.decayed else (0 if t < i else 1 if t == i else 2)


def attention(nc, S, a):
    W, dv = a.W, a.dv
    NS, NV, NN = len(a.rows), (3 if a.decayed else 1), len(a.near_steps)
    NF = NT - NN
    TILES = 2 * NQ
    BODY = TILES * NT
    with ExitStack() as ctx:
        R = Room(nc, ctx, "t" if a.decayed else "u")
        K = [R.sb(f"K{i}", [P, NS, T], BF16) for i in range(NQ if a.decayed else 1)]
        Q = [R.sb(f"Q{i}", [P, NS, NV, QT], BF16) for i in range(NQ)]
        if a.decayed:
            G, V = R.sb("G", [P, 2, GW]), R.sb("V", [P, 2, NT, W])
            T1, T2 = R.sb("T1", [P, 2, QT]), R.sb("T2", [P, 2, QT])
            junk, mb = R.sb("junk", [P, 2, QT]), R.sb("mb", [P, 2, QT])
        E = R.sb("E", [P, a.PSLOTS, QT])
        mx, nm = R.sb("mx", [P, 2, 4, 4]), R.sb("nm", [P, 2, 4])
        hi = R.sb("hi", [2, QT], BF16)
        O4 = R.sb("O4", [P, QT])
        rc = R.sb("rc", [P, 4])
        ps = R.psum()
        A_BANK, B_BANK, PV_BANK, MISC = 0, 4, 6, 7
        set_up, started = R.sem("set_up"), R.sem("started")
        tile_loaded = [R.sem(f"tile_loaded{i}") for i in range(NQ)]
        keys_loaded = R.sem("keys_loaded")
        mask_loaded, v_copied = [R.sem(f"mask_loaded{i}") for i in range(2)], R.sem("v_copied")
        a_scored, a_reduced = R.sem("a_scored"), R.sem("a_reduced")
        max_ready, row_ready, high_ready, shift_ready = (R.sem(n) for n in ("max_ready", "row_ready", "high_ready", "shift_ready"))
        spread_ready, spread_kept = R.sem("spread_ready"), R.sem("spread_kept")
        b_scored, near_masked, near_shifted = R.sem("b_scored"), R.sem("near_masked"), R.sem("near_shifted")
        near_exp, far_exp, pv_done = R.sem("near_exp"), R.sem("far_exp"), R.sem("pv_done")
        o_kept, o_turned, o_inverse, o_normed = (R.sem(n) for n in ("o_kept", "o_turned", "o_inverse", "o_normed"))
        block = ctx.enter_context(nc.Block())
        per_load = 16 * (12 if a.decayed else 6)

        def counts(b):
            tile, s = divmod(b, NT)
            near = sum(x < s for x in a.near_steps)
            return tile * NN + near, tile * NF + s - near

        def wait(engine, sem, hp, per_pair, count):
            if not isinstance(hp, int) or hp * per_pair + count > 0:
                engine.wait_ge(sem, hp * per_pair + count)

        def over_pairs(engine, emit):
            emit(0, False)
            if a.pairs > 2:
                with engine.Fori(1, a.pairs - 1) as hp:
                    emit(hp, False)
            emit(a.pairs - 1, True)

        def next_tile(hp, u):
            return (hp, u + 1) if u < TILES - 1 else (hp + 1, 0)

        def last_tile(hp, u):
            return (hp, u - 1) if u else (hp - 1, TILES - 1)

        def any_before(hp, u):
            return u > 0 or not isinstance(hp, int) or hp > 0

        @block.sync
        def _(sp):
            if not a.decayed:
                for r in range(6):
                    st, q = divmod(r, 3)
                    sp.dma_start(K[0][32 * q:32 * q + 32, st, :], S.KDF[SPLIT_K[r], :, :]).then_inc(keys_loaded, 16)

            def load(hp, u):
                i = u % NQ
                h = hp * 2 + u // NQ
                wait(sp, b_scored, hp, BODY, NT * (u - NQ + 1))
                for r in range(6):
                    if a.decayed:
                        sp.dma_start(K[i][16 * r:16 * r + 16, 0, :], S.KD[i, SPLIT_K[r], bass.ds(h * 16, 16), :]).then_inc(tile_loaded[i], 16)
                        sp.dma_start(Q[i][16 * r:16 * r + 16, 0, :, :],
                                     S.QD[:, SPLIT_Q[r], bass.ds(h * 16, 16), QT * i:QT * i + QT].rearrange("v r c -> r v c")).then_inc(tile_loaded[i], 16)
                    else:
                        st, q = divmod(r, 3)
                        sp.dma_start(Q[i][32 * q:32 * q + 32, st, 0, :], S.QDF[SPLIT_Q[r], bass.ds(h * 32, 32), QT * i:QT * i + QT]).then_inc(tile_loaded[i], 16)

            def mask(hp, par):
                if a.decayed:
                    wait(sp, near_masked, hp, TILES * NN, (par - 1) * NQ * NN)
                    sp.dma_start(G[:, par, :], S.GD[bass.ds(hp * 2 + par, 1), :, :].rearrange("a p c -> (a p) c")).then_inc(mask_loaded[par], 16)

            def emit(hp, last):
                if isinstance(hp, int) and hp == 0:
                    mask(0, 0)
                    for u in range(NQ):
                        load(0, u)
                mask(hp, 1)
                for u in range(NQ, TILES):
                    load(hp, u)
                if not last:
                    mask(hp + 1, 0)
                    for u in range(NQ):
                        load(hp + 1, u)
            over_pairs(sp, emit)

        @block.tensor
        def _(pe):
            def score_a(hp, n):
                u, j, t = n // NT, n // 4 % 4, n % 4
                i = u % NQ
                if n % NT == 0:
                    wait(pe, tile_loaded[i], hp, 2 * per_load, per_load * (u // NQ + 1))
                wait(pe, a_reduced, hp, BODY, n - 3)
                kk = K[i if a.decayed else 0]
                for st in range(NS):
                    ins = nc.tensor.matmul(ps[:, A_BANK + t, :], Q[i][0:96, st, a.variant(i, t), P * j:P * j + P],
                                           kk[0:96, st, QT * t:QT * t + QT], start=st == 0, stop=st == NS - 1)
                ins.then_inc(a_scored, 1)

            def rows_of_max(hp, u):
                wait(pe, max_ready, hp, TILES, u + 1)
                wait(pe, o_normed, hp, TILES, u - 1)
                for j in range(4):
                    ins = nc.tensor.matmul(ps[0:2, MISC, P * j:P * j + P], nm[:, u % 2, j:j + 1].to_broadcast([P, 2]),
                                           S.ident[:, :], start=True, stop=True)
                ins.then_inc(row_ready, 1)

            def spread(hp, u):
                if a.decayed:
                    wait(pe, shift_ready, hp, TILES, u + 1)
                    nc.tensor.matmul(ps[:, MISC, :], S.spread[0:98, :], Q[u % NQ][0:98, 0, 0, :], start=True, stop=True).then_inc(spread_ready, 1)

            def score_b(hp, b):
                u, s = divmod(b, NT)
                i = u % NQ
                kb, _ = a.key_blocks(i)[s]
                was_near = (b - 2) % NT in a.near_steps
                cn, cf = counts(b - 2)
                if was_near:
                    wait(pe, near_masked, hp, TILES * NN, cn + 1)
                else:
                    wait(pe, far_exp, hp, TILES * NF, cf + 1)
                if s == 0:
                    wait(pe, shift_ready, hp, TILES, u + 1)
                kk = K[i if a.decayed else 0]
                for st in range(NS):
                    rows = 98 if st == NS - 1 else 96
                    ins = nc.tensor.matmul(ps[:, B_BANK + b % 2, :], kk[0:rows, st, P * kb:P * kb + P],
                                           Q[i][0:rows, st, a.variant(i, kb // 4), :], start=st == 0, stop=st == NS - 1)
                ins.then_inc(b_scored, 1)

            def times_v(hp, b):
                u, s = divmod(b, NT)
                kb, near = a.key_blocks(u % NQ)[s]
                cn, cf = counts(b)
                if near:
                    wait(pe, near_exp, hp, TILES * NN, cn + 1)
                else:
                    wait(pe, far_exp, hp, TILES * NF, cf + 1)
                if s == 0:
                    wait(pe, o_kept, hp, TILES, u)
                    if a.decayed and u % NQ == 0:
                        wait(pe, v_copied, hp, 2, u // NQ + 1)
                g = s % a.groups
                v = V[:, u // NQ, kb, :] if a.decayed else S.Vcp[:, kb, :]
                nc.tensor.matmul(ps[W * g:W * g + W, PV_BANK, :], v, E[:, b % a.PSLOTS, :],
                                 start=s < a.groups, stop=s >= NT - a.groups).then_inc(pv_done, 1)

            def turn(hp, u, last=False):
                wait(pe, o_kept, hp, TILES, u + 1)
                if last:
                    wait(pe, o_normed, hp, TILES, u)
                elif a.decayed:
                    wait(pe, spread_kept, hp, TILES, u + 2)
                for j in range(4):
                    ins = nc.tensor.matmul(ps[:, MISC, W * j:W * j + W], O4[:, P * j:P * j + P],
                                           (S.selo if W == 32 else S.selo2)[:, :], start=True, stop=True)
                ins.then_inc(o_turned, 1)

            def emit(hp, last):
                if isinstance(hp, int) and hp == 0:
                    pe.wait_ge(set_up, 1)
                    if not a.decayed:
                        pe.wait_ge(keys_loaded, 16 * 6)
                    for n in range(NT):
                        score_a(0, n)
                    rows_of_max(0, 0)
                    for n in range(NT, a.LEAD):
                        score_a(0, n)
                    spread(0, 0)
                for b in range(BODY):
                    u, s = divmod(b, NT)
                    n = b + a.LEAD
                    if n < BODY:
                        score_a(hp, n)
                    elif not last:
                        score_a(hp + 1, n - BODY)
                    score_b(hp, b)
                    if b >= a.LAG:
                        times_v(hp, b - a.LAG)
                    elif any_before(hp, 0):
                        times_v(hp - 1, b - a.LAG + BODY)
                    if s == a.LAG + 2 and any_before(hp, u):
                        turn(*last_tile(hp, u))
                    if not (last and u == TILES - 1):
                        if s == 13:
                            rows_of_max(*next_tile(hp, u))
                        if s == 15:
                            spread(*next_tile(hp, u))
                if last:
                    for b in range(BODY - a.LAG, BODY):
                        times_v(hp, b)
                    turn(hp, TILES - 1, True)
            over_pairs(pe, emit)

        @block.vector
        def _(dve):
            def reduce_a(hp, n):
                u, j, t = n // NT, n // 4 % 4, n % 4
                i = u % NQ
                if a.decayed and n % (NQ * NT) == 0:
                    wait(dve, mask_loaded[u // NQ], hp, 16, 16)
                wait(dve, a_scored, hp, BODY, n + 1)
                src, m = ps[:, A_BANK + t, :], mx[:, u % 2, j, t:t + 1]
                if a.decayed and t == i:
                    o = QT - P - P * j
                    wait(dve, a_reduced, hp, BODY, n - 4)
                    dve.nop(nofuse=True)
                    ins = nc.vector.tensor_tensor_reduce(junk[:, j % 2, :], src, G[:, u // NQ, o:o + QT], 1.0, LEAST, ALU.mult, ALU.max, m)
                else:
                    ins = nc.vector.tensor_reduce(m, src, AX.X, ALU.max)
                ins.then_inc(a_reduced, 1)

            def finish_max(hp, u):
                wait(dve, a_reduced, hp, BODY, NT * (u + 1))
                nc.vector.tensor_reduce(nm[:, u % 2, :], mx[:, u % 2, :, :], AX.X, ALU.max, negate=True).then_inc(max_ready, 1)

            def cut_max(hp, u):
                wait(dve, row_ready, hp, TILES, u + 1)
                nc.vector.tensor_copy(hi[:, :], ps[0:2, MISC, :]).then_inc(high_ready, 1)
                wait(dve, high_ready, hp, TILES, u + 1)
                for v in ((0, 2) if a.decayed else (0,)):
                    ins = nc.vector.scalar_tensor_tensor(Q[u % NQ][96:98, NS - 1, v, :], hi[:, :], S.low_row[:, 0:1], ps[0:2, MISC, :], ALU.mult, ALU.add)
                ins.then_inc(shift_ready, 1)

            def mask_b(hp, b):
                u, s = divmod(b, NT)
                kb, _ = a.key_blocks(u % NQ)[s]
                cn, _ = counts(b)
                wait(dve, b_scored, hp, BODY, b + 1)
                wait(dve, near_shifted, hp, TILES * NN, cn - 1)
                o = QT - P - P * (kb - 4 * (u % NQ))
                nc.vector.tensor_tensor(T1[:, cn % 2, :], ps[:, B_BANK + b % 2, :], G[:, u // NQ, o:o + QT], ALU.mult).then_inc(near_masked, 1)

            def norm(hp, u):
                h = hp * 2 + u // NQ
                i = u % NQ
                wait(dve, o_turned, hp, TILES, u + 1)
                o = ps[:, MISC, 0:4 * W].rearrange("p (j w) -> p j w", w=W)
                nc.vector.reciprocal(rc[:, :].unsqueeze(2), o[:, :, dv:dv + 1]).then_inc(o_inverse, 1)
                wait(dve, o_inverse, hp, TILES, u + 1)
                dst = (S.AO if a.decayed else S.AOF)[:, 4 * i:4 * i + 4, bass.ds(h * dv, dv)]
                nc.vector.tensor_tensor(dst, o[:, :, 0:dv], rc[:, :].unsqueeze(2).to_broadcast([P, 4, dv]), ALU.mult).then_inc(o_normed, 1)

            def values_of(hp, par):
                if a.decayed:
                    wait(dve, pv_done, hp, BODY, (par - 1) * BODY // 2)
                    src = S.Vp[:, :, bass.ds(hp * 2 + par, 1), :].rearrange("p t a w -> p t (a w)")
                    nc.vector.tensor_copy(V[:, par, :, :], src).then_inc(v_copied, 1)

            def emit(hp, last):
                if isinstance(hp, int) and hp == 0:
                    for i in range(NQ):
                        nc.vector.memset(Q[i][96:98, NS - 1, :, :], 0.0).then_inc(started, 1)
                        if i < len(K):
                            nc.vector.memset(K[i][96:98, NS - 1, :], 1.0).then_inc(started, 1)
                    dve.wait_ge(started, NQ + len(K))
                    nc.vector.memset(rc[:, :], 0.0).then_inc(set_up, 1)
                    values_of(0, 0)
                    for n in range(NT):
                        reduce_a(0, n)
                    finish_max(0, 0)
                    cut_max(0, 0)
                    for n in range(NT, a.LEAD):
                        reduce_a(0, n)
                for b in range(BODY):
                    u, s = divmod(b, NT)
                    n = b + a.LEAD
                    if n < BODY:
                        reduce_a(hp, n)
                    elif not last:
                        reduce_a(hp + 1, n - BODY)
                    if s in a.near_steps:
                        mask_b(hp, b)
                    if s == a.LAG + 3 and any_before(hp, u):
                        norm(*last_tile(hp, u))
                    if b == a.LAG + 4:
                        values_of(hp, 1)
                    if b == BODY // 2 + a.LAG + 4 and not last:
                        values_of(hp + 1, 0)
                    if not (last and u == TILES - 1):
                        if s == 11:
                            finish_max(*next_tile(hp, u))
                        if s == 14:
                            cut_max(*next_tile(hp, u))
                if last:
                    norm(hp, TILES - 1)
            over_pairs(dve, emit)

        @block.gpsimd
        def _(pool):
            def emit(hp, last):
                for b in range(BODY):
                    u, s = divmod(b, NT)
                    if s in a.near_steps:
                        cn, _ = counts(b)
                        wait(pool, near_masked, hp, TILES * NN, cn + 1)
                        wait(pool, spread_kept, hp, TILES, u + 1)
                        wait(pool, near_exp, hp, TILES * NN, cn - 1)
                        nc.gpsimd.tensor_tensor(T2[:, cn % 2, :], T1[:, cn % 2, :], mb[:, u % 2, :], ALU.add).then_inc(near_shifted, 1)
            if a.decayed:
                over_pairs(pool, emit)

        @block.scalar
        def _(act):
            def slot(hp, b):
                wait(act, pv_done, hp, BODY, b - a.PSLOTS + 1)
                return E[:, b % a.PSLOTS, :]

            def keep_spread(hp, u):
                if a.decayed:
                    wait(act, spread_ready, hp, TILES, u + 1)
                    wait(act, near_shifted, hp, TILES * NN, NN * (u - 1))
                    nc.scalar.activation(mb[:, u % 2, :], ps[:, MISC, :], ACT.Copy).then_inc(spread_kept, 1)

            def keep_sums(hp, u):
                wait(act, pv_done, hp, BODY, NT * (u + 1))
                wait(act, o_turned, hp, TILES, u)
                nc.scalar.activation(O4[:, :], ps[:, PV_BANK, :], ACT.Copy).then_inc(o_kept, 1)

            def emit(hp, last):
                if isinstance(hp, int) and hp == 0:
                    keep_spread(0, 0)
                for b in range(BODY):
                    u, s = divmod(b, NT)
                    if s == a.LAG and any_before(hp, u):
                        keep_sums(*last_tile(hp, u))
                    if s not in a.near_steps:
                        out = slot(hp, b)
                        wait(act, b_scored, hp, BODY, b + 1)
                        nc.scalar.activation(out, ps[:, B_BANK + b % 2, :], ACT.Exp).then_inc(far_exp, 1)
                    if s - a.NEAR_LATE in a.near_steps:
                        bn = b - a.NEAR_LATE
                        cn, _ = counts(bn)
                        out = slot(hp, bn)
                        wait(act, near_shifted, hp, TILES * NN, cn + 1)
                        nc.scalar.activation(out, T2[:, cn % 2, :], ACT.Exp).then_inc(near_exp, 1)
                    if s == 15 and not (last and u == TILES - 1):
                        keep_spread(*next_tile(hp, u))
                if last:
                    keep_sums(hp, TILES - 1)
            over_pairs(act, emit)


def transposed(nc, pe, ps, bank, src, tiles, ident):
    for j, t in enumerate(tiles):
        ins = nc.tensor.transpose(ps[:, bank, j * P:(j + 1) * P], src[:, t, :], ident[:, :])
    return ins


def choose_two(nc, link, prob, rev, first, second, key, val, E):
    wide = [P, NT, E]
    for n, hot in ((0, first), (1, second)):
        link(nc.vector.tensor_reduce(val[:, n, :], prob[:, :, :], AX.X, ALU.max))
        link(nc.vector.tensor_tensor(key[:, :, :], prob[:, :, :], val[:, n, :].unsqueeze(2).to_broadcast(wide), ALU.is_equal))
        link(nc.vector.tensor_tensor(key[:, :, :], key[:, :, :], rev[:, 0:E].unsqueeze(1).to_broadcast(wide), ALU.mult))
        link(nc.vector.tensor_reduce(val[:, 2, :], key[:, :, :], AX.X, ALU.max))
        link(nc.vector.tensor_tensor(hot[:, :, :], key[:, :, :], val[:, 2, :].unsqueeze(2).to_broadcast(wide), ALU.is_equal))
        if n == 0:
            link(nc.vector.scalar_tensor_tensor(prob[:, :, :].rearrange("p t e -> p (t e)"), hot[:, :, :].rearrange("p t e -> p (t e)"), -2.0,
                                                prob[:, :, :].rearrange("p t e -> p (t e)"), ALU.mult, ALU.add))


def mixture0(nc, S, dram):
    E, NE = 8, 9
    with ExitStack() as ctx:
        R = Room(nc, ctx, "m")
        AT = R.sb("AT", [P, T])
        AFT = R.sb("AFT", [P, T])
        y = R.sb("y", [P, NT, D])
        s0 = R.sb("s0", [P, NT, D])
        nx, tmp, st = R.sb("nx", [P, NT, D]), R.sb("tmp", [P, NT, D]), R.sb("st", [P, 4, NT])
        x = R.sb("x", [P, NT, D])
        WoT, fWoT, WrT = R.sb("WoT", [P, D]), R.sb("fWoT", [P, D]), R.sb("WrT", [P, E])
        W1, W3, W2 = (R.sb(n, [P, NE, D]) for n in ("W1", "W3", "W2"))
        rev = R.sb("rev", [P, E])
        prob, key, hot1, hot2 = (R.sb(n, [P, NT, E]) for n in ("prob", "key", "hot1", "hot2"))
        val = R.sb("val", [P, 8, NT])
        share = R.sb("share", [P, NT, NE])
        gate, h = R.sb("gate", [P, 2, QT]), R.sb("h", [P, 2, QT])
        ps = R.psum()
        loaded, x_loaded, linked, rev_ready = R.sem("loaded"), R.sem("x_loaded"), R.sem("linked"), R.sem("rev_ready")
        turned, turned_kept, projected, added = R.sem("turned"), R.sem("turned_kept"), R.sem("projected"), R.sem("added")
        squares, roots, nx_ready = R.sem("squares"), R.sem("roots"), R.sem("nx_ready")
        nx_turned, nx_kept, routed = R.sem("nx_turned"), R.sem("nx_kept"), R.sem("routed")
        shifted, expd = R.sem("shifted"), R.sem("expd")
        up_done, gated, h_ready, down_done, summed = (R.sem(n) for n in ("up_done", "gated", "h_ready", "down_done", "summed"))
        y_ready, silu_ready = R.sem("y_ready"), R.sem("silu_ready")
        block = ctx.enter_context(nc.Block())
        wide = [P, NT, E]
        STEPS = NE * NQ

        @block.sync
        def _(sp):
            sp.dma_start(WoT[:, :], dram["WoT"]).then_inc(loaded, 16)
            sp.dma_start(fWoT[:, :], dram["fWoT"]).then_inc(loaded, 16)
            sp.dma_start(WrT[:, :], dram["WrT"]).then_inc(loaded, 16)
            for w, n in ((W1, "eW1"), (W3, "eW3"), (W2, "eW2")):
                for e in range(NE):
                    sp.dma_start(w[:, e, :], dram[n][e, :, :]).then_inc(loaded, 16)
            for t in range(NT):
                sp.dma_start(x[:, t, :], dram["x"][t * P:(t + 1) * P, :]).then_inc(x_loaded, 16)

        @block.gpsimd
        def _(pool):
            nc.gpsimd.iota(rev[:, :], [[-1, E]], base=E, channel_multiplier=0, allow_small_or_imprecise_dtypes=True).then_inc(rev_ready, 1)

        @block.scalar
        def _(act):
            for n in range(8):
                act.wait_ge(turned, n + 1)
                dst = (AT, AFT)[n // 4]
                nc.scalar.activation(dst[:, (n % 4) * QT:(n % 4 + 1) * QT], ps[:, n % 4, :], ACT.Copy).then_inc(turned_kept, 1)
            act.wait_ge(squares, 1)
            nc.scalar.activation(st[:, 2, :], st[:, 1, :], ACT.Sqrt).then_inc(roots, 1)
            for n in range(4):
                act.wait_ge(nx_turned, n + 1)
                nc.scalar.activation(AT[:, n * QT:(n + 1) * QT], ps[:, n % 4, :], ACT.Copy, scale=S.g[:, 1:2]).then_inc(nx_kept, 1)
            act.wait_ge(shifted, 1)
            nc.scalar.activation(prob[:, :, :], prob[:, :, :], ACT.Exp).then_inc(expd, 1)
            act.wait_ge(shifted, 2)
            nc.scalar.activation(val[:, 3, :], val[:, 3, :], ACT.Exp).then_inc(expd, 1)
            for n in range(STEPS):
                act.wait_ge(up_done, n + 1)
                if n >= 2:
                    act.wait_ge(h_ready, n - 1)
                nc.scalar.activation(gate[:, n % 2, :], ps[:, 2 * (n % 2), :], ACT.Silu).then_inc(gated, 1)
            act.wait_ge(y_ready, 1)
            nc.scalar.activation(y[:, :, :], y[:, :, :], ACT.Silu).then_inc(silu_ready, 1)

        @block.tensor
        def _(pe):
            for n in range(8):
                if n >= 4:
                    pe.wait_ge(turned_kept, n - 3)
                transposed(nc, pe, ps, n % 4, (S.AO, S.AOF)[n // 4], range(4 * (n % 4), 4 * (n % 4) + 4), S.ident).then_inc(turned, 1)
            pe.wait_ge(loaded, 16 * (3 + 3 * NE))
            for n in range(8):
                a, w = ((AT, WoT), (AFT, fWoT))[n // 4]
                pe.wait_ge(turned_kept, n + 1)
                if n >= 4:
                    pe.wait_ge(added, n - 3)
                for j in range(4):
                    t = 4 * (n % 4) + j
                    ins = nc.tensor.matmul(ps[:, 4 + n % 4, j * P:(j + 1) * P], a[:, t * P:(t + 1) * P], w[:, :], start=True, stop=True)
                ins.then_inc(projected, 1)
            pe.wait_ge(nx_ready, 1)
            pe.wait_ge(turned_kept, 8)
            for n in range(4):
                transposed(nc, pe, ps, n, nx, range(4 * n, 4 * n + 4), S.ident).then_inc(nx_turned, 1)
            pe.wait_ge(nx_kept, 4)
            pe.wait_ge(added, 8)
            for t in range(NT):
                ins = nc.tensor.matmul(ps[:, 4, t * E:(t + 1) * E], AT[:, t * P:(t + 1) * P], WrT[:, :], start=True, stop=True)
            ins.then_inc(routed, 1)

            def up(n):
                e, c = divmod(n, NQ)
                if n >= 2:
                    pe.wait_ge(h_ready, n - 1)
                for k, w in ((0, W1), (1, W3)):
                    ins = nc.tensor.matmul(ps[:, 2 * (n % 2) + k, :], w[:, e, :], AT[:, c * QT:(c + 1) * QT], start=True, stop=True)
                ins.then_inc(up_done, 1)

            def down(n):
                e, c = divmod(n, NQ)
                pe.wait_ge(h_ready, n + 1)
                if n >= 2:
                    pe.wait_ge(summed, n - 1)
                for j in range(4):
                    ins = nc.tensor.matmul(ps[:, 5 + n % 2, j * P:(j + 1) * P], h[:, n % 2, j * P:(j + 1) * P], W2[:, e, :], start=True, stop=True)
                ins.then_inc(down_done, 1)
            for n in range(STEPS):
                up(n)
                if n:
                    down(n - 1)
            down(STEPS - 1)

        @block.vector
        def _(dve):
            link = Links(dve, linked)
            for n in range(8):
                dve.wait_ge(projected, n + 1)
                src = ps[:, 4 + n % 4, :].rearrange("p (j d) -> p j d", d=D)
                c = n % 4
                if n < 4:
                    nc.vector.tensor_tensor(s0[:, 4 * c:4 * c + 4, :], src, S.bo[:, :].unsqueeze(1).to_broadcast([P, 4, D]), ALU.add).then_inc(added, 1)
                else:
                    nc.vector.tensor_tensor(y[:, 4 * c:4 * c + 4, :], src, S.xn[:, 4 * c:4 * c + 4, :], ALU.add).then_inc(added, 1)
            dve.wait_ge(added, 8)
            normalise(nc, dve, link, y, nx, tmp, st, False, 1e-6, squares, roots, 0).then_inc(nx_ready, 1)
            dve.wait_ge(rev_ready, 1)
            dve.wait_ge(routed, 1)
            link(nc.vector.tensor_tensor(prob[:, :, :], ps[:, 4, 0:NT * E].rearrange("p (t e) -> p t e", e=E),
                                         S.rbias[:, :].unsqueeze(1).to_broadcast(wide), ALU.add))
            link(nc.vector.tensor_reduce(val[:, 4, :], prob[:, :, :], AX.X, ALU.max))
            nc.vector.tensor_tensor(prob[:, :, :], prob[:, :, :], val[:, 4, :].unsqueeze(2).to_broadcast(wide), ALU.subtract).then_inc(shifted, 1)
            dve.wait_ge(expd, 1)
            link(nc.vector.tensor_reduce(val[:, 4, :], prob[:, :, :], AX.X, ALU.add))
            link(nc.vector.reciprocal(val[:, 5, :], val[:, 4, :]))
            link(nc.vector.tensor_tensor(prob[:, :, :], prob[:, :, :], val[:, 5, :].unsqueeze(2).to_broadcast(wide), ALU.mult))
            choose_two(nc, link, prob, rev, hot1, hot2, key, val, E)
            nc.vector.tensor_tensor(val[:, 3, :], val[:, 1, :], val[:, 0, :], ALU.subtract).then_inc(shifted, 1)
            dve.wait_ge(expd, 2)
            link(nc.vector.tensor_scalar(val[:, 4, :], val[:, 3, :], 1.0, None, ALU.add))
            link(nc.vector.reciprocal(val[:, 5, :], val[:, 4, :]))
            link(nc.vector.tensor_tensor(val[:, 6, :], val[:, 5, :], val[:, 3, :], ALU.mult))
            link(nc.vector.tensor_tensor(hot1[:, :, :], hot1[:, :, :], val[:, 5, :].unsqueeze(2).to_broadcast(wide), ALU.mult))
            link(nc.vector.tensor_tensor(hot2[:, :, :], hot2[:, :, :], val[:, 6, :].unsqueeze(2).to_broadcast(wide), ALU.mult))
            link(nc.vector.tensor_tensor(share[:, :, 0:E], hot1[:, :, :], hot2[:, :, :], ALU.add))
            link(nc.vector.memset(share[:, :, E:NE], 1.0))

            def hidden(n):
                dve.wait_ge(gated, n + 1)
                if n >= 2:
                    dve.wait_ge(down_done, n - 1)
                nc.vector.tensor_tensor(h[:, n % 2, :], gate[:, n % 2, :], ps[:, 2 * (n % 2) + 1, :], ALU.mult).then_inc(h_ready, 1)

            def add_up(n):
                e, c = divmod(n, NQ)
                dve.wait_ge(down_done, n + 1)
                if n >= NQ:
                    dve.wait_ge(summed, n - NQ + 1)
                for j in range(4):
                    t = 4 * c + j
                    ins = nc.vector.scalar_tensor_tensor(y[:, t, :], ps[:, 5 + n % 2, j * P:(j + 1) * P], share[:, t, e:e + 1], y[:, t, :],
                                                         ALU.mult, ALU.add)
                ins.then_inc(summed, 1)
            for n in range(STEPS):
                hidden(n)
                if n:
                    add_up(n - 1)
            add_up(STEPS - 1)
            dve.wait_ge(summed, STEPS)
            nc.vector.tensor_copy(val[:, 7, :], val[:, 6, :]).then_inc(y_ready, 1)
            dve.wait_ge(silu_ready, 1)
            dve.wait_ge(x_loaded, 16 * NT)
            link(nc.vector.tensor_tensor(y[:, :, :], y[:, :, :], s0[:, :, :], ALU.mult))
            link(nc.vector.tensor_tensor(S.x1[:, :, :], y[:, :, :], x[:, :, :], ALU.add))


H1, N1 = 8, 32
HN = H1 * N1
E1, I1 = 64, 64
PAIRS = E1 // 2 + 1
CAPACITY = 128


def prepare1(nc, S, dram):
    with ExitStack() as ctx:
        R = Room(nc, ctx, "r")
        nT = R.sb("nT", [P, T])
        xpT = R.sb("xpT", [P, T])
        tmp, st = R.sb("tmp", [P, NT, D]), R.sb("st", [P, 4, NT])
        WinT, WkT, WqT, WvT, WbT = R.sb("WinT", [P, D]), R.sb("WkT", [P, HN]), R.sb("WqT", [P, HN]), R.sb("WvT", [P, HN]), R.sb("WbT", [P, HN])
        bb, gT = R.sb("bb", [P, 2]), R.sb("gT", [P, E1])
        kq = R.sb("kq", [P, 2, 2, HN])
        kraw = R.sb("kraw", [P, NT, HN])
        kn = R.sb("kn", [P, NT, H1, N1 + 1])
        nrm = R.sb("nrm", [P, 3, NT * H1])
        rev = R.sb("rev", [P, E1])
        prob, key, hot1, hot2 = (R.sb(n, [P, NT, E1]) for n in ("prob", "key", "hot1", "hot2"))
        val = R.sb("val", [P, 6, NT])
        before = R.sb("before", [P, P])
        ones = R.sb("ones", [P, P])
        shareT = R.sb("shareT", [E1, T])
        rows = R.sb("rows", [2, T])
        ps = R.psum()
        loaded, linked = R.sem("loaded"), R.sem("linked")
        squares, roots, n_ready, m_ready = R.sem("squares"), R.sem("roots"), R.sem("n_ready"), R.sem("m_ready")
        turned, turned_kept, xp_done, xp_kept = R.sem("turned"), R.sem("turned_kept"), R.sem("xp_done"), R.sem("xp_kept")
        vb_done, vb_kept, kq_done, kq_kept, q_out = (R.sem(n) for n in ("vb_done", "vb_kept", "kq_done", "kq_kept", "q_out0"))
        q_out = [q_out, R.sem("q_out1")]
        k_kept, norms, norm_roots, kn_ready, kn_out = (R.sem(n) for n in ("k_kept", "norms", "norm_roots", "kn_ready", "kn_out"))
        pool_made, m_turned, m_kept, routed, shifted, expd = (R.sem(n) for n in ("pool_made", "m_turned", "m_kept", "routed", "shifted", "expd"))
        chosen, placed, shares_ready, share_turned, share_kept, out_done = (
            R.sem(n) for n in ("chosen", "placed", "shares_ready", "share_turned", "share_kept", "out_done"))
        block = ctx.enter_context(nc.Block())
        wide = [P, NT, E1]
        nm = tmp

        @block.sync
        def _(sp):
            for dst, n in ((WinT, "WinT"), (WkT, "rWkT"), (WqT, "rWqT"), (WvT, "rWvT"), (WbT, "rWbT"), (bb, "bbeta"), (gT, "gateT")):
                sp.dma_start(dst[:, :], dram[n]).then_inc(loaded, 16)
            for t in range(NT // 2):
                sp.wait_ge(kq_kept, t + 1)
                for j in range(2):
                    tok = (2 * t + j) * P
                    sp.dma_start(S.QN[:, tok:tok + P, :].rearrange("h p c -> p h c"),
                                 kq[:, t % 2, j, :].rearrange("p (h c) -> p h c", c=N1)).then_inc(q_out[t % 2], 16)
            sp.wait_ge(kn_ready, 1)
            for t in range(NT):
                sp.dma_start(S.KN[:, t * P:(t + 1) * P, :].rearrange("h p c -> p h c"), kn[:, t, :, :]).then_inc(kn_out, 16)
            sp.wait_ge(share_kept, 4)
            sp.dma_start(S.ST[0:E1, :], shareT[:, :]).then_inc(out_done, 16)
            sp.dma_start(S.ST[E1:E1 + 2, :], rows[:, :]).then_inc(out_done, 16)
            for m in range(2):
                sp.wait_ge(q_out[m], 8 * NT)
            sp.wait_ge(kn_out, 16 * NT)
            sp.wait_ge(out_done, 32)

        @block.gpsimd
        def _(pool):
            nc.gpsimd.iota(rev[:, :], [[-1, E1]], base=E1, channel_multiplier=0, allow_small_or_imprecise_dtypes=True).then_inc(pool_made, 1)
            nc.gpsimd.memset(ones[:, :], 1.0).then_inc(pool_made, 1)
            nc.gpsimd.memset(rows[:, :], 0.5).then_inc(pool_made, 1)
            pool.wait_ge(pool_made, 3)
            nc.gpsimd.affine_select(out=before[:, :], in_=ones[:, :], compare_op=ALU.is_gt, fill=0.0,
                                    base=0, pattern=[[1, P]], channel_multiplier=-1).then_inc(pool_made, 1)
            nc.gpsimd.affine_select(out=rows[:, :], in_=rows[:, :], compare_op=ALU.is_gt, fill=0.0,
                                    base=1, pattern=[[0, T]], channel_multiplier=-1).then_inc(pool_made, 1)
            pool.wait_ge(pool_made, 5)

        @block.scalar
        def _(act):
            for n in range(2):
                act.wait_ge(squares, n + 1)
                nc.scalar.activation(st[:, 2, :], st[:, 1, :], ACT.Sqrt).then_inc(roots, 1)
            for n in range(4):
                act.wait_ge(turned, n + 1)
                nc.scalar.activation(nT[:, n * QT:(n + 1) * QT], ps[:, n, :], ACT.Copy).then_inc(turned_kept, 1)
            for n in range(4):
                act.wait_ge(m_turned, n + 1)
                nc.scalar.activation(S.mT[:, n * QT:(n + 1) * QT], ps[:, n, :], ACT.Copy, scale=S.g[:, 2:3]).then_inc(m_kept, 1)
            for n in range(4):
                act.wait_ge(xp_done, n + 1)
                nc.scalar.activation(xpT[:, n * QT:(n + 1) * QT], ps[:, n, :], ACT.Silu).then_inc(xp_kept, 1)
            for n in range(16):
                act.wait_ge(vb_done, n + 1)
                g, c = n // 4 % 2, n % 4
                if n < 8:
                    nc.scalar.activation(S.vT[:, g, c * QT:(c + 1) * QT], ps[:, n % 4, :], ACT.Copy).then_inc(vb_kept, 1)
                else:
                    nc.scalar.activation(S.beta[:, g, c * QT:(c + 1) * QT], ps[:, n % 4, :], ACT.Sigmoid, bias=bb[:, g:g + 1]).then_inc(vb_kept, 1)
            for n in range(8):
                act.wait_ge(kq_done, n + 1)
                if n >= 2:
                    act.wait_ge(q_out[n % 2], 32 * (n // 2))
                nc.scalar.activation(kq[:, n % 2, :, :], ps[:, 4 + n % 2, :].rearrange("p (j c) -> p j c", j=2), ACT.Copy).then_inc(kq_kept, 1)
            for n in range(8):
                act.wait_ge(kq_done, 8 + n + 1)
                nc.scalar.activation(kraw[:, 2 * n:2 * n + 2, :], ps[:, 4 + n % 2, :].rearrange("p (j c) -> p j c", j=2), ACT.Copy).then_inc(k_kept, 1)
            act.wait_ge(norms, 1)
            nc.scalar.activation(nrm[:, 1, :], nrm[:, 0, :], ACT.Sqrt).then_inc(norm_roots, 1)
            act.wait_ge(shifted, 1)
            nc.scalar.activation(prob[:, :, :], prob[:, :, :], ACT.Exp).then_inc(expd, 1)
            for n in range(4):
                act.wait_ge(share_turned, n + 1)
                nc.scalar.activation(shareT[:, n * QT:(n + 1) * QT], ps[0:E1, n, :], ACT.Copy).then_inc(share_kept, 1)

        @block.tensor
        def _(pe):
            pe.wait_ge(n_ready, 1)
            for n in range(4):
                transposed(nc, pe, ps, n, S.xn, range(4 * n, 4 * n + 4), S.ident).then_inc(turned, 1)
            pe.wait_ge(m_ready, 1)
            for n in range(4):
                pe.wait_ge(turned_kept, n + 1)
                transposed(nc, pe, ps, n, nm, range(4 * n, 4 * n + 4), S.ident).then_inc(m_turned, 1)
            pe.wait_ge(loaded, 16 * 7)
            for n in range(4):
                pe.wait_ge(m_kept, n + 1)
                nc.tensor.matmul(ps[:, n, :], WinT[:, :], nT[:, n * QT:(n + 1) * QT], start=True, stop=True).then_inc(xp_done, 1)
            for t in range(NT):
                ins = nc.tensor.matmul(ps[:, 6 + t // 8, (t % 8) * E1:(t % 8 + 1) * E1], S.mT[:, t * P:(t + 1) * P], gT[:, :], start=True, stop=True)
            ins.then_inc(routed, 1)
            pe.wait_ge(xp_kept, 4)
            for n in range(16):
                if n >= 4:
                    pe.wait_ge(vb_kept, n - 3)
                g, c = n // 4 % 2, n % 4
                w = WvT if n < 8 else WbT
                nc.tensor.matmul(ps[:, n % 4, :], w[:, g * P:(g + 1) * P], xpT[:, c * QT:(c + 1) * QT], start=True, stop=True).then_inc(vb_done, 1)
            for n in range(16):
                if 2 <= n < 10:
                    pe.wait_ge(kq_kept, n - 1)
                elif n >= 10:
                    pe.wait_ge(k_kept, n - 9)
                for j in range(2):
                    t = 2 * (n % 8) + j
                    ins = nc.tensor.matmul(ps[:, 4 + n % 2, j * HN:(j + 1) * HN], xpT[:, t * P:(t + 1) * P], (WqT if n < 8 else WkT)[:, :], start=True, stop=True)
                ins.then_inc(kq_done, 1)
            pe.wait_ge(pool_made, 5)
            pe.wait_ge(chosen, 1)
            for n in range(2):
                nc.tensor.matmul(ps[:, 6 + n, :], before[:, :], hot2[:, 8 * n:8 * n + 8, :], start=True, stop=False)
                ins = nc.tensor.matmul(ps[:, 6 + n, :], ones[:, :], key[:, 8 * n:8 * n + 8, :], start=False, stop=True)
            ins.then_inc(placed, 1)
            pe.wait_ge(shares_ready, 1)
            pe.wait_ge(vb_kept, 16)
            for n in range(4):
                for j in range(4):
                    ins = nc.tensor.transpose(ps[0:E1, n, j * P:(j + 1) * P], prob[:, 4 * n + j, :], S.ident[:, :])
                ins.then_inc(share_turned, 1)

        @block.vector
        def _(dve):
            link = Links(dve, linked)
            link(nc.vector.memset(kn[:, :, :, N1:N1 + 1], -1.0))
            link(nc.vector.memset(S.vT[:, :, T:T + 1], 0.0))
            normalise(nc, dve, link, S.x1, S.xn, tmp, st, True, 1e-5, squares, roots, 0).then_inc(n_ready, 1)
            dve.wait_ge(n_ready, 1)
            normalise(nc, dve, link, S.xn, nm, tmp, st, False, 1e-6, squares, roots, 1).then_inc(m_ready, 1)
            dve.wait_ge(pool_made, 5)
            dve.wait_ge(routed, 1)
            for n in range(2):
                link(nc.vector.tensor_copy(prob[:, 8 * n:8 * n + 8, :], ps[:, 6 + n, :].rearrange("p (t e) -> p t e", e=E1)))
            link(nc.vector.tensor_reduce(val[:, 4, :], prob[:, :, :], AX.X, ALU.max))
            nc.vector.tensor_tensor(prob[:, :, :], prob[:, :, :], val[:, 4, :].unsqueeze(2).to_broadcast(wide), ALU.subtract).then_inc(shifted, 1)
            dve.wait_ge(k_kept, 8)
            sq = kn[:, :, :, 0:N1]
            link(nc.vector.tensor_tensor(sq, kraw[:, :, :].rearrange("p t (h c) -> p t h c", c=N1), kraw[:, :, :].rearrange("p t (h c) -> p t h c", c=N1), ALU.mult))
            link(nc.vector.tensor_reduce(nrm[:, 0, :].rearrange("p (t h) -> p t h", h=H1), sq, AX.X, ALU.add))
            nc.vector.tensor_copy(nrm[:, 2, :], nrm[:, 0, :]).then_inc(norms, 1)
            dve.wait_ge(norm_roots, 1)
            link(nc.vector.tensor_scalar(nrm[:, 1, :], nrm[:, 1, :], 1e-6, None, ALU.add))
            link(nc.vector.reciprocal(nrm[:, 2, :], nrm[:, 1, :]))
            for t in range(NT):
                ins = nc.vector.tensor_tensor(kn[:, t, :, 0:N1], kraw[:, t, :].rearrange("p (h c) -> p h c", c=N1),
                                              nrm[:, 2, H1 * t:H1 * t + H1].unsqueeze(2).to_broadcast([P, H1, N1]), ALU.mult)
            ins.then_inc(kn_ready, 1)
            dve.wait_ge(vb_kept, 16)
            link(nc.vector.tensor_scalar(S.beta[:, :, :], S.beta[:, :, :], 1e-30, None, ALU.max))
            for g in range(2):
                link(nc.vector.reciprocal(S.nrb[:, g, :], S.beta[:, g, :]))
                link(nc.vector.tensor_scalar(S.nrb[:, g, :], S.nrb[:, g, :], -1.0, None, ALU.mult))
            dve.wait_ge(expd, 1)
            choose_two(nc, link, prob, rev, hot1, hot2, key, val, E1)
            link(nc.vector.tensor_tensor(val[:, 3, :], val[:, 0, :], val[:, 1, :], ALU.add))
            link(nc.vector.reciprocal(val[:, 4, :], val[:, 3, :]))
            link(nc.vector.tensor_scalar(val[:, 4, :], val[:, 4, :], 0.5, None, ALU.mult))
            link(nc.vector.tensor_tensor(val[:, 0, :], val[:, 0, :], val[:, 4, :], ALU.mult))
            link(nc.vector.tensor_tensor(val[:, 1, :], val[:, 1, :], val[:, 4, :], ALU.mult))
            link(nc.vector.tensor_tensor(prob[:, :, :], hot1[:, :, :], val[:, 0, :].unsqueeze(2).to_broadcast(wide), ALU.mult))
            link(nc.vector.tensor_tensor(key[:, :, :], hot2[:, :, :], val[:, 1, :].unsqueeze(2).to_broadcast(wide), ALU.mult))
            link(nc.vector.tensor_tensor(prob[:, :, :], prob[:, :, :], key[:, :, :], ALU.add))
            link(nc.vector.tensor_tensor(hot2[:, :, :], hot1[:, :, :], hot2[:, :, :], ALU.add))
            link(nc.vector.memset(key[:, 0, :], 0.0))
            for t in range(1, NT):
                link(nc.vector.tensor_tensor(key[:, t, :], key[:, t - 1, :], hot2[:, t - 1, :], ALU.add))
            nc.vector.tensor_copy(val[:, 5, :], val[:, 4, :]).then_inc(chosen, 1)
            dve.wait_ge(placed, 1)
            for n in range(2):
                src = ps[:, 6 + n, :].rearrange("p (t e) -> p t e", e=E1)
                ins = nc.vector.scalar_tensor_tensor(prob[:, 8 * n:8 * n + 8, :].rearrange("p t e -> p (t e)"), ps[:, 6 + n, :], float(CAPACITY),
                                                     prob[:, 8 * n:8 * n + 8, :].rearrange("p t e -> p (t e)"), ALU.is_lt, ALU.mult)
            ins.then_inc(shares_ready, 1)


def recurrence(nc, S, dram):
    C = 32
    TURN = 2 * C
    TURNS = T // TURN
    PIECE = 2
    HALF = QT // 2
    ACT_AT = (12, 22, 34, 44)
    GATE_AT = (18, 28, 40, 50)
    SUM_AT = 14
    with ExitStack() as ctx:
        R = Room(nc, ctx, "w")
        SQ = S.SQ
        K, Qb = R.sb("K", [P, 2, 2, C, N1 + 1]), R.sb("Qb", [P, 2, 2, C, N1])
        KP = R.sb("KP", [P, 2, 2, C, N1])
        St = R.sb("St", [P, 2, 2, C, N1 + 1])
        PR = R.sb("PR", [P, 2, C, N1])
        X, J, ND = R.sb("X", [P, 2, 2, N1]), R.sb("J", [P, 2, N1 + 1]), R.sb("ND", [P, 2, 2, C])
        W = R.sb("W", [P, 3 * P])
        share = R.sb("share", [P, T])
        th, ga, up, h = (R.sb(n, [P, 2, QT]) for n in ("th", "ga", "up", "h"))
        ps = R.psum()
        k_loaded, q_loaded = [R.sem(f"k_loaded{i}") for i in range(2)], [R.sem(f"q_loaded{i}") for i in range(2)]
        nd_made, x_made, tanh_done = ([R.sem(f"{n}{g}") for g in range(2)] for n in ("nd_made", "x_made", "tanh_done"))
        state_zeroed, state_set, v_placed, kp_made = R.sem("state_zeroed"), R.sem("state_set"), R.sem("v_placed"), R.sem("kp_made")
        sq_multiplied, sq_summed = R.sem("sq_multiplied"), R.sem("sq_summed")
        w_loaded, up_done, taken, gate_made = (R.sem(n) for n in ("w_loaded", "up_done", "taken", "gate_made"))
        up_shared, h_ready, down_done = R.sem("up_shared"), R.sem("h_ready"), R.sem("down_done")
        block = ctx.enter_context(nc.Block())

        def wait(engine, sem, turn, per_turn, count):
            if not isinstance(turn, int) or turn * per_turn + count > 0:
                engine.wait_ge(sem, turn * per_turn + count)

        def over_turns(engine, emit):
            emit(0)
            with engine.Fori(1, TURNS - 1) as turn:
                emit(turn)
            emit(TURNS - 1)

        def first(turn):
            return isinstance(turn, int) and turn == 0

        def last(turn):
            return isinstance(turn, int) and turn == TURNS - 1

        @block.sync
        def _(sp):
            def keys(turn, c):
                for g in range(2):
                    wait(sp, x_made[g], turn, TURN, C * (c - 1))
                for g in range(2):
                    for q in range(4):
                        sp.dma_start(K[32 * q:32 * q + 32, c % 2, g, :, :].rearrange("p t c -> p (t c)"),
                                     S.KN[4 * g + q, bass.ds(turn * TURN + C * c, C), :].rearrange("t c -> (t c)").partition_broadcast(32)).then_inc(k_loaded[c % 2], 16)

            def queries(turn, c):
                wait(sp, sq_multiplied, turn, 4, 2 * (c - 1))
                for g in range(2):
                    for q in range(4):
                        sp.dma_start(Qb[32 * q:32 * q + 32, c % 2, g, :, :].rearrange("p t c -> p (t c)"),
                                     S.QN[4 * g + q, bass.ds(turn * TURN + C * c, C), :].rearrange("t c -> (t c)").partition_broadcast(32)).then_inc(q_loaded[c % 2], 16)

            def experts(turn):
                wait(sp, down_done, turn, 4, 0)
                pair = bass.ds(turn, 1)
                sp.dma_start(W[:, :], dram["experts"][pair, :, :].rearrange("a p c -> (a p) c")).then_inc(w_loaded, 16)
                for half in range(2):
                    row = S.ST[bass.ds(turn * 2 + half, 1), :].rearrange("a t -> (a t)")
                    sp.dma_start(share[64 * half:64 * half + 64, :], row.partition_broadcast(64)).then_inc(w_loaded, 16)

            def emit(turn):
                if first(turn):
                    keys(0, 0)
                    queries(0, 0)
                keys(turn, 1)
                experts(turn)
                queries(turn, 1)
                if not last(turn):
                    keys(turn, 2)
                    queries(turn, 2)
            over_turns(sp, emit)
            experts(TURNS)

        @block.vector
        def _(dve):
            def step(turn, s):
                b, t = s // C, s % C
                pb, pt = (s - 1) // C % 2, (s - 1) % C
                if t == 0:
                    wait(dve, k_loaded[b], turn, 128, 128)
                    wait(dve, kp_made, turn, 4, 2 * (b + 1))
                if t == 1:
                    wait(dve, v_placed, turn, 4, 2 * (b + 1))
                for g in range(2):
                    wait(dve, tanh_done[g], turn, TURN, s)
                    nc.vector.scalar_tensor_tensor(J[:, g, :], St[:, pb, g, pt, :], 1.0, K[:, b, g, t, :], ALU.mult, ALU.mult,
                                                   accum_out=ND[:, b, g, t:t + 1]).then_inc(nd_made[g], 1)
                    wait(dve, nd_made[g], turn, TURN, s + 1)
                    nc.vector.scalar_tensor_tensor(X[:, g, s % 2, :], KP[:, b, g, t, :], ND[:, b, g, t:t + 1], St[:, pb, g, pt, 0:N1],
                                                   ALU.mult, ALU.add).then_inc(x_made[g], 1)

            def sum_piece(turn, c, n):
                if n == 0:
                    wait(dve, sq_multiplied, turn, 4, 2 * (c + 1))
                nc.vector.tensor_reduce(SQ[:, :, bass.ds(turn * TURN + (C * c + PIECE * n), PIECE)], PR[:, :, PIECE * n:PIECE * (n + 1), :],
                                        AX.X, ALU.add).then_inc(sq_summed, 1)

            def gate(turn, c, n):
                if n == 0:
                    wait(dve, taken, turn, 16, 4 * c + 2)
                    wait(dve, h_ready, turn, 4, c - 1)
                part = slice(P * n, P * n + P)
                nc.vector.scalar_tensor_tensor(ga[:, c % 2, part], th[:, c % 2, part], 1.0, ps[:, 2 * (c % 2), part],
                                               ALU.add, ALU.mult).then_inc(gate_made, 1)

            def emit(turn):
                if first(turn):
                    dve.wait_ge(state_set, 2)
                for s in range(TURN):
                    step(turn, s)
                    for c, at in enumerate(GATE_AT):
                        if at <= s < at + 4:
                            gate(turn, c, s - at)
                    n = s % C - SUM_AT
                    if 0 <= n < C // PIECE and not (first(turn) and s < C):
                        if s < C:
                            sum_piece(turn - 1, 1, n)
                        else:
                            sum_piece(turn, 0, n)
            over_turns(dve, emit)
            for n in range(C // PIECE):
                sum_piece(TURNS - 1, 1, n)
            for c in range(4):
                for n in range(4):
                    gate(TURNS, c, n)
            dve.wait_ge(sq_summed, T // PIECE)

        @block.scalar
        def _(act):
            def piece(turn, c, n):
                kind, half = divmod(n, 2)
                if n == 0:
                    wait(act, up_done, turn, 4, c + 1)
                    wait(act, gate_made, turn, 16, 4 * (c - 1))
                elif n == 2:
                    wait(act, h_ready, turn, 4, c - 1)
                src = ps[:, 2 * (c % 2) + kind, HALF * half:HALF * (half + 1)]
                dst = (th, up)[kind][:, c % 2, HALF * half:HALF * (half + 1)]
                nc.scalar.activation(dst, src, (ACT.Tanh, ACT.Copy)[kind], scale=(0.5, 1.0)[kind]).then_inc(taken, 1)

            def emit(turn):
                for s in range(TURN):
                    b, t = s // C, s % C
                    if t == 0:
                        wait(act, sq_multiplied, turn, 4, 2 * (b - 1))
                    for g in range(2):
                        wait(act, x_made[g], turn, TURN, s + 1)
                        nc.scalar.activation(St[:, b, g, t, 0:N1], X[:, g, s % 2, :], ACT.Tanh,
                                             scale=S.beta[:, g, bass.ds(turn * TURN + s, 1)]).then_inc(tanh_done[g], 1)
                    for c, at in enumerate(ACT_AT):
                        if at <= s < at + 4:
                            piece(turn, c, s - at)
            over_turns(act, emit)
            for c in range(4):
                for n in range(4):
                    piece(TURNS, c, n)
            for c in range(4):
                act.wait_ge(down_done, 4 * TURNS + c + 1)
                nc.scalar.activation(S.mixT[:, QT * c:QT * c + QT], ps[:, 4 + c, :], ACT.Copy).then_inc(taken, 1)
            act.wait_ge(taken, 16 * (TURNS + 1) + 4)

        @block.gpsimd
        def _(pool):
            def values(turn, c):
                for g in range(2):
                    wait(pool, x_made[g], turn, TURN, C * (c - 1) + 1)
                    nc.gpsimd.tensor_copy(St[:, c % 2, g, :, N1:N1 + 1], S.vT[:, g, bass.ds(turn * TURN + (C * c + 1), C)].unsqueeze(2)).then_inc(v_placed, 1)

            def keys_over_beta(turn, c):
                wait(pool, k_loaded[c % 2], turn, 128, 128 * (c // 2 + 1))
                for g in range(2):
                    wait(pool, x_made[g], turn, TURN, C * (c - 1))
                    nb = S.nrb[:, g, bass.ds(turn * TURN + C * c, C)].unsqueeze(2).to_broadcast([P, C, N1])
                    nc.gpsimd.tensor_tensor(KP[:, c % 2, g, :, :], K[:, c % 2, g, :, 0:N1], nb, ALU.mult).then_inc(kp_made, 1)

            def times_queries(turn, c):
                wait(pool, q_loaded[c % 2], turn, 128, 128 * (c // 2 + 1))
                wait(pool, sq_summed, turn, TURN // PIECE, C // PIECE * c)
                for g in range(2):
                    wait(pool, tanh_done[g], turn, TURN, C * (c + 1))
                    nc.gpsimd.tensor_tensor(PR[:, g, :, :], St[:, c % 2, g, :, 0:N1], Qb[:, c % 2, g, :, :], ALU.mult).then_inc(sq_multiplied, 1)

            def hidden(turn, c):
                wait(pool, taken, turn, 16, 4 * c + 4)
                wait(pool, w_loaded, turn, 48, 48)
                nc.gpsimd.tensor_tensor(up[:, c % 2, :], up[:, c % 2, :], share[:, QT * c:QT * c + QT], ALU.mult).then_inc(up_shared, 1)
                wait(pool, up_shared, turn, 4, c + 1)
                wait(pool, gate_made, turn, 16, 4 * c + 4)
                wait(pool, down_done, turn, 4, c - 1)
                nc.gpsimd.tensor_tensor(h[:, c % 2, :], up[:, c % 2, :], ga[:, c % 2, :], ALU.mult).then_inc(h_ready, 1)

            def emit(turn):
                if first(turn):
                    nc.gpsimd.memset(St[:, 1, :, C - 1, 0:N1], 0.0).then_inc(state_set, 1)
                    nc.gpsimd.tensor_copy(St[:, 1, :, C - 1, N1:N1 + 1], S.vT[:, :, 0:1]).then_inc(state_set, 1)
                    values(0, 0)
                    keys_over_beta(0, 0)
                values(turn, 1)
                if not first(turn):
                    times_queries(turn - 1, 1)
                keys_over_beta(turn, 1)
                hidden(turn, 0)
                hidden(turn, 1)
                if not last(turn):
                    values(turn, 2)
                times_queries(turn, 0)
                if not last(turn):
                    keys_over_beta(turn, 2)
                hidden(turn, 2)
                hidden(turn, 3)
            over_turns(pool, emit)
            times_queries(TURNS - 1, 1)
            for c in range(4):
                hidden(TURNS, c)

        @block.tensor
        def _(pe):
            def ups(turn, c):
                if c == 0:
                    wait(pe, w_loaded, turn, 48, 48)
                wait(pe, taken, turn, 16, 4 * (c - 1))
                wait(pe, gate_made, turn, 16, 4 * (c - 1))
                for k in range(2):
                    ins = nc.tensor.matmul(ps[:, 2 * (c % 2) + k, :], W[:, P * k:P * k + P], S.mT[:, QT * c:QT * c + QT], start=True, stop=True)
                ins.then_inc(up_done, 1)

            def downs(turn, c):
                wait(pe, h_ready, turn, 4, c + 1)
                nc.tensor.matmul(ps[:, 4 + c, :], W[:, 2 * P:3 * P], h[:, c % 2, :], start=first(turn),
                                 stop=isinstance(turn, int) and turn == TURNS).then_inc(down_done, 1)

            def emit(turn):
                for c in range(4):
                    ups(turn, c)
                    if c:
                        downs(turn, c - 1)
                downs(turn, 3)
            over_turns(pe, emit)
            emit(TURNS)


def finish(nc, S, dram, out):
    with ExitStack() as ctx:
        R = Room(nc, ctx, "f")
        sg, WoutT = R.sb("sg", [P, 2, T]), R.sb("WoutT", [P, 2, D])
        gate, y = R.sb("gate", [P, NT, D]), R.sb("y", [P, NT, D])
        ps = R.psum()
        loaded, sig, out_made, turned, residual, silu, projected, times, result, stored = (
            R.sem(n) for n in ("loaded", "sig", "out_made", "turned", "residual", "silu", "projected", "times", "result", "stored"))
        squared = R.sem("squared")
        block = ctx.enter_context(nc.Block())

        @block.sync
        def _(sp):
            for g in range(2):
                sp.dma_start(WoutT[:, g, :], dram["WoutT"][g, :, :]).then_inc(loaded, 16)
            for n in range(4):
                sp.wait_ge(result, n + 1)
                for t in range(4 * n, 4 * n + 4):
                    sp.dma_start(out[t * P:(t + 1) * P, :], y[:, t, :]).then_inc(stored, 16)
            sp.wait_ge(stored, 16 * NT)

        @block.scalar
        def _(act):
            for g in range(2):
                nc.scalar.activation(sg[:, g, :], S.SQ[:, g, :], ACT.Silu).then_inc(sig, 1)
            for n in range(4):
                act.wait_ge(residual, n + 1)
                nc.scalar.activation(gate[:, 4 * n:4 * n + 4, :], gate[:, 4 * n:4 * n + 4, :], ACT.Silu).then_inc(silu, 1)

        @block.tensor
        def _(pe):
            for n in range(4):
                for j in range(4):
                    ins = nc.tensor.transpose(ps[:, n, j * P:(j + 1) * P], S.mixT[:, (4 * n + j) * P:(4 * n + j + 1) * P], S.ident[:, :])
                ins.then_inc(turned, 1)
            pe.wait_ge(loaded, 32)
            pe.wait_ge(out_made, 2)
            for n in range(4):
                for j in range(4):
                    t = 4 * n + j
                    for g in range(2):
                        ins = nc.tensor.matmul(ps[:, 4 + n, j * P:(j + 1) * P], sg[:, g, t * P:(t + 1) * P], WoutT[:, g, :], start=g == 0, stop=g == 1)
                ins.then_inc(projected, 1)

        @block.vector
        def _(dve):
            for g in range(2):
                dve.wait_ge(sig, g + 1)
                nc.vector.tensor_tensor(sg[:, g, :], sg[:, g, :], S.SQ[:, g, :], ALU.mult).then_inc(out_made, 1)
            for n in range(4):
                dve.wait_ge(turned, n + 1)
                nc.vector.tensor_tensor(gate[:, 4 * n:4 * n + 4, :], ps[:, n, :].rearrange("p (j d) -> p j d", d=D), S.xn[:, 4 * n:4 * n + 4, :], ALU.add).then_inc(residual, 1)
            for n in range(4):
                part = slice(4 * n, 4 * n + 4)
                dve.wait_ge(silu, n + 1)
                dve.wait_ge(projected, n + 1)
                nc.vector.tensor_tensor(y[:, part, :], ps[:, 4 + n, :].rearrange("p (j d) -> p j d", d=D), gate[:, part, :], ALU.mult).then_inc(times, 1)
                dve.wait_ge(times, n + 1)
                nc.vector.tensor_tensor(y[:, part, :], y[:, part, :], S.x1[:, part, :], ALU.add).then_inc(result, 1)


def build_program(nc, dram, out, upto=99):
    ctx = ExitStack()
    with ctx:
        R = Room(nc, ctx, "s")
        S = Shared()
        S.scale_f = float(np.float32(1.0) / np.sqrt(np.float32(32.0)))
        S.KD, S.QD = nc.dram_tensor("KD", [NQ, 3, 2 * P, T], BF16).ap(), nc.dram_tensor("QD", [3, 3, 2 * P, T], BF16).ap()
        S.KDF, S.QDF = nc.dram_tensor("KDF", [3, 32, T], BF16).ap(), nc.dram_tensor("QDF", [3, P, T], BF16).ap()
        S.GD = nc.dram_tensor("GD", [16, P, GW], F32).ap()
        S.scale = float(np.float32(1.0) / np.sqrt(np.float32(8.0)))
        S.ident, S.bv, S.bo = R.sb("ident", [P, P]), R.sb("bv", [P, D]), R.sb("bo", [P, D])
        S.selo, S.selo2 = R.sb("selo", [P, 32]), R.sb("selo2", [P, 64])
        S.spread = R.sb("spread", [P, P], BF16)
        S.low_row = R.sb("low_row", [2, 1])
        S.rbias = R.sb("rbias", [P, 8])
        S.g, S.cols, S.dwb = R.sb("g", [P, 3]), R.sb("cols", [P, 10]), R.sb("dwb", [P, 2, 32])
        S.xn, S.xnT = R.sb("xn", [P, NT, D]), R.sb("xnT", [P, T])
        S.x1 = S.xnT[:, :].rearrange("p (t d) -> p t d", d=D)
        constants(nc, S, dram)
        with ExitStack() as attn:
            A = Room(nc, attn, "a")
            S.Vp, S.Vcp = A.sb("Vp", [P, NT, 16, 32]), A.sb("Vcp", [P, NT, 64])
            with ExitStack() as proj:
                B = Room(nc, proj, "q")
                S.Q2, S.K2 = B.sb("Q2", [P, 2, T]), B.sb("K2", [P, 2, T])
                S.QF, S.KF = B.sb("QF", [P, T]), B.sb("KF", [P, T])
                prepare(nc, S, dram)
                if upto < 2: return
                pieces(nc, S)
            S.AO, S.AOF = A.sb("AO", [P, NT, D]), A.sb("AOF", [P, NT, D])
            if upto < 3: return
            if upto != 4: attention(nc, S, Attention(16, 8, 32, True))
            attention(nc, S, Attention(4, 32, 64, False))
            if upto < 5: return
            mixture0(nc, S, dram)
        if upto < 6: return
        S.KN, S.QN = nc.dram_tensor("KN", [H1, T, N1 + 1], F32).ap(), nc.dram_tensor("QN", [H1, T, N1], F32).ap()
        S.ST = nc.dram_tensor("ST", [E1 + 2, T], F32).ap()
        S.vT, S.beta, S.nrb = R.sb("vT", [P, 2, T + 1]), R.sb("beta", [P, 2, T]), R.sb("nrb", [P, 2, T])
        S.mT = R.sb("mT", [P, T])
        prepare1(nc, S, dram)
        if upto < 7: return
        S.SQ = R.sb("SQ", [P, 2, T])
        S.mixT = S.mT
        recurrence(nc, S, dram)
        finish(nc, S, dram, out)


def layout(i):
    a = {}
    a["x"] = i["L0_attn_x"][0]
    for n in ("Wq", "Wk", "Wv", "Wo"):
        a[n + "T"] = i[f"L0_attn_{n}"].T
    for n in ("bq", "bk", "bv", "bo"):
        a[n] = i[f"L0_attn_{n}"]
    a["decay"], a["mix"] = i["L0_attn_decay_params"].reshape(-1), i["L0_attn_mix_weights"].reshape(-1)
    a["fWqT"], a["WkcT"], a["WvcT"], a["fWoT"] = (i[f"L0_ffn_{n}"].T for n in ("Wq", "Wkc", "Wvc", "Wo"))
    a["g"] = np.stack([i["L0_ffn_g1"], i["L0_ffn_g2"], i["L1_ffn_rms_w"]], axis=1)
    a["WrT"], a["rb"] = i["L0_ffn_Wr"].T, i["L0_ffn_expert_bias"]
    for n in ("W1", "W3", "W2"):
        a["e" + n] = np.concatenate([i[f"L0_ffn_e{n}"], i[f"L0_ffn_s{n}"][None]]).transpose(0, 2, 1)
    a["WinT"] = i["L1_attn_W_in"].T
    for n in ("k", "q", "v"):
        a[f"rW{n}T"] = i[f"L1_attn_W_{n}"].T
    a["rWbT"], a["bbeta"] = i["L1_attn_W_beta"].T, i["L1_attn_b_beta"].reshape(2, P).T
    a["WoutT"] = i["L1_attn_W_out"].T.reshape(2, P, D)
    a["gateT"] = i["L1_ffn_gate_w"].T
    w13, empty = i["L1_ffn_w13"].reshape(E1 // 2, 2, D, 2, I1), np.zeros((D, I1), i["L1_ffn_w13"].dtype)
    halves = [np.concatenate([w13[:, 0, :, k], w13[:, 1, :, k]], axis=2) for k in range(2)]
    pairs = np.concatenate(halves + [i["L1_ffn_w2"].reshape(E1 // 2, P, D)], axis=2)
    last = np.concatenate([i["L1_ffn_sw_gate"], empty, i["L1_ffn_sw_up"], empty,
                           np.concatenate([i["L1_ffn_sw_down"], empty.T], axis=0)], axis=1)
    a["experts"] = np.concatenate([pairs, last[None]])
    return {k: np.ascontiguousarray(v) for k, v in a.items()}


def kernel(**inputs):
    import concourse.bacc as bacc
    from concourse.bass_utils import run_bass_kernel_spmd

    arrays = layout({k: np.asarray(v) for k, v in inputs.items()})
    nc = bacc.Bacc("TRN2", target_bir_lowering=False, num_devices=1)
    dram = {n: nc.dram_tensor(f"in_{n}", a.shape, mybir.dt.from_np(a.dtype), kind="ExternalInput").ap() for n, a in arrays.items()}
    shape = inputs["L0_attn_x"].shape
    out = nc.dram_tensor("out", shape, F32, kind="ExternalOutput").ap()
    build_program(nc, dram, out[0])
    r = run_bass_kernel_spmd(nc, [{f"in_{n}": a for n, a in arrays.items()}], core_ids=[0])
    return r.results[0]["out"]
```

```python
from contextlib import ExitStack

import numpy as np
import concourse.bass as bass
from concourse import mybir

F32 = mybir.dt.float32
BF16 = mybir.dt.bfloat16
ALU = mybir.AluOpType
ACT = mybir.ActivationFunctionType
AX = mybir.AxisListType

P = 128
D = 128
T = 2048
NT = T // P
QT = 512
NQ = T // QT
GW = 2 * QT - P
LEAST = -3.0e38
SPLIT_K = (0, 0, 1, 0, 1, 2)
SPLIT_Q = (0, 1, 0, 2, 1, 0)


class Links:

    def __init__(self, engine, sem):
        self.engine, self.sem, self.n = engine, sem, 0

    def __call__(self, ins):
        ins.then_inc(self.sem, 1)
        self.n += 1
        self.engine.wait_ge(self.sem, self.n)


class Shared:
    pass


class Room:

    def __init__(self, nc, ctx, tag):
        self.nc, self.ctx, self.tag = nc, ctx, tag
        ctx.enter_context(nc.cleanup_on_exit())

    def sb(self, name, shape, dt=F32):
        return self.ctx.enter_context(self.nc.sbuf_tensor(f"{self.tag}_{name}", shape, dt))

    def psum(self):
        return self.ctx.enter_context(self.nc.psum_tensor(f"{self.tag}_ps", [P, 8, QT], F32))

    def sem(self, name):
        return self.nc.alloc_semaphore(name=f"{self.tag}_{name}")


def normalise(nc, dve, link, src, dst, tmp, st, center, eps, squares_ready, roots_ready, n):
    if center:
        link(nc.vector.tensor_reduce(st[:, 0, :], src[:, :, :], AX.X, ALU.add))
        link(nc.vector.tensor_scalar(st[:, 0, :], st[:, 0, :], 1.0 / D, None, ALU.mult))
        link(nc.vector.tensor_tensor(dst[:, :, :], src[:, :, :],
                                     st[:, 0, :].unsqueeze(2).to_broadcast([P, NT, D]), ALU.subtract))
        src = dst
    link(nc.vector.tensor_tensor(tmp[:, :, :], src[:, :, :], src[:, :, :], ALU.mult))
    link(nc.vector.tensor_reduce(st[:, 1, :], tmp[:, :, :], AX.X, ALU.add))
    nc.vector.tensor_scalar(st[:, 1, :], st[:, 1, :], 1.0 / D, eps, ALU.mult, ALU.add).then_inc(squares_ready, 1)
    dve.wait_ge(roots_ready, n + 1)
    link(nc.vector.reciprocal(st[:, 3, :], st[:, 2, :]))
    return nc.vector.tensor_tensor(dst[:, :, :], src[:, :, :],
                                   st[:, 3, :].unsqueeze(2).to_broadcast([P, NT, D]), ALU.mult)


def constants(nc, S, dram):
    with ExitStack() as ctx:
        R = Room(nc, ctx, "c")
        zeroed, placed, loaded = R.sem("zeroed"), R.sem("placed"), R.sem("loaded")
        block = ctx.enter_context(nc.Block())

        @block.sync
        def _(sp):
            for n, dst in (("bv", S.bv), ("bo", S.bo), ("rb", S.rbias)):
                sp.dma_start(dst[:, :], dram[n].partition_broadcast(P)).then_inc(loaded, 16)
            sp.wait_ge(loaded, 48)

        @block.gpsimd
        def _(pool):
            nc.gpsimd.memset(S.ident[:, :], 0.0).then_inc(zeroed, 1)
            nc.gpsimd.memset(S.selo[:, :], 0.0).then_inc(zeroed, 1)
            nc.gpsimd.memset(S.spread[:, :], 0.0).then_inc(zeroed, 1)
            pool.wait_ge(zeroed, 3)
            nc.gpsimd.affine_select(out=S.ident[:, :], in_=S.ident[:, :], compare_op=ALU.not_equal, fill=1.0,
                                    base=0, pattern=[[-1, P]], channel_multiplier=1).then_inc(placed, 1)
            for g in range(4):
                nc.gpsimd.affine_select(out=S.selo[:, :], in_=S.selo[:, :], compare_op=ALU.not_equal, fill=1.0,
                                        base=-32 * g, pattern=[[-1, 32]], channel_multiplier=1).then_inc(placed, 1)
                pool.wait_ge(placed, 2 + g)
            nc.gpsimd.memset(S.spread[96:98, :], 1.0).then_inc(placed, 1)
            pool.wait_ge(placed, 6)


def prepare(nc, S, dram):
    with ExitStack() as ctx:
        R = Room(nc, ctx, "p")
        x, nx = R.sb("x", [P, NT, D]), R.sb("nx", [P, NT, D])
        tmp, st = R.sb("tmp", [P, NT, D]), R.sb("st", [P, 4, NT])
        n1T = R.sb("n1T", [P, T])
        W = R.sb("W", [P, 6, D])
        Wd = R.sb("Wd", [P, 4, D])
        prow = R.sb("prow", [1, 2, D])
        pdup = R.sb("pdup", [1, 9, D])
        dec = R.sb("dec", [1, 12, 32])
        one = R.sb("one", [1, P])
        cols = S.cols
        ps = R.psum()
        x_loaded, w_loaded, par_loaded = R.sem("x_loaded"), R.sem("w_loaded"), R.sem("par_loaded")
        squares, roots = R.sem("squares"), R.sem("roots")
        linked, xn_ready, nx_ready = R.sem("linked"), R.sem("xn_ready"), R.sem("nx_ready")
        wd_ready, clipped, logged = R.sem("wd_ready"), R.sem("clipped"), R.sem("logged")
        shifted, expd, rows_ready, cols_done, cols_kept = (R.sem(n) for n in ("shifted", "expd", "rows", "cols", "colk"))
        a_filled, a_kept, v_filled, v_kept = (R.sem(n) for n in ("a_filled", "a_kept", "v_filled", "v_kept"))
        block = ctx.enter_context(nc.Block())
        filled = R.sem("filled")
        NA = 32

        @block.gpsimd
        def _(pool):
            nc.gpsimd.memset(S.Vp[:, :, :, :], 0.0).then_inc(filled, 1)
            nc.gpsimd.memset(S.Vcp[:, :, :], 0.0).then_inc(filled, 1)
            pool.wait_ge(filled, 2)
            nc.gpsimd.memset(S.Vp[:, :, :, 8:9], 1.0).then_inc(filled, 1)
            nc.gpsimd.memset(S.Vcp[:, :, 32:33], 1.0).then_inc(filled, 1)

        @block.sync
        def _(sp):
            for t in range(NT):
                sp.dma_start(x[:, t, :], dram["x"][t * P:(t + 1) * P, :]).then_inc(x_loaded, 16)
            for n, name in enumerate(("WqT", "WkT", "WvT", "fWqT")):
                sp.dma_start(W[:, n, :], dram[name]).then_inc(w_loaded, 16)
            sp.dma_start(W[:, 4, 0:32], dram["WkcT"]).then_inc(w_loaded, 16)
            sp.dma_start(W[:, 5, 0:32], dram["WvcT"]).then_inc(w_loaded, 16)
            sp.dma_start(S.g[:, :], dram["g"]).then_inc(w_loaded, 16)
            sp.dma_start(prow[0:1, 0, :], dram["bq"].unsqueeze(0)).then_inc(par_loaded, 16)
            sp.dma_start(prow[0:1, 1, :], dram["bk"].unsqueeze(0)).then_inc(par_loaded, 16)
            sp.dma_start(dec[0:1, 0, :], dram["decay"].unsqueeze(0)).then_inc(par_loaded, 16)
            sp.dma_start(dec[0:1, 1, :], dram["mix"].unsqueeze(0)).then_inc(par_loaded, 16)
            sp.wait_ge(w_loaded, 16 * 7)
            sp.wait_ge(par_loaded, 16 * 4)

        @block.scalar
        def _(act):
            for n in range(2):
                act.wait_ge(squares, n + 1)
                nc.scalar.activation(st[:, 2, :], st[:, 1, :], ACT.Sqrt).then_inc(roots, 1)
            dst = ([(S.xnT[:, :], None)] + [(n1T[:, :], S.g[:, 0:1])]
                   + [(S.Q2[:, i, :], cols[:, i:i + 1]) for i in range(2)]
                   + [(S.K2[:, i, :], cols[:, 2 + i:3 + i]) for i in range(2)] + [(S.QF[:, :], None), (S.KF[0:32, :], None)])
            for n in range(NA):
                if n == 4:
                    act.wait_ge(clipped, 1)
                    nc.scalar.activation(dec[0:1, 3, :], dec[0:1, 2, :], ACT.Ln).then_inc(logged, 1)
                    act.wait_ge(shifted, 1)
                    nc.scalar.activation(dec[0:1, 5, :], dec[0:1, 4, :], ACT.Exp).then_inc(expd, 1)
                    act.wait_ge(w_loaded, 16 * 7)
                if n == 8:
                    act.wait_ge(cols_done, 1)
                    nc.scalar.activation(cols[:, :], ps[:, 7, 0:10], ACT.Copy).then_inc(cols_kept, 1)
                    act.wait_ge(cols_kept, 1)
                out, par = dst[n // 4]
                rows = out.shape[0]
                out = out[:, (n % 4) * QT:(n % 4 + 1) * QT]
                act.wait_ge(a_filled, n + 1)
                src = ps[0:rows, n % 4, :]
                if par is None:
                    ins = nc.scalar.activation(out, src, ACT.Copy)
                elif n // 4 == 1:
                    ins = nc.scalar.activation(out, src, ACT.Copy, scale=par)
                else:
                    ins = nc.scalar.activation(out, src, ACT.Identity, bias=par)
                ins.then_inc(a_kept, 1)

        @block.tensor
        def _(pe):
            for n in range(NA):
                if n >= 4:
                    pe.wait_ge(a_kept, n - 3)
                kind, c = n // 4, n % 4
                if kind < 2:
                    pe.wait_ge((xn_ready, nx_ready)[kind], 1)
                    for j in range(4):
                        last = nc.tensor.transpose(ps[:, c, j * P:(j + 1) * P],
                                                   (S.xn, nx)[kind][:, 4 * c + j, :], S.ident[:, :])
                    last.then_inc(a_filled, 1)
                    continue
                if kind == 2 and c == 0:
                    pe.wait_ge(rows_ready, 1)
                    for k in range(9):
                        nc.tensor.matmul(ps[:, 7, k:k + 1], pdup[0:1, k, :], one[0:1, 0:1], start=True, stop=True)
                    last = nc.tensor.matmul(ps[:, 7, 9:10], one[0:1, :], one[0:1, 0:1], start=True, stop=True)
                    last.then_inc(cols_done, 1)
                    last = nc.tensor.matmul(ps[:, 6, 0:64], one[0:1, :], dec[0:1, 10:12, :], start=True, stop=True)
                    last.then_inc(cols_done, 1)
                    pe.wait_ge(w_loaded, 16 * 7)
                    pe.wait_ge(wd_ready, 1)
                if kind < 6:
                    w, r = Wd[:, kind - 2, :], S.xnT
                else:
                    w, r = (W[:, 3, :], W[:, 4, 0:32])[kind - 6], n1T
                rows = w.shape[1]
                nc.tensor.matmul(ps[0:rows, c, :], w, r[:, c * QT:(c + 1) * QT], start=True, stop=True).then_inc(a_filled, 1)
            for c in range(4):
                if c >= 2:
                    pe.wait_ge(v_kept, c - 1)
                for j in range(4):
                    t = 4 * c + j
                    last = nc.tensor.matmul(ps[:, 4 + c % 2, j * P:(j + 1) * P], S.xnT[:, t * P:(t + 1) * P], W[:, 2, :],
                                            start=True, stop=True)
                last.then_inc(v_filled, 1)
            pe.wait_ge(v_kept, 3)
            for t in range(NT):
                last = nc.tensor.matmul(ps[:, 4, t * 32:(t + 1) * 32], n1T[:, t * P:(t + 1) * P], W[:, 5, 0:32],
                                        start=True, stop=True)
            last.then_inc(v_filled, 1)

        @block.vector
        def _(dve):
            link = Links(dve, linked)
            link(nc.vector.memset(one[:, :], 1.0))
            dve.wait_ge(x_loaded, 16 * NT)
            normalise(nc, dve, link, x, S.xn, tmp, st, True, 1e-5, squares, roots, 0).then_inc(xn_ready, 1)
            dve.wait_ge(xn_ready, 1)
            normalise(nc, dve, link, S.xn, nx, tmp, st, False, 1e-6, squares, roots, 1).then_inc(nx_ready, 1)
            dve.wait_ge(par_loaded, 64)
            nc.vector.tensor_scalar(dec[0:1, 2, :], dec[0:1, 0, :], 0.01, 0.9999, ALU.max, ALU.min).then_inc(clipped, 1)
            mix = dec[0:1, 1, :].rearrange("p (h n) -> p h n", n=2)
            link(nc.vector.tensor_reduce(dec[0:1, 6, 0:16], mix, AX.X, ALU.max))
            nc.vector.tensor_tensor(dec[0:1, 4, :].rearrange("p (h n) -> p h n", n=2), mix,
                                    dec[0:1, 6, 0:16].unsqueeze(2).to_broadcast([1, 16, 2]), ALU.subtract).then_inc(shifted, 1)
            dve.wait_ge(expd, 1)
            ex = dec[0:1, 5, :].rearrange("p (h n) -> p h n", n=2)
            link(nc.vector.tensor_reduce(dec[0:1, 7, 0:16], ex, AX.X, ALU.add))
            link(nc.vector.reciprocal(dec[0:1, 8, 0:16], dec[0:1, 7, 0:16]))
            link(nc.vector.tensor_tensor(dec[0:1, 11, :].rearrange("p (h n) -> p h n", n=2), ex,
                                         dec[0:1, 8, 0:16].unsqueeze(2).to_broadcast([1, 16, 2]), ALU.mult))
            dve.wait_ge(logged, 1)
            link(nc.vector.tensor_copy(dec[0:1, 10, :], dec[0:1, 3, :]))
            link(nc.vector.tensor_scalar(dec[0:1, 9, :], dec[0:1, 11, :], S.scale, None, ALU.mult))
            for i in range(2):
                for n in range(2):
                    def dup(c):
                        return pdup[0:1, c, :].rearrange("p (h n d) -> p h n d", n=2, d=8)[:, :, n, :]
                    for c in range(2):
                        link(nc.vector.tensor_copy(dup(2 * c + i), prow[0:1, c, 64 * i:64 * i + 64].rearrange("p (h d) -> p h d", d=8)))
                    for c, r in ((4, 10), (6, 9)):
                        v = dec[0:1, r, 16 * i:16 * i + 16].rearrange("p (h n) -> p h n", n=2)[:, :, n:n + 1]
                        link(nc.vector.tensor_copy(dup(c + i), v.to_broadcast([1, 8, 8])))
            link(nc.vector.memset(pdup[0:1, 8, :], 0.0))
            nc.vector.memset(pdup[0:1, 8, :].rearrange("p (h n d) -> p h n d", n=2, d=8)[:, :, 0, :], S.scale).then_inc(rows_ready, 1)
            dve.wait_ge(w_loaded, 16 * 7)
            for c in range(4):
                for n in range(2):
                    link(nc.vector.tensor_copy(Wd[:, c, :].rearrange("p (h n d) -> p h n d", n=2, d=8)[:, :, n, :],
                                               W[:, c // 2, 64 * (c % 2):64 * (c % 2) + 64].rearrange("p (h d) -> p h d", d=8)))
            nc.vector.tensor_copy(Wd[0:1, 0, 0:1], Wd[0:1, 0, 0:1]).then_inc(wd_ready, 1)
            dve.wait_ge(filled, 4)
            dve.wait_ge(cols_done, 2)
            link(nc.vector.tensor_copy(S.dwb[:, :, :], ps[:, 6, 0:64].rearrange("p (c n) -> p c n", c=2)))
            for c in range(4):
                dve.wait_ge(v_filled, c + 1)
                nc.vector.tensor_tensor(S.Vp[:, 4 * c:4 * c + 4, :, 0:8],
                                        ps[:, 4 + c % 2, :].rearrange("p (j h d) -> p j h d", j=4, d=8),
                                        S.bv[:, :].rearrange("p (h d) -> p h d", d=8).unsqueeze(1).to_broadcast([P, 4, 16, 8]),
                                        ALU.add).then_inc(v_kept, 1)
            dve.wait_ge(v_filled, 5)
            link(nc.vector.tensor_copy(S.Vcp[:, :, 0:32], ps[:, 4, :].rearrange("p (t c) -> p t c", c=32)))



def pieces(nc, S):
    with ExitStack() as ctx:
        R = Room(nc, ctx, "d")
        fw, rv = R.sb("fw", [P, 2, T]), R.sb("rv", [P, 2, T])
        full = R.sb("full", [P, 2, T])
        rest = R.sb("rest", [P, 2, T])
        up, down = rest[:, 0, :], rest[:, 1, :]
        cut = R.sb("cut", [P, 2, 3, T], BF16)
        dist = R.sb("dist", [P, GW])
        def ge(h, n):
            return full[:, h % 2, n * GW:(n + 1) * GW]
        g = R.sb("g", [P, 3, GW])
        iotas, fw_ready, rv_ready, made, high, rested, middle, low = (
            R.sem(n) for n in ("iotas", "fw_ready", "rv_ready", "made", "high", "rested", "middle", "low"))
        linked, ge_ready, g_ready, near_ready = (R.sem(n) for n in ("linked", "ge_ready", "g_ready", "near_ready"))
        piece_written = [[R.sem(f"piece{c}_written{m}") for m in range(2)] for c in range(3)]
        mask_written = [R.sem(f"mask_written{m}") for m in range(3)]
        block = ctx.enter_context(nc.Block())
        jobs = [(i, k, v) for i in range(2) for k, vs in (("k", range(4)), ("q", range(3))) for v in vs] + [(2, "k", 0), (2, "q", 0)]

        def rows(n):
            return 32 if jobs[n][:2] == (2, "k") else P

        @block.gpsimd
        def _(pool):
            nc.gpsimd.iota(up, [[1, T]], base=0, channel_multiplier=0, allow_small_or_imprecise_dtypes=True).then_inc(iotas, 1)
            nc.gpsimd.iota(down, [[-1, T]], base=T - 1, channel_multiplier=0, allow_small_or_imprecise_dtypes=True).then_inc(iotas, 1)
            nc.gpsimd.iota(dist[:, :], [[1, GW]], base=-(QT - P), channel_multiplier=-1, allow_small_or_imprecise_dtypes=True).then_inc(iotas, 1)
            for n in range(len(jobs)):
                r = rows(n)
                pool.wait_ge(high, n + 1)
                if n >= 2:
                    pool.wait_ge(low, n - 1)
                nc.gpsimd.tensor_tensor(rest[0:r, n % 2, :], full[0:r, n % 2, :], cut[0:r, n % 2, 0, :], ALU.subtract).then_inc(rested, 1)

        @block.scalar
        def _(act):
            act.wait_ge(iotas, 3)
            for i in range(2):
                nc.scalar.activation(fw[:, i, :], up, ACT.Exp, scale=S.cols[:, 4 + i:5 + i]).then_inc(fw_ready, 1)
                nc.scalar.activation(rv[:, i, :], down, ACT.Exp, scale=S.cols[:, 4 + i:5 + i]).then_inc(rv_ready, 1)
            act.wait_ge(near_ready, 2)
            for h in range(16):
                if h >= 2:
                    act.wait_ge(g_ready, h - 1)
                for n in range(2):
                    nc.scalar.activation(ge(h, n), dist[:, :], ACT.Exp, scale=S.dwb[:, 0, 2 * h + n:2 * h + n + 1]).then_inc(ge_ready, 1)

            def cut_middle(n):
                r = rows(n)
                act.wait_ge(rested, n + 1)
                if n >= 2:
                    act.wait_ge(piece_written[1][n % 2], 16 * (n // 2))
                    act.wait_ge(low, n - 1)
                nc.scalar.activation(cut[0:r, n % 2, 1, :], rest[0:r, n % 2, :], ACT.Copy).then_inc(middle, 1)

            for n in range(len(jobs)):
                r = rows(n)
                act.wait_ge(made, n + 1)
                if n >= 2:
                    act.wait_ge(piece_written[0][n % 2], 16 * (n // 2))
                    act.wait_ge(rested, n - 1)
                nc.scalar.activation(cut[0:r, n % 2, 0, :], full[0:r, n % 2, :], ACT.Copy).then_inc(high, 1)
                if n >= 1:
                    cut_middle(n - 1)
            cut_middle(len(jobs) - 1)

        @block.vector
        def _(dve):
            link = Links(dve, linked)
            dve.wait_ge(iotas, 3)
            nc.vector.tensor_scalar(ge(0, 0), dist[:, :], -1.0, None, ALU.mult).then_inc(near_ready, 1)
            dve.wait_ge(near_ready, 1)
            nc.vector.tensor_tensor(dist[:, :], dist[:, :], ge(0, 0), ALU.max).then_inc(near_ready, 1)
            for h in range(16):
                dve.wait_ge(ge_ready, 2 * h + 2)
                if h >= 3:
                    dve.wait_ge(mask_written[h % 3], 16 * (h // 3))
                link(nc.vector.tensor_scalar(ge(h, 0), ge(h, 0), S.dwb[:, 1, 2 * h:2 * h + 1], None, ALU.mult))
                nc.vector.scalar_tensor_tensor(g[:, h % 3, :], ge(h, 1), S.dwb[:, 1, 2 * h + 1:2 * h + 2], ge(h, 0),
                                               ALU.mult, ALU.add).then_inc(g_ready, 1)

            def finish(n):
                dve.wait_ge(middle, n + 1)
                r = rows(n)
                if n >= 2:
                    dve.wait_ge(piece_written[2][n % 2], 16 * (n // 2))
                nc.vector.tensor_tensor(cut[0:r, n % 2, 2, :], rest[0:r, n % 2, :], cut[0:r, n % 2, 1, :], ALU.subtract).then_inc(low, 1)

            for n, (i, kind, v) in enumerate(jobs):
                if n >= 2:
                    dve.wait_ge(rested, n - 1)
                else:
                    dve.wait_ge(g_ready, 16)
                f = full[:, n % 2, :]
                ins = []
                if i == 2:
                    r = rows(n)
                    ins = [nc.vector.tensor_scalar(f[0:r], (S.KF if kind == "k" else S.QF)[0:r, :],
                                                   1.0 if kind == "k" else S.scale_f, None, ALU.mult)]
                elif kind == "k":
                    q0, q1 = QT * v, QT * v + QT
                    if v == 0:
                        dve.wait_ge(fw_ready, i + 1)
                        dve.wait_ge(rv_ready, i + 1)
                    if q0:
                        ins.append(nc.vector.tensor_tensor(f[:, 0:q0], S.K2[:, i, 0:q0], rv[:, i, T - 1 - q0:T - 1], ALU.mult))
                    ins.append(nc.vector.tensor_copy(f[:, q0:q1], S.K2[:, i, q0:q1]))
                    if q1 < T:
                        ins.append(nc.vector.tensor_tensor(f[:, q1:T], S.K2[:, i, q1:T], fw[:, i, 1:T - q1 + 1], ALU.mult))
                elif v == 1:
                    ins = [nc.vector.tensor_scalar(f, S.Q2[:, i, :], S.cols[:, 8:9], None, ALU.mult)]
                else:
                    part = fw[:, i, 0:QT] if v == 0 else rv[:, i, T - QT:T]
                    ins = [nc.vector.scalar_tensor_tensor(f.rearrange("p (a b) -> p a b", b=QT), S.Q2[:, i, :].rearrange("p (a b) -> p a b", b=QT),
                                                          S.cols[:, 6 + i:7 + i], part.unsqueeze(1).to_broadcast([P, NQ, QT]),
                                                          ALU.mult, ALU.mult)]
                ins[-1].then_inc(made, 1)
                if n >= 2:
                    finish(n - 2)
            finish(len(jobs) - 2)
            finish(len(jobs) - 1)

        @block.sync
        def _(sp):
            for h in range(16):
                sp.wait_ge(g_ready, h + 1)
                sp.dma_start(S.GD[h, :, :], g[:, h % 3, :]).then_inc(mask_written[h % 3], 16)

            def store(n, c):
                i, kind, v = jobs[n]
                sp.wait_ge((high, middle, low)[c], n + 1)
                if i == 2:
                    dst = (S.KDF if kind == "k" else S.QDF)[c, :, :]
                else:
                    dst = (S.KD if kind == "k" else S.QD)[v, c, P * i:P * i + P, :]
                sp.dma_start(dst, cut[0:rows(n), n % 2, c, :]).then_inc(piece_written[c][n % 2], 16)

            for n in range(len(jobs)):
                store(n, 0)
                if n >= 1:
                    store(n - 1, 1)
                    store(n - 1, 2)
            store(len(jobs) - 1, 1)
            store(len(jobs) - 1, 2)
            for m in range(3):
                sp.wait_ge(mask_written[m], 16 * len(range(m, 16, 3)))
            for m in range(2):
                for c in range(3):
                    sp.wait_ge(piece_written[c][m], 16 * len(jobs[m::2]))


class Attention:
    LEAD, LAG, PSLOTS, NEAR_LATE = 24, 5, 16, 4
    A_BANKS = (0, 1, 2) * 5 + (1,)
    B_BANKS = (3, 4, 5) * 5 + (4,)
    SUMS_AT, TURN_AT, NORM_AT = 5, 6, 8
    MAX_AT, ROWS_AT, SHIFT_AT, SPREAD_AT, SPREAD_KEEP_AT = 7, 11, 12, 14, 15

    def __init__(self, heads, dv, width, decayed):
        self.heads, self.dv, self.W, self.decayed = heads, dv, width, decayed
        self.rows = [96] if decayed else [96, 96]
        self.added = () if decayed else ((2, 4, 7, 9, 12, 14), (0, 1, 3, 5, 6, 8, 10, 11, 13, 15))
        self.near_steps = (0, 4, 7, 10) if decayed else ()
        self.groups = P // width
        self.pairs = heads // 2

    def key_blocks(self, i):
        if not self.decayed:
            return [(kb, False) for kb in range(NT)]
        near = list(range(4 * i, 4 * i + 4))
        far = [kb for kb in range(NT) if kb not in near]
        return [(near.pop(0), True) if s in self.near_steps else (far.pop(0), False) for s in range(NT)]

    def variant(self, i, t):
        return 0 if not self.decayed else (0 if t < i else 1 if t == i else 2)


def attention(nc, S, a):
    W, dv = a.W, a.dv
    NS, NV, NN = len(a.rows), (3 if a.decayed else 1), len(a.near_steps)
    NF = NT - NN
    TILES = 2 * NQ
    BODY = TILES * NT
    with ExitStack() as ctx:
        R = Room(nc, ctx, "t" if a.decayed else "u")
        K = [R.sb(f"K{i}", [P, NS, T], BF16) for i in range(NQ if a.decayed else 1)]
        Q = [R.sb(f"Q{i}", [P, NS, NV, QT], BF16) for i in range(NQ)]
        if a.decayed:
            G, V = R.sb("G", [P, 2, GW]), R.sb("V", [P, 2, NT, W])
            T1, T2 = R.sb("T1", [P, 2, QT]), R.sb("T2", [P, 2, QT])
            junk, mb = R.sb("junk", [P, 2, QT]), R.sb("mb", [P, 2, QT])
        else:
            total = R.sb("total", [P, 2, 2, QT])
        E = R.sb("E", [P, a.PSLOTS, QT])
        mx = R.sb("mx", [P, 2, 4, 4])
        nm, nm16, nm_parts = R.sb("nm", [P, 4]), R.sb("nm16", [P, 4], BF16), R.sb("nm_parts", [P, 2, 4, 2])
        O4 = R.sb("O4", [P, QT])
        rc = R.sb("rc", [P, 4])
        ps = R.psum()
        PV_BANK, MISC = 6, 7

        def since(banks, s):
            return next(d for d in range(1, NT + 1) if banks[(s - d) % NT] == banks[s % NT])
        set_up, started = R.sem("set_up"), R.sem("started")
        tile_loaded = [R.sem(f"tile_loaded{i}") for i in range(NQ)]
        keys_loaded = R.sem("keys_loaded")
        mask_loaded, v_copied = [R.sem(f"mask_loaded{i}") for i in range(2)], R.sem("v_copied")
        a_scored, a_reduced = R.sem("a_scored"), R.sem("a_reduced")
        max_cut, max_ready, row_ready, shift_ready = (R.sem(n) for n in ("max_cut", "max_ready", "row_ready", "shift_ready"))
        spread_ready, spread_kept = R.sem("spread_ready"), R.sem("spread_kept")
        b_scored, near_masked, near_shifted = R.sem("b_scored"), R.sem("near_masked"), R.sem("near_shifted")
        near_exp, far_exp, pv_done = R.sem("near_exp"), R.sem("far_exp"), R.sem("pv_done")
        o_kept, o_turned, o_inverse, o_normed = (R.sem(n) for n in ("o_kept", "o_turned", "o_inverse", "o_normed"))
        totalled, total_ready = [R.sem("dve_totalled"), R.sem("pool_totalled")], R.sem("total_ready")
        block = ctx.enter_context(nc.Block())
        per_load = 16 * (12 if a.decayed else 6)

        def counts(b):
            tile, s = divmod(b, NT)
            near = sum(x < s for x in a.near_steps)
            return tile * NN + near, tile * NF + s - near

        def wait(engine, sem, hp, per_pair, count):
            if not isinstance(hp, int) or hp * per_pair + count > 0:
                engine.wait_ge(sem, hp * per_pair + count)

        def wait_added(engine, hp, b):
            u, s = divmod(b, NT)
            for steps, sem in zip(a.added, totalled):
                if s in steps:
                    n = len(steps) - 1
                    wait(engine, sem, hp, TILES * n, u * n + max(1, steps.index(s)))

        def add_exp(engine, ops, which, hp, b):
            steps, sem = a.added[which], totalled[which]
            u, s = divmod(b, NT)
            if s not in steps[1:]:
                return
            k, n = steps.index(s), len(steps) - 1
            wait(engine, far_exp, hp, BODY, b + 1)
            wait(engine, sem, hp, TILES * n, u * n + k - 1)
            if k == 1:
                wait(engine, o_turned, hp, TILES, u - 1)
            acc = total[:, u % 2, which, :]
            first = E[:, (b - s + steps[0]) % a.PSLOTS, :] if k == 1 else acc
            ops.tensor_tensor(acc, first, E[:, b % a.PSLOTS, :], ALU.add).then_inc(sem, 1)

        def over_pairs(engine, emit):
            emit(0, False)
            if a.pairs > 2:
                with engine.Fori(1, a.pairs - 1) as hp:
                    emit(hp, False)
            emit(a.pairs - 1, True)

        def next_tile(hp, u):
            return (hp, u + 1) if u < TILES - 1 else (hp + 1, 0)

        def last_tile(hp, u):
            return (hp, u - 1) if u else (hp - 1, TILES - 1)

        def any_before(hp, u):
            return u > 0 or not isinstance(hp, int) or hp > 0

        @block.sync
        def _(sp):
            if not a.decayed:
                for r in range(6):
                    st, q = divmod(r, 3)
                    sp.dma_start(K[0][32 * q:32 * q + 32, st, :], S.KDF[SPLIT_K[r], :, :]).then_inc(keys_loaded, 16)

            def load(hp, u):
                i = u % NQ
                h = hp * 2 + u // NQ
                wait(sp, b_scored, hp, BODY, NT * (u - NQ + 1))
                for r in range(6):
                    if a.decayed:
                        sp.dma_start(K[i][16 * r:16 * r + 16, 0, :], S.KD[i, SPLIT_K[r], bass.ds(h * 16, 16), :]).then_inc(tile_loaded[i], 16)
                        sp.dma_start(Q[i][16 * r:16 * r + 16, 0, :, :],
                                     S.QD[:, SPLIT_Q[r], bass.ds(h * 16, 16), QT * i:QT * i + QT].rearrange("v r c -> r v c")).then_inc(tile_loaded[i], 16)
                    else:
                        st, q = divmod(r, 3)
                        sp.dma_start(Q[i][32 * q:32 * q + 32, st, 0, :], S.QDF[SPLIT_Q[r], bass.ds(h * 32, 32), QT * i:QT * i + QT]).then_inc(tile_loaded[i], 16)

            def mask(hp, par):
                if a.decayed:
                    wait(sp, near_masked, hp, TILES * NN, (par - 1) * NQ * NN)
                    sp.dma_start(G[:, par, :], S.GD[bass.ds(hp * 2 + par, 1), :, :].rearrange("a p c -> (a p) c")).then_inc(mask_loaded[par], 16)

            def emit(hp, last):
                if isinstance(hp, int) and hp == 0:
                    mask(0, 0)
                    for u in range(NQ):
                        load(0, u)
                mask(hp, 1)
                for u in range(NQ, TILES):
                    load(hp, u)
                if not last:
                    mask(hp + 1, 0)
                    for u in range(NQ):
                        load(hp + 1, u)
            over_pairs(sp, emit)

        @block.tensor
        def _(pe):
            def score_a(hp, n):
                u, j, t = n // NT, n // 4 % 4, n % 4
                i = u % NQ
                if n % NT == 0:
                    wait(pe, tile_loaded[i], hp, 2 * per_load, per_load * (u // NQ + 1))
                wait(pe, a_reduced, hp, BODY, n - since(a.A_BANKS, n) + 1)
                kk = K[i if a.decayed else 0]
                nc.tensor.matmul(ps[:, a.A_BANKS[n % NT], :], Q[i][0:96, 0, a.variant(i, t), P * j:P * j + P],
                                 kk[0:96, 0, QT * t:QT * t + QT], start=True, stop=True).then_inc(a_scored, 1)

            def rows_of_max(hp, u):
                wait(pe, max_ready, hp, 2 * TILES, 2 * u + 2)
                wait(pe, o_normed, hp, TILES, u - 1)
                for j in range(4):
                    ins = nc.tensor.matmul(ps[0:2, MISC, P * j:P * j + P], nm_parts[:, u % 2, j, :],
                                           S.ident[:, :], start=True, stop=True)
                ins.then_inc(row_ready, 1)

            def spread(hp, u):
                if a.decayed:
                    wait(pe, shift_ready, hp, TILES, u + 1)
                    nc.tensor.matmul(ps[:, MISC, :], S.spread[0:98, :], Q[u % NQ][0:98, 0, 0, :], start=True, stop=True).then_inc(spread_ready, 1)

            def score_b(hp, b):
                u, s = divmod(b, NT)
                i = u % NQ
                kb, _ = a.key_blocks(i)[s]
                ago = b - since(a.B_BANKS, b)
                was_near = ago % NT in a.near_steps
                cn, cf = counts(ago)
                if was_near:
                    wait(pe, near_masked, hp, TILES * NN, cn + 1)
                else:
                    wait(pe, far_exp, hp, TILES * NF, cf + 1)
                if s == 0:
                    wait(pe, shift_ready, hp, TILES, u + 1)
                kk = K[i if a.decayed else 0]
                for st in range(NS):
                    rows = 98 if st == NS - 1 else 96
                    ins = nc.tensor.matmul(ps[:, a.B_BANKS[b % NT], :], kk[0:rows, st, P * kb:P * kb + P],
                                           Q[i][0:rows, st, a.variant(i, kb // 4), :], start=st == 0, stop=st == NS - 1)
                ins.then_inc(b_scored, 1)

            def times_v(hp, b):
                u, s = divmod(b, NT)
                kb, near = a.key_blocks(u % NQ)[s]
                cn, cf = counts(b)
                if near:
                    wait(pe, near_exp, hp, TILES * NN, cn + 1)
                else:
                    wait(pe, far_exp, hp, TILES * NF, cf + 1)
                if s == 0:
                    wait(pe, o_kept, hp, TILES, u)
                    if a.decayed and u % NQ == 0:
                        wait(pe, v_copied, hp, 2, u // NQ + 1)
                g = s % a.groups
                v = V[:, u // NQ, kb, :] if a.decayed else S.Vcp[:, kb, 0:W]
                nc.tensor.matmul(ps[W * g:W * g + W, PV_BANK, :], v, E[:, b % a.PSLOTS, :],
                                 start=s < a.groups, stop=s >= NT - a.groups).then_inc(pv_done, 1)

            def turn(hp, u, last=False):
                wait(pe, o_kept, hp, TILES, u + 1)
                if last:
                    wait(pe, o_normed, hp, TILES, u)
                elif a.decayed:
                    wait(pe, spread_kept, hp, TILES, u + 2)
                for j in range(4):
                    ins = nc.tensor.matmul(ps[:, MISC, W * j:W * j + W], O4[:, P * j:P * j + P],
                                           S.selo[:, :], start=True, stop=True)
                if a.added:
                    wait(pe, total_ready, hp, TILES, u + 1)
                    for j in range(4):
                        ins = nc.tensor.matmul(ps[:, MISC, 4 * W + j:4 * W + j + 1], total[:, u % 2, 1, P * j:P * j + P],
                                               S.Vcp[:, 0, dv:dv + 1], start=True, stop=True)
                ins.then_inc(o_turned, 1)

            def emit(hp, last):
                if isinstance(hp, int) and hp == 0:
                    pe.wait_ge(set_up, 1)
                    if not a.decayed:
                        pe.wait_ge(keys_loaded, 16 * 6)
                    for n in range(NT):
                        score_a(0, n)
                    rows_of_max(0, 0)
                    for n in range(NT, a.LEAD):
                        score_a(0, n)
                    spread(0, 0)
                for b in range(BODY):
                    u, s = divmod(b, NT)
                    n = b + a.LEAD
                    if n < BODY:
                        score_a(hp, n)
                    elif not last:
                        score_a(hp + 1, n - BODY)
                    score_b(hp, b)
                    for done in range(b - a.LAG - 3, b - a.LAG + 1) if s % 4 == 0 else ():
                        if done >= 0:
                            times_v(hp, done)
                        elif any_before(hp, 0):
                            times_v(hp - 1, done + BODY)
                    if s == a.TURN_AT and any_before(hp, u):
                        turn(*last_tile(hp, u))
                    if not (last and u == TILES - 1):
                        if s == a.ROWS_AT:
                            rows_of_max(*next_tile(hp, u))
                        if s == a.SPREAD_AT:
                            spread(*next_tile(hp, u))
                if last:
                    for b in range(BODY - a.LAG - 3, BODY):
                        times_v(hp, b)
                    turn(hp, TILES - 1, True)
            over_pairs(pe, emit)

        @block.vector
        def _(dve):
            def reduce_a(hp, n):
                u, j, t = n // NT, n // 4 % 4, n % 4
                i = u % NQ
                if a.decayed and n % (NQ * NT) == 0:
                    wait(dve, mask_loaded[u // NQ], hp, 16, 16)
                wait(dve, a_scored, hp, BODY, n + 1)
                src, m = ps[:, a.A_BANKS[n % NT], :], mx[:, u % 2, j, t:t + 1]
                if a.decayed and t == i:
                    o = QT - P - P * j
                    wait(dve, a_reduced, hp, BODY, n - 4)
                    dve.nop(nofuse=True)
                    ins = nc.vector.tensor_tensor_reduce(junk[:, j % 2, :], src, G[:, u // NQ, o:o + QT], 1.0, LEAST, ALU.mult, ALU.max, m)
                else:
                    ins = nc.vector.tensor_reduce(m, src, AX.X, ALU.max)
                ins.then_inc(a_reduced, 1)

            def finish_max(hp, u):
                wait(dve, a_reduced, hp, BODY, NT * (u + 1))
                wait(dve, max_ready, hp, 2 * TILES, 2 * u)
                nc.vector.tensor_reduce(nm[:, :], mx[:, u % 2, :, :], AX.X, ALU.max, negate=True).then_inc(max_cut, 1)
                wait(dve, max_cut, hp, 2 * TILES, 2 * u + 1)
                nc.vector.tensor_copy(nm16[:, :], nm[:, :]).then_inc(max_cut, 1)
                wait(dve, max_cut, hp, 2 * TILES, 2 * u + 2)
                wait(dve, row_ready, hp, TILES, u - 1)
                nc.vector.tensor_copy(nm_parts[:, u % 2, :, 0:1], nm16[:, :].unsqueeze(2)).then_inc(max_ready, 1)
                nc.vector.tensor_tensor(nm_parts[:, u % 2, :, 1:2], nm[:, :].unsqueeze(2), nm16[:, :].unsqueeze(2), ALU.subtract).then_inc(max_ready, 1)

            def mask_b(hp, b):
                u, s = divmod(b, NT)
                kb, _ = a.key_blocks(u % NQ)[s]
                cn, _ = counts(b)
                wait(dve, b_scored, hp, BODY, b + 1)
                wait(dve, near_shifted, hp, TILES * NN, cn - 1)
                o = QT - P - P * (kb - 4 * (u % NQ))
                nc.vector.tensor_tensor(T1[:, cn % 2, :], ps[:, a.B_BANKS[b % NT], :], G[:, u // NQ, o:o + QT], ALU.mult).then_inc(near_masked, 1)

            def norm(hp, u):
                h = hp * 2 + u // NQ
                i = u % NQ
                wait(dve, o_turned, hp, TILES, u + 1)
                o = ps[:, MISC, 0:4 * W].rearrange("p (j w) -> p j w", w=W)
                sums = ps[:, MISC, 4 * W:4 * W + 4].unsqueeze(2) if a.added else o[:, :, dv:dv + 1]
                nc.vector.reciprocal(rc[:, :].unsqueeze(2), sums).then_inc(o_inverse, 1)
                wait(dve, o_inverse, hp, TILES, u + 1)
                dst = (S.AO if a.decayed else S.AOF)[:, 4 * i:4 * i + 4, bass.ds(h * dv, dv)]
                nc.vector.tensor_tensor(dst, o[:, :, 0:dv], rc[:, :].unsqueeze(2).to_broadcast([P, 4, dv]), ALU.mult).then_inc(o_normed, 1)

            def values_of(hp, par):
                if a.decayed:
                    wait(dve, pv_done, hp, BODY, (par - 1) * BODY // 2)
                    src = S.Vp[:, :, bass.ds(hp * 2 + par, 1), :].rearrange("p t a w -> p t (a w)")
                    nc.vector.tensor_copy(V[:, par, :, :], src).then_inc(v_copied, 1)

            def emit(hp, last):
                if isinstance(hp, int) and hp == 0:
                    for i in range(NQ):
                        nc.vector.memset(Q[i][96:98, NS - 1, :, :], 0.0).then_inc(started, 1)
                        if i < len(K):
                            nc.vector.memset(K[i][96:98, NS - 1, :], 1.0).then_inc(started, 1)
                    dve.wait_ge(started, NQ + len(K))
                    nc.vector.memset(rc[:, :], 0.0).then_inc(set_up, 1)
                    values_of(0, 0)
                    for n in range(NT):
                        reduce_a(0, n)
                    finish_max(0, 0)
                    for n in range(NT, a.LEAD):
                        reduce_a(0, n)
                for b in range(BODY):
                    u, s = divmod(b, NT)
                    n = b + a.LEAD
                    if n < BODY:
                        reduce_a(hp, n)
                    elif not last:
                        reduce_a(hp + 1, n - BODY)
                    if s in a.near_steps:
                        mask_b(hp, b)
                    if a.added and b >= 3:
                        add_exp(dve, nc.vector, 0, hp, b - 3)
                    elif a.added and any_before(hp, 0):
                        add_exp(dve, nc.vector, 0, hp - 1, b - 3 + BODY)
                    if s == a.NORM_AT and any_before(hp, u):
                        norm(*last_tile(hp, u))
                    if b == a.LAG + 4:
                        values_of(hp, 1)
                    if b == BODY // 2 + a.LAG + 4 and not last:
                        values_of(hp + 1, 0)
                    if s == a.MAX_AT and not (last and u == TILES - 1):
                        finish_max(*next_tile(hp, u))
                if last:
                    for b in range(BODY - 3, BODY) if a.added else ():
                        add_exp(dve, nc.vector, 0, hp, b)
                    norm(hp, TILES - 1)
            over_pairs(dve, emit)

        @block.gpsimd
        def _(pool):
            def emit(hp, last):
                for b in range(BODY):
                    u, s = divmod(b, NT)
                    if s in a.near_steps:
                        cn, _ = counts(b)
                        wait(pool, near_masked, hp, TILES * NN, cn + 1)
                        wait(pool, spread_kept, hp, TILES, u + 1)
                        wait(pool, near_exp, hp, TILES * NN, cn - 1)
                        nc.gpsimd.tensor_tensor(T2[:, cn % 2, :], T1[:, cn % 2, :], mb[:, u % 2, :], ALU.add).then_inc(near_shifted, 1)
            def join_totals(hp, u):
                for steps, sem in zip(a.added, totalled):
                    wait(pool, sem, hp, TILES * (len(steps) - 1), (u + 1) * (len(steps) - 1))
                nc.gpsimd.tensor_tensor(total[:, u % 2, 1, :], total[:, u % 2, 1, :], total[:, u % 2, 0, :], ALU.add).then_inc(total_ready, 1)

            def emit_totals(hp, last):
                for b in range(BODY):
                    u, s = divmod(b, NT)
                    add_exp(pool, nc.gpsimd, 1, hp, b)
                    if s == 2 and any_before(hp, u):
                        join_totals(*last_tile(hp, u))
                if last:
                    join_totals(hp, TILES - 1)
            over_pairs(pool, emit if a.decayed else emit_totals)

        @block.scalar
        def _(act):
            def slot(hp, b):
                wait(act, pv_done, hp, BODY, b - a.PSLOTS + 1)
                wait_added(act, hp, b - a.PSLOTS)
                return E[:, b % a.PSLOTS, :]

            def shift(hp, u):
                wait(act, row_ready, hp, TILES, u + 1)
                for v in ((0, 2) if a.decayed else (0,)):
                    ins = nc.scalar.activation(Q[u % NQ][96:98, NS - 1, v, :], ps[0:2, MISC, :], ACT.Copy)
                ins.then_inc(shift_ready, 1)

            def keep_spread(hp, u):
                if a.decayed:
                    wait(act, spread_ready, hp, TILES, u + 1)
                    wait(act, near_shifted, hp, TILES * NN, NN * (u - 1))
                    nc.scalar.activation(mb[:, u % 2, :], ps[:, MISC, :], ACT.Copy).then_inc(spread_kept, 1)

            def keep_sums(hp, u):
                wait(act, pv_done, hp, BODY, NT * (u + 1))
                wait(act, o_turned, hp, TILES, u)
                nc.scalar.activation(O4[:, :], ps[:, PV_BANK, :], ACT.Copy).then_inc(o_kept, 1)

            def emit(hp, last):
                if isinstance(hp, int) and hp == 0:
                    shift(0, 0)
                    keep_spread(0, 0)
                for b in range(BODY):
                    u, s = divmod(b, NT)
                    if s == a.SUMS_AT and any_before(hp, u):
                        keep_sums(*last_tile(hp, u))
                    if s not in a.near_steps:
                        out = slot(hp, b)
                        wait(act, b_scored, hp, BODY, b + 1)
                        nc.scalar.activation(out, ps[:, a.B_BANKS[b % NT], :], ACT.Exp).then_inc(far_exp, 1)
                    if s - a.NEAR_LATE in a.near_steps:
                        bn = b - a.NEAR_LATE
                        cn, _ = counts(bn)
                        out = slot(hp, bn)
                        wait(act, near_shifted, hp, TILES * NN, cn + 1)
                        nc.scalar.activation(out, T2[:, cn % 2, :], ACT.Exp).then_inc(near_exp, 1)
                    if not (last and u == TILES - 1):
                        if s == a.SHIFT_AT:
                            shift(*next_tile(hp, u))
                        if s == a.SPREAD_KEEP_AT:
                            keep_spread(*next_tile(hp, u))
                if last:
                    keep_sums(hp, TILES - 1)
            over_pairs(act, emit)


def transposed(nc, pe, ps, bank, src, tiles, ident):
    for j, t in enumerate(tiles):
        ins = nc.tensor.transpose(ps[:, bank, j * P:(j + 1) * P], src[:, t, :], ident[:, :])
    return ins


def choose_two(nc, link, prob, rev, first, second, key, val, E):
    wide = [P, NT, E]
    for n, hot in ((0, first), (1, second)):
        link(nc.vector.tensor_reduce(val[:, n, :], prob[:, :, :], AX.X, ALU.max))
        link(nc.vector.tensor_tensor(key[:, :, :], prob[:, :, :], val[:, n, :].unsqueeze(2).to_broadcast(wide), ALU.is_equal))
        link(nc.vector.tensor_tensor(key[:, :, :], key[:, :, :], rev[:, 0:E].unsqueeze(1).to_broadcast(wide), ALU.mult))
        link(nc.vector.tensor_reduce(val[:, 2, :], key[:, :, :], AX.X, ALU.max))
        link(nc.vector.tensor_tensor(hot[:, :, :], key[:, :, :], val[:, 2, :].unsqueeze(2).to_broadcast(wide), ALU.is_equal))
        if n == 0:
            link(nc.vector.scalar_tensor_tensor(prob[:, :, :].rearrange("p t e -> p (t e)"), hot[:, :, :].rearrange("p t e -> p (t e)"), -2.0,
                                                prob[:, :, :].rearrange("p t e -> p (t e)"), ALU.mult, ALU.add))


def mixture0(nc, S, dram):
    E, NE = 8, 9
    with ExitStack() as ctx:
        R = Room(nc, ctx, "m")
        AT = R.sb("AT", [P, T])
        AFT = R.sb("AFT", [P, T])
        y = R.sb("y", [P, NT, D])
        s0 = R.sb("s0", [P, NT, D])
        nx, tmp, st = R.sb("nx", [P, NT, D]), R.sb("tmp", [P, NT, D]), R.sb("st", [P, 4, NT])
        x = R.sb("x", [P, NT, D])
        WoT, fWoT, WrT = R.sb("WoT", [P, D]), R.sb("fWoT", [P, D]), R.sb("WrT", [P, E])
        W1, W3, W2 = (R.sb(n, [P, NE, D]) for n in ("W1", "W3", "W2"))
        rev = R.sb("rev", [P, E])
        prob, key, hot1, hot2 = (R.sb(n, [P, NT, E]) for n in ("prob", "key", "hot1", "hot2"))
        val = R.sb("val", [P, 8, NT])
        share = R.sb("share", [P, NT, NE])
        gate, h = R.sb("gate", [P, 2, QT]), R.sb("h", [P, 2, QT])
        ps = R.psum()
        wo_loaded = R.sem("wo_loaded")
        loaded, x_loaded, linked, rev_ready = R.sem("loaded"), R.sem("x_loaded"), R.sem("linked"), R.sem("rev_ready")
        turned, turned_kept, projected, added = R.sem("turned"), R.sem("turned_kept"), R.sem("projected"), R.sem("added")
        squares, roots, nx_ready = R.sem("squares"), R.sem("roots"), R.sem("nx_ready")
        nx_turned, nx_kept, routed = R.sem("nx_turned"), R.sem("nx_kept"), R.sem("routed")
        shifted, expd = R.sem("shifted"), R.sem("expd")
        up_done, gated, h_ready, down_done, summed = (R.sem(n) for n in ("up_done", "gated", "h_ready", "down_done", "summed"))
        y_ready, silu_ready = R.sem("y_ready"), R.sem("silu_ready")
        block = ctx.enter_context(nc.Block())
        wide = [P, NT, E]
        STEPS = NE * NQ

        @block.sync
        def _(sp):
            sp.dma_start(WoT[:, :], dram["WoT"]).then_inc(wo_loaded, 16)
            sp.dma_start(fWoT[:, :], dram["fWoT"]).then_inc(wo_loaded, 16)
            sp.dma_start(WrT[:, :], dram["WrT"]).then_inc(loaded, 16)
            for w, n in ((W1, "eW1"), (W3, "eW3"), (W2, "eW2")):
                for e in range(NE):
                    sp.dma_start(w[:, e, :], dram[n][e, :, :]).then_inc(loaded, 16)
            for t in range(NT):
                sp.dma_start(x[:, t, :], dram["x"][t * P:(t + 1) * P, :]).then_inc(x_loaded, 16)

        @block.gpsimd
        def _(pool):
            nc.gpsimd.iota(rev[:, :], [[-1, E]], base=E, channel_multiplier=0, allow_small_or_imprecise_dtypes=True).then_inc(rev_ready, 1)

        @block.scalar
        def _(act):
            for n in range(8):
                act.wait_ge(turned, n + 1)
                dst = (AT, AFT)[n // 4]
                nc.scalar.activation(dst[:, (n % 4) * QT:(n % 4 + 1) * QT], ps[:, n % 4, :], ACT.Copy).then_inc(turned_kept, 1)
            act.wait_ge(squares, 1)
            nc.scalar.activation(st[:, 2, :], st[:, 1, :], ACT.Sqrt).then_inc(roots, 1)
            for n in range(4):
                act.wait_ge(nx_turned, n + 1)
                nc.scalar.activation(AT[:, n * QT:(n + 1) * QT], ps[:, n % 4, :], ACT.Copy, scale=S.g[:, 1:2]).then_inc(nx_kept, 1)
            act.wait_ge(shifted, 1)
            nc.scalar.activation(prob[:, :, :], prob[:, :, :], ACT.Exp).then_inc(expd, 1)
            act.wait_ge(shifted, 2)
            nc.scalar.activation(val[:, 3, :], val[:, 3, :], ACT.Exp).then_inc(expd, 1)
            for n in range(STEPS):
                act.wait_ge(up_done, n + 1)
                if n >= 2:
                    act.wait_ge(h_ready, n - 1)
                nc.scalar.activation(gate[:, n % 2, :], ps[:, 2 * (n % 2), :], ACT.Silu).then_inc(gated, 1)
            act.wait_ge(y_ready, 1)
            nc.scalar.activation(y[:, :, :], y[:, :, :], ACT.Silu).then_inc(silu_ready, 1)

        @block.tensor
        def _(pe):
            for n in range(8):
                if n >= 4:
                    pe.wait_ge(turned_kept, n - 3)
                transposed(nc, pe, ps, n % 4, (S.AO, S.AOF)[n // 4], range(4 * (n % 4), 4 * (n % 4) + 4), S.ident).then_inc(turned, 1)
            pe.wait_ge(wo_loaded, 16 * 2)
            for n in range(8):
                a, w = ((AT, WoT), (AFT, fWoT))[n // 4]
                pe.wait_ge(turned_kept, n + 1)
                if n >= 4:
                    pe.wait_ge(added, n - 3)
                for j in range(4):
                    t = 4 * (n % 4) + j
                    ins = nc.tensor.matmul(ps[:, 4 + n % 4, j * P:(j + 1) * P], a[:, t * P:(t + 1) * P], w[:, :], start=True, stop=True)
                ins.then_inc(projected, 1)
            pe.wait_ge(nx_ready, 1)
            pe.wait_ge(turned_kept, 8)
            for n in range(4):
                transposed(nc, pe, ps, n, nx, range(4 * n, 4 * n + 4), S.ident).then_inc(nx_turned, 1)
            pe.wait_ge(loaded, 16 * (1 + 3 * NE))
            pe.wait_ge(nx_kept, 4)
            pe.wait_ge(added, 8)
            for t in range(NT):
                ins = nc.tensor.matmul(ps[:, 4, t * E:(t + 1) * E], AT[:, t * P:(t + 1) * P], WrT[:, :], start=True, stop=True)
            ins.then_inc(routed, 1)

            def up(n):
                e, c = divmod(n, NQ)
                if n >= 2:
                    pe.wait_ge(h_ready, n - 1)
                for k, w in ((0, W1), (1, W3)):
                    ins = nc.tensor.matmul(ps[:, 2 * (n % 2) + k, :], w[:, e, :], AT[:, c * QT:(c + 1) * QT], start=True, stop=True)
                ins.then_inc(up_done, 1)

            def down(n):
                e, c = divmod(n, NQ)
                pe.wait_ge(h_ready, n + 1)
                if n >= 2:
                    pe.wait_ge(summed, n - 1)
                for j in range(4):
                    ins = nc.tensor.matmul(ps[:, 5 + n % 2, j * P:(j + 1) * P], h[:, n % 2, j * P:(j + 1) * P], W2[:, e, :], start=True, stop=True)
                ins.then_inc(down_done, 1)
            for n in range(STEPS):
                up(n)
                if n:
                    down(n - 1)
            down(STEPS - 1)

        @block.vector
        def _(dve):
            link = Links(dve, linked)
            for n in range(8):
                dve.wait_ge(projected, n + 1)
                src = ps[:, 4 + n % 4, :].rearrange("p (j d) -> p j d", d=D)
                c = n % 4
                if n < 4:
                    nc.vector.tensor_tensor(s0[:, 4 * c:4 * c + 4, :], src, S.bo[:, :].unsqueeze(1).to_broadcast([P, 4, D]), ALU.add).then_inc(added, 1)
                else:
                    nc.vector.tensor_tensor(y[:, 4 * c:4 * c + 4, :], src, S.xn[:, 4 * c:4 * c + 4, :], ALU.add).then_inc(added, 1)
            dve.wait_ge(added, 8)
            normalise(nc, dve, link, y, nx, tmp, st, False, 1e-6, squares, roots, 0).then_inc(nx_ready, 1)
            dve.wait_ge(rev_ready, 1)
            dve.wait_ge(routed, 1)
            link(nc.vector.tensor_tensor(prob[:, :, :], ps[:, 4, 0:NT * E].rearrange("p (t e) -> p t e", e=E),
                                         S.rbias[:, :].unsqueeze(1).to_broadcast(wide), ALU.add))
            link(nc.vector.tensor_reduce(val[:, 4, :], prob[:, :, :], AX.X, ALU.max))
            nc.vector.tensor_tensor(prob[:, :, :], prob[:, :, :], val[:, 4, :].unsqueeze(2).to_broadcast(wide), ALU.subtract).then_inc(shifted, 1)
            dve.wait_ge(expd, 1)
            link(nc.vector.tensor_reduce(val[:, 4, :], prob[:, :, :], AX.X, ALU.add))
            link(nc.vector.reciprocal(val[:, 5, :], val[:, 4, :]))
            link(nc.vector.tensor_tensor(prob[:, :, :], prob[:, :, :], val[:, 5, :].unsqueeze(2).to_broadcast(wide), ALU.mult))
            choose_two(nc, link, prob, rev, hot1, hot2, key, val, E)
            nc.vector.tensor_tensor(val[:, 3, :], val[:, 1, :], val[:, 0, :], ALU.subtract).then_inc(shifted, 1)
            dve.wait_ge(expd, 2)
            link(nc.vector.tensor_scalar(val[:, 4, :], val[:, 3, :], 1.0, None, ALU.add))
            link(nc.vector.reciprocal(val[:, 5, :], val[:, 4, :]))
            link(nc.vector.tensor_tensor(val[:, 6, :], val[:, 5, :], val[:, 3, :], ALU.mult))
            link(nc.vector.tensor_tensor(hot1[:, :, :], hot1[:, :, :], val[:, 5, :].unsqueeze(2).to_broadcast(wide), ALU.mult))
            link(nc.vector.tensor_tensor(hot2[:, :, :], hot2[:, :, :], val[:, 6, :].unsqueeze(2).to_broadcast(wide), ALU.mult))
            link(nc.vector.tensor_tensor(share[:, :, 0:E], hot1[:, :, :], hot2[:, :, :], ALU.add))
            link(nc.vector.memset(share[:, :, E:NE], 1.0))

            def hidden(n):
                dve.wait_ge(gated, n + 1)
                if n >= 2:
                    dve.wait_ge(down_done, n - 1)
                nc.vector.tensor_tensor(h[:, n % 2, :], gate[:, n % 2, :], ps[:, 2 * (n % 2) + 1, :], ALU.mult).then_inc(h_ready, 1)

            def add_up(n):
                e, c = divmod(n, NQ)
                dve.wait_ge(down_done, n + 1)
                if n >= NQ:
                    dve.wait_ge(summed, n - NQ + 1)
                for j in range(4):
                    t = 4 * c + j
                    ins = nc.vector.scalar_tensor_tensor(y[:, t, :], ps[:, 5 + n % 2, j * P:(j + 1) * P], share[:, t, e:e + 1], y[:, t, :],
                                                         ALU.mult, ALU.add)
                ins.then_inc(summed, 1)
            for n in range(STEPS):
                hidden(n)
                if n:
                    add_up(n - 1)
            add_up(STEPS - 1)
            dve.wait_ge(summed, STEPS)
            nc.vector.tensor_copy(val[:, 7, :], val[:, 6, :]).then_inc(y_ready, 1)
            dve.wait_ge(silu_ready, 1)
            dve.wait_ge(x_loaded, 16 * NT)
            link(nc.vector.tensor_tensor(y[:, :, :], y[:, :, :], s0[:, :, :], ALU.mult))
            link(nc.vector.tensor_tensor(S.x1[:, :, :], y[:, :, :], x[:, :, :], ALU.add))


H1, N1 = 8, 32
HN = H1 * N1
E1, I1 = 64, 64
PAIRS = E1 // 2 + 1
CAPACITY = 128


def prepare1(nc, S, dram):
    with ExitStack() as ctx:
        R = Room(nc, ctx, "r")
        nT = R.sb("nT", [P, T])
        xpT = R.sb("xpT", [P, T])
        tmp, st = R.sb("tmp", [P, NT, D]), R.sb("st", [P, 4, NT])
        WinT, WkT, WqT, WvT, WbT = R.sb("WinT", [P, D]), R.sb("WkT", [P, HN]), R.sb("WqT", [P, HN]), R.sb("WvT", [P, HN]), R.sb("WbT", [P, HN])
        nbb = R.sb("nbb", [P, 2])
        bb, gT = R.sb("bb", [P, 2]), R.sb("gT", [P, E1])
        kq = R.sb("kq", [P, 2, 2, HN])
        kraw = R.sb("kraw", [P, NT, HN])
        kn = R.sb("kn", [P, NT, H1, N1 + 1])
        nrm = R.sb("nrm", [P, 3, NT * H1])
        rev = R.sb("rev", [P, E1])
        prob, key, hot1, hot2 = (R.sb(n, [P, NT, E1]) for n in ("prob", "key", "hot1", "hot2"))
        val = R.sb("val", [P, 6, NT])
        before = R.sb("before", [P, P])
        ones = R.sb("ones", [P, P])
        shareT = R.sb("shareT", [E1, T])
        rows = R.sb("rows", [2, T])
        ps = R.psum()
        loaded, linked = R.sem("loaded"), R.sem("linked")
        squares, roots, n_ready, m_ready = R.sem("squares"), R.sem("roots"), R.sem("n_ready"), R.sem("m_ready")
        turned, turned_kept, xp_done, xp_kept = R.sem("turned"), R.sem("turned_kept"), R.sem("xp_done"), R.sem("xp_kept")
        vb_done, vb_kept, k_done, q_done, q_kept, q_out = (R.sem(n) for n in ("vb_done", "vb_kept", "k_done", "q_done", "q_kept", "q_out0"))
        nbb_ready, squared, ones_column = R.sem("nbb_ready"), R.sem("squared"), R.sem("ones_column")
        q_out = [q_out, R.sem("q_out1")]
        k_kept, norms, norm_roots, kn_ready, kn_out = (R.sem(n) for n in ("k_kept", "norms", "norm_roots", "kn_ready", "kn_out"))
        pool_made, m_turned, m_kept, routed, shifted, expd = (R.sem(n) for n in ("pool_made", "m_turned", "m_kept", "routed", "shifted", "expd"))
        chosen, placed, shares_ready, share_turned, share_kept, out_done = (
            R.sem(n) for n in ("chosen", "placed", "shares_ready", "share_turned", "share_kept", "out_done"))
        block = ctx.enter_context(nc.Block())
        wide = [P, NT, E1]
        nm = tmp

        @block.sync
        def _(sp):
            for dst, n in ((WinT, "WinT"), (WkT, "rWkT"), (WqT, "rWqT"), (WvT, "rWvT"), (WbT, "rWbT"), (bb, "bbeta"), (gT, "gateT")):
                sp.dma_start(dst[:, :], dram[n]).then_inc(loaded, 16)
            for t in range(NT):
                sp.wait_ge(kn_ready, t + 1)
                sp.dma_start(S.KN[:, t * P:(t + 1) * P, :].rearrange("h p c -> p h c"), kn[:, t, :, :]).then_inc(kn_out, 16)
            for t in range(NT // 2):
                sp.wait_ge(q_kept, t + 1)
                for j in range(2):
                    tok = (2 * t + j) * P
                    sp.dma_start(S.QN[:, tok:tok + P, :].rearrange("h p c -> p h c"),
                                 kq[:, t % 2, j, :].rearrange("p (h c) -> p h c", c=N1)).then_inc(q_out[t % 2], 16)
            sp.wait_ge(share_kept, 4)
            sp.dma_start(S.ST[0:E1, :], shareT[:, :]).then_inc(out_done, 16)
            sp.dma_start(S.ST[E1:E1 + 2, :], rows[:, :]).then_inc(out_done, 16)
            for m in range(2):
                sp.wait_ge(q_out[m], 8 * NT)
            sp.wait_ge(kn_out, 16 * NT)
            sp.wait_ge(out_done, 32)

        @block.gpsimd
        def _(pool):
            nc.gpsimd.iota(rev[:, :], [[-1, E1]], base=E1, channel_multiplier=0, allow_small_or_imprecise_dtypes=True).then_inc(pool_made, 1)
            nc.gpsimd.memset(ones[:, :], 1.0).then_inc(pool_made, 1)
            nc.gpsimd.memset(rows[:, :], 0.5).then_inc(pool_made, 1)
            pool.wait_ge(pool_made, 3)
            nc.gpsimd.affine_select(out=before[:, :], in_=ones[:, :], compare_op=ALU.is_gt, fill=0.0,
                                    base=0, pattern=[[1, P]], channel_multiplier=-1).then_inc(pool_made, 1)
            nc.gpsimd.affine_select(out=rows[:, :], in_=rows[:, :], compare_op=ALU.is_gt, fill=0.0,
                                    base=1, pattern=[[0, T]], channel_multiplier=-1).then_inc(pool_made, 1)
            pool.wait_ge(pool_made, 5)
            pool.wait_ge(ones_column, 1)
            for n in range(8):
                k = kraw[:, 2 * n:2 * n + 2, :].rearrange("p t (h c) -> p t h c", c=N1)
                pool.wait_ge(k_kept, n + 1)
                nc.gpsimd.tensor_tensor(kn[:, 2 * n:2 * n + 2, :, 0:N1], k, k, ALU.mult).then_inc(squared, 1)

        @block.scalar
        def _(act):
            for n in range(2):
                act.wait_ge(squares, n + 1)
                nc.scalar.activation(st[:, 2, :], st[:, 1, :], ACT.Sqrt).then_inc(roots, 1)
            for n in range(4):
                act.wait_ge(turned, n + 1)
                nc.scalar.activation(nT[:, n * QT:(n + 1) * QT], ps[:, n, :], ACT.Copy).then_inc(turned_kept, 1)
            for n in range(4):
                act.wait_ge(m_turned, n + 1)
                nc.scalar.activation(S.mT[:, n * QT:(n + 1) * QT], ps[:, n, :], ACT.Copy, scale=S.g[:, 2:3]).then_inc(m_kept, 1)
            for n in range(4):
                act.wait_ge(xp_done, n + 1)
                nc.scalar.activation(xpT[:, n * QT:(n + 1) * QT], ps[:, n, :], ACT.Silu).then_inc(xp_kept, 1)
            for n in range(8):
                act.wait_ge(k_done, n + 1)
                nc.scalar.activation(kraw[:, 2 * n:2 * n + 2, :], ps[:, 4 + n % 2, :].rearrange("p (j c) -> p j c", j=2), ACT.Copy).then_inc(k_kept, 1)
            for n in range(24):
                g, c = n // 4 % 2, n % 4
                if n == 8:
                    act.wait_ge(norms, 1)
                    nc.scalar.activation(nrm[:, 1, :], nrm[:, 0, :], ACT.Sqrt).then_inc(norm_roots, 1)
                    act.wait_ge(shifted, 1)
                    nc.scalar.activation(prob[:, :, :], prob[:, :, :], ACT.Exp).then_inc(expd, 1)
                    act.wait_ge(nbb_ready, 1)
                act.wait_ge(vb_done, n + 1)
                if n < 8:
                    nc.scalar.activation(S.vT[:, g, c * QT:(c + 1) * QT], ps[:, n % 4, :], ACT.Copy).then_inc(vb_kept, 1)
                elif n < 16:
                    nc.scalar.activation(S.rb[:, g, c * QT:(c + 1) * QT], ps[:, n % 4, :], ACT.Exp, bias=nbb[:, g:g + 1], scale=-1.0).then_inc(vb_kept, 1)
                else:
                    nc.scalar.activation(S.beta[:, g, c * QT:(c + 1) * QT], ps[:, n % 4, :], ACT.Sigmoid, bias=bb[:, g:g + 1]).then_inc(vb_kept, 1)
            for n in range(8):
                act.wait_ge(q_done, n + 1)
                if n >= 2:
                    act.wait_ge(q_out[n % 2], 32 * (n // 2))
                nc.scalar.activation(kq[:, n % 2, :, :], ps[:, 4 + n % 2, :].rearrange("p (j c) -> p j c", j=2), ACT.Copy).then_inc(q_kept, 1)
            for n in range(4):
                act.wait_ge(share_turned, n + 1)
                nc.scalar.activation(shareT[:, n * QT:(n + 1) * QT], ps[0:E1, n, :], ACT.Copy).then_inc(share_kept, 1)

        @block.tensor
        def _(pe):
            pe.wait_ge(n_ready, 1)
            for n in range(4):
                transposed(nc, pe, ps, n, S.xn, range(4 * n, 4 * n + 4), S.ident).then_inc(turned, 1)
            pe.wait_ge(m_ready, 1)
            for n in range(4):
                pe.wait_ge(turned_kept, n + 1)
                transposed(nc, pe, ps, n, nm, range(4 * n, 4 * n + 4), S.ident).then_inc(m_turned, 1)
            pe.wait_ge(loaded, 16 * 7)
            for n in range(4):
                pe.wait_ge(m_kept, n + 1)
                nc.tensor.matmul(ps[:, n, :], WinT[:, :], nT[:, n * QT:(n + 1) * QT], start=True, stop=True).then_inc(xp_done, 1)
            for t in range(NT):
                ins = nc.tensor.matmul(ps[:, 6 + t // 8, (t % 8) * E1:(t % 8 + 1) * E1], S.mT[:, t * P:(t + 1) * P], gT[:, :], start=True, stop=True)
            ins.then_inc(routed, 1)
            def keys_or_queries(w, done, kept):
                for n in range(8):
                    if n >= 2:
                        pe.wait_ge(kept, n - 1)
                    for j in range(2):
                        t = 2 * n + j
                        ins = nc.tensor.matmul(ps[:, 4 + n % 2, j * HN:(j + 1) * HN], xpT[:, t * P:(t + 1) * P], w[:, :], start=True, stop=True)
                    ins.then_inc(done, 1)

            pe.wait_ge(xp_kept, 4)
            keys_or_queries(WkT, k_done, k_kept)
            pe.wait_ge(k_kept, 8)
            for n in range(24):
                if n >= 4:
                    pe.wait_ge(vb_kept, n - 3)
                g, c = n // 4 % 2, n % 4
                w = WvT if n < 8 else WbT
                nc.tensor.matmul(ps[:, n % 4, :], w[:, g * P:(g + 1) * P], xpT[:, c * QT:(c + 1) * QT], start=True, stop=True).then_inc(vb_done, 1)
            keys_or_queries(WqT, q_done, q_kept)
            pe.wait_ge(pool_made, 5)
            pe.wait_ge(chosen, 1)
            for n in range(2):
                nc.tensor.matmul(ps[:, 6 + n, :], before[:, :], hot2[:, 8 * n:8 * n + 8, :], start=True, stop=False)
                ins = nc.tensor.matmul(ps[:, 6 + n, :], ones[:, :], key[:, 8 * n:8 * n + 8, :], start=False, stop=True)
            ins.then_inc(placed, 1)
            pe.wait_ge(shares_ready, 1)
            pe.wait_ge(vb_kept, 24)
            for n in range(4):
                for j in range(4):
                    ins = nc.tensor.transpose(ps[0:E1, n, j * P:(j + 1) * P], prob[:, 4 * n + j, :], S.ident[:, :])
                ins.then_inc(share_turned, 1)

        @block.vector
        def _(dve):
            link = Links(dve, linked)
            nc.vector.memset(kn[:, :, :, N1:N1 + 1], -1.0).then_inc(ones_column, 1)
            link(nc.vector.memset(S.vT[:, :, T:T + 1], 0.0))
            normalise(nc, dve, link, S.x1, S.xn, tmp, st, True, 1e-5, squares, roots, 0).then_inc(n_ready, 1)
            dve.wait_ge(n_ready, 1)
            normalise(nc, dve, link, S.xn, nm, tmp, st, False, 1e-6, squares, roots, 1).then_inc(m_ready, 1)
            dve.wait_ge(pool_made, 5)
            dve.wait_ge(routed, 1)
            for n in range(2):
                link(nc.vector.tensor_copy(prob[:, 8 * n:8 * n + 8, :], ps[:, 6 + n, :].rearrange("p (t e) -> p t e", e=E1)))
            link(nc.vector.tensor_reduce(val[:, 4, :], prob[:, :, :], AX.X, ALU.max))
            nc.vector.tensor_tensor(prob[:, :, :], prob[:, :, :], val[:, 4, :].unsqueeze(2).to_broadcast(wide), ALU.subtract).then_inc(shifted, 1)
            dve.wait_ge(loaded, 16 * 7)
            nc.vector.tensor_scalar(nbb[:, :], bb[:, :], -1.0, None, ALU.mult).then_inc(nbb_ready, 1)
            dve.wait_ge(squared, 8)
            link(nc.vector.tensor_reduce(nrm[:, 0, :].rearrange("p (t h) -> p t h", h=H1), kn[:, :, :, 0:N1], AX.X, ALU.add))
            nc.vector.tensor_copy(nrm[:, 2, :], nrm[:, 0, :]).then_inc(norms, 1)
            dve.wait_ge(norm_roots, 1)
            link(nc.vector.tensor_scalar(nrm[:, 1, :], nrm[:, 1, :], 1e-6, None, ALU.add))
            link(nc.vector.reciprocal(nrm[:, 2, :], nrm[:, 1, :]))
            for t in range(NT):
                nc.vector.tensor_tensor(kn[:, t, :, 0:N1], kraw[:, t, :].rearrange("p (h c) -> p h c", c=N1),
                                        nrm[:, 2, H1 * t:H1 * t + H1].unsqueeze(2).to_broadcast([P, H1, N1]), ALU.mult).then_inc(kn_ready, 1)
            dve.wait_ge(expd, 1)
            choose_two(nc, link, prob, rev, hot1, hot2, key, val, E1)
            link(nc.vector.tensor_tensor(val[:, 3, :], val[:, 0, :], val[:, 1, :], ALU.add))
            link(nc.vector.reciprocal(val[:, 4, :], val[:, 3, :]))
            link(nc.vector.tensor_scalar(val[:, 4, :], val[:, 4, :], 0.5, None, ALU.mult))
            link(nc.vector.tensor_tensor(val[:, 0, :], val[:, 0, :], val[:, 4, :], ALU.mult))
            link(nc.vector.tensor_tensor(val[:, 1, :], val[:, 1, :], val[:, 4, :], ALU.mult))
            link(nc.vector.tensor_tensor(prob[:, :, :], hot1[:, :, :], val[:, 0, :].unsqueeze(2).to_broadcast(wide), ALU.mult))
            link(nc.vector.tensor_tensor(key[:, :, :], hot2[:, :, :], val[:, 1, :].unsqueeze(2).to_broadcast(wide), ALU.mult))
            link(nc.vector.tensor_tensor(prob[:, :, :], prob[:, :, :], key[:, :, :], ALU.add))
            link(nc.vector.tensor_tensor(hot2[:, :, :], hot1[:, :, :], hot2[:, :, :], ALU.add))
            link(nc.vector.memset(key[:, 0, :], 0.0))
            for t in range(1, NT):
                link(nc.vector.tensor_tensor(key[:, t, :], key[:, t - 1, :], hot2[:, t - 1, :], ALU.add))
            nc.vector.tensor_copy(val[:, 5, :], val[:, 4, :]).then_inc(chosen, 1)
            dve.wait_ge(vb_kept, 24)
            link(nc.vector.tensor_scalar(S.rb[:, :, :], S.rb[:, :, :], 1.0, 1e30, ALU.add, ALU.min))
            link(nc.vector.tensor_scalar(S.beta[:, :, :], S.beta[:, :, :], 1e-30, -1.0, ALU.max, ALU.mult))
            dve.wait_ge(placed, 1)
            for n in range(2):
                src = ps[:, 6 + n, :].rearrange("p (t e) -> p t e", e=E1)
                ins = nc.vector.scalar_tensor_tensor(prob[:, 8 * n:8 * n + 8, :].rearrange("p t e -> p (t e)"), ps[:, 6 + n, :], float(CAPACITY),
                                                     prob[:, 8 * n:8 * n + 8, :].rearrange("p t e -> p (t e)"), ALU.is_lt, ALU.mult)
            ins.then_inc(shares_ready, 1)


def recurrence(nc, S, dram):
    C = 32
    TURN = 2 * C
    TURNS = T // TURN
    TAKE_AT = (0, 9, C, C + 9)
    TAKES = 8
    GATE_AT = (3, 12, C + 3, C + 12)
    GATES = 8
    SUM_AT = 16
    X_BANK, DOWN_BANK = 2, 4
    with ExitStack() as ctx:
        R = Room(nc, ctx, "w")
        SQ = S.SQ
        K, Qb = R.sb("K", [P, 2, 2, C, N1 + 1]), R.sb("Qb", [P, 2, 2, C, N1])
        KP = R.sb("KP", [P, 2, 2, C, N1])
        St = R.sb("St", [P, 2, 2, C, N1 + 1])
        PR = R.sb("PR", [P, 2, C, N1])
        J, ND = R.sb("J", [P, 2, N1 + 1]), R.sb("ND", [P, 2, 2, C])
        W = R.sb("W", [P, 3 * P])
        share = R.sb("share", [P, T])
        Bc = R.sb("Bc", [P, 2, 2, C])
        SQc = R.sb("SQc", [P, 2, 2, C])
        th, ga, up, h = (R.sb(n, [P, 2, QT]) for n in ("th", "ga", "up", "h"))
        ps = R.psum()
        k_loaded, q_loaded = [R.sem(f"k_loaded{i}") for i in range(2)], [R.sem(f"q_loaded{i}") for i in range(2)]
        nd_made, x_made, tanh_done = ([R.sem(f"{n}{g}") for g in range(2)] for n in ("nd_made", "x_made", "tanh_done"))
        state_set, kp_made = R.sem("state_set"), R.sem("kp_made")
        beta_placed, sq_placed = R.sem("beta_placed"), R.sem("sq_placed")
        sq_multiplied, sq_summed = R.sem("sq_multiplied"), R.sem("sq_summed")
        w_loaded, up_done, taken, gate_made = (R.sem(n) for n in ("w_loaded", "up_done", "taken", "gate_made"))
        up_shared, h_ready, down_done = R.sem("up_shared"), R.sem("h_ready"), R.sem("down_done")
        block = ctx.enter_context(nc.Block())

        def wait(engine, sem, turn, per_turn, count):
            if not isinstance(turn, int) or turn * per_turn + count > 0:
                engine.wait_ge(sem, turn * per_turn + count)

        def over_turns(engine, emit):
            emit(0)
            with engine.Fori(1, TURNS - 1) as turn:
                emit(turn)
            emit(TURNS - 1)

        def first(turn):
            return isinstance(turn, int) and turn == 0

        def last(turn):
            return isinstance(turn, int) and turn == TURNS - 1

        @block.sync
        def _(sp):
            def keys(turn, c):
                for g in range(2):
                    wait(sp, x_made[g], turn, TURN, C * (c - 1))
                for g in range(2):
                    for q in range(4):
                        sp.dma_start(K[32 * q:32 * q + 32, c % 2, g, :, :].rearrange("p t c -> p (t c)"),
                                     S.KN[4 * g + q, bass.ds(turn * TURN + C * c, C), :].rearrange("t c -> (t c)").partition_broadcast(32)).then_inc(k_loaded[c % 2], 16)

            def queries(turn, c):
                wait(sp, sq_multiplied, turn, 4, 2 * (c - 1))
                for g in range(2):
                    for q in range(4):
                        sp.dma_start(Qb[32 * q:32 * q + 32, c % 2, g, :, :].rearrange("p t c -> p (t c)"),
                                     S.QN[4 * g + q, bass.ds(turn * TURN + C * c, C), :].rearrange("t c -> (t c)").partition_broadcast(32)).then_inc(q_loaded[c % 2], 16)

            def experts(turn):
                wait(sp, down_done, turn, 4, 0)
                pair = bass.ds(turn, 1)
                sp.dma_start(W[:, :], dram["experts"][pair, :, :].rearrange("a p c -> (a p) c")).then_inc(w_loaded, 16)
                for half in range(2):
                    row = S.ST[bass.ds(turn * 2 + half, 1), :].rearrange("a t -> (a t)")
                    sp.dma_start(share[64 * half:64 * half + 64, :], row.partition_broadcast(64)).then_inc(w_loaded, 16)

            def emit(turn):
                if first(turn):
                    keys(0, 0)
                    experts(0)
                    queries(0, 0)
                keys(turn, 1)
                queries(turn, 1)
                if not last(turn):
                    keys(turn, 2)
                    queries(turn, 2)
                experts(turn + 1)
            over_turns(sp, emit)

        @block.vector
        def _(dve):
            def step(turn, s, between):
                b, t = s // C, s % C
                pb, pt = (s - 1) // C % 2, (s - 1) % C
                if t == 0:
                    wait(dve, kp_made, turn, 4, 2 * (b + 1))
                for g in range(2):
                    wait(dve, tanh_done[g], turn, TURN, s)
                    nc.vector.scalar_tensor_tensor(J[:, g, :], St[:, pb, g, pt, :], 1.0, K[:, b, g, t, :], ALU.mult, ALU.mult,
                                                   accum_out=ND[:, b, g, t:t + 1]).then_inc(nd_made[g], 1)
                    between[g]()
                    wait(dve, nd_made[g], turn, TURN, s + 1)
                    nc.vector.scalar_tensor_tensor(ps[:, X_BANK + g, 0:N1], KP[:, b, g, t, :], ND[:, b, g, t:t + 1], St[:, pb, g, pt, 0:N1],
                                                   ALU.mult, ALU.subtract).then_inc(x_made[g], 1)

            def sum_piece(turn, c, n):
                if n == 0:
                    wait(dve, sq_multiplied, turn, 4, 2 * (c + 1))
                nc.vector.tensor_reduce(SQc[:, c, :, n:n + 1], PR[:, :, n:n + 1, :], AX.X, ALU.add).then_inc(sq_summed, 1)

            def gate(turn, c, n):
                if n == 0:
                    wait(dve, taken, turn, 4 * TAKES, TAKES * c + TAKES // 2 + 1)
                part = slice(QT // GATES * n, QT // GATES * (n + 1))
                nc.vector.scalar_tensor_tensor(ga[:, c % 2, part], th[:, c % 2, part], 1.0, ps[:, 0, part],
                                               ALU.add, ALU.mult).then_inc(gate_made, 1)

            def filling(turn, s, g):
                for c, at in enumerate(GATE_AT):
                    if at <= s < at + GATES // 2:
                        gate(turn, c, 2 * (s - at) + g)
                n = 2 * (s % C - SUM_AT) + g
                if 0 <= n < C and not (first(turn) and s < C):
                    if s < C:
                        sum_piece(turn - 1, 1, n)
                    else:
                        sum_piece(turn, 0, n)

            def emit(turn):
                if first(turn):
                    dve.wait_ge(state_set, 2)
                for s in range(TURN):
                    step(turn, s, [lambda: filling(turn, s, 0), lambda: filling(turn, s, 1)])
            over_turns(dve, emit)
            for n in range(C):
                sum_piece(TURNS - 1, 1, n)
            for c in range(4):
                for n in range(GATES):
                    gate(TURNS, c, n)
            dve.wait_ge(sq_summed, T)

        @block.scalar
        def _(act):
            def piece(turn, c, n):
                kind, quarter = divmod(n, 4)
                if n == 0:
                    wait(act, up_done, turn, 8, 2 * c + 2)
                elif n == 4:
                    wait(act, h_ready, turn, 4, c - 1)
                part = slice(P * quarter, P * (quarter + 1))
                nc.scalar.activation((th, up)[kind][:, c % 2, part], ps[:, kind, part], (ACT.Tanh, ACT.Copy)[kind],
                                     scale=(0.5, 1.0)[kind]).then_inc(taken, 1)

            def emit(turn):
                for s in range(TURN):
                    b, t = s // C, s % C
                    if t == 0:
                        if first(turn):
                            act.wait_ge(beta_placed, b + 1)
                        else:
                            wait(act, sq_multiplied, turn, 4, 2 * (b - 1))
                    for g in range(2):
                        wait(act, x_made[g], turn, TURN, s + 1)
                        nc.scalar.activation(St[:, b, g, t, 0:N1], ps[:, X_BANK + g, 0:N1], ACT.Tanh,
                                             scale=Bc[:, b, g, t:t + 1]).then_inc(tanh_done[g], 1)
                        for c, at in enumerate(TAKE_AT):
                            if at <= s < at + TAKES // 2:
                                piece(turn, c, 2 * (s - at) + g)
            over_turns(act, emit)
            for c in range(4):
                for n in range(TAKES):
                    piece(TURNS, c, n)
            for c in range(4):
                act.wait_ge(down_done, 4 * TURNS + c + 1)
                nc.scalar.activation(S.mixT[:, QT * c:QT * c + QT], ps[:, DOWN_BANK + c, :], ACT.Copy).then_inc(taken, 1)
            act.wait_ge(taken, 4 * TAKES * (TURNS + 1) + 4)

        @block.gpsimd
        def _(pool):
            def values(turn, c):
                for g in range(2):
                    wait(pool, x_made[g], turn, TURN, C * (c - 1) + 1)
                    nc.gpsimd.tensor_copy(St[:, c % 2, g, :, N1:N1 + 1], S.vT[:, g, bass.ds(turn * TURN + (C * c + 1), C)].unsqueeze(2))

            def keys_over_beta(turn, c):
                wait(pool, k_loaded[c % 2], turn, 128, 128 * (c // 2 + 1))
                for g in range(2):
                    wait(pool, x_made[g], turn, TURN, C * (c - 1))
                    rb = S.rb[:, g, bass.ds(turn * TURN + C * c, C)].unsqueeze(2).to_broadcast([P, C, N1])
                    nc.gpsimd.tensor_tensor(KP[:, c % 2, g, :, :], K[:, c % 2, g, :, 0:N1], rb, ALU.mult).then_inc(kp_made, 1)

            def betas(turn, c):
                for g in range(2):
                    wait(pool, tanh_done[g], turn, TURN, C * (c - 1))
                nc.gpsimd.tensor_copy(Bc[:, c % 2, :, :], S.beta[:, :, bass.ds(turn * TURN + C * c, C)]).then_inc(beta_placed, 1)

            def place_sums(turn, c):
                wait(pool, sq_summed, turn, TURN, C * (c + 1))
                nc.gpsimd.tensor_copy(SQ[:, :, bass.ds(turn * TURN + C * c, C)], SQc[:, c, :, :]).then_inc(sq_placed, 1)

            def times_queries(turn, c):
                wait(pool, q_loaded[c % 2], turn, 128, 128 * (c // 2 + 1))
                wait(pool, sq_summed, turn, TURN, C * c)
                for g in range(2):
                    wait(pool, tanh_done[g], turn, TURN, C * (c + 1))
                    nc.gpsimd.tensor_tensor(PR[:, g, :, :], St[:, c % 2, g, :, 0:N1], Qb[:, c % 2, g, :, :], ALU.mult).then_inc(sq_multiplied, 1)

            def hidden(turn, c):
                wait(pool, taken, turn, 4 * TAKES, TAKES * (c + 1))
                wait(pool, w_loaded, turn, 48, 48)
                nc.gpsimd.tensor_tensor(up[:, c % 2, :], up[:, c % 2, :], share[:, QT * c:QT * c + QT], ALU.mult).then_inc(up_shared, 1)
                wait(pool, up_shared, turn, 4, c + 1)
                wait(pool, gate_made, turn, 4 * GATES, GATES * (c + 1))
                wait(pool, down_done, turn, 4, c - 1)
                nc.gpsimd.tensor_tensor(h[:, c % 2, :], up[:, c % 2, :], ga[:, c % 2, :], ALU.mult).then_inc(h_ready, 1)

            def emit(turn):
                if first(turn):
                    nc.gpsimd.memset(St[:, 1, :, C - 1, 0:N1], 0.0).then_inc(state_set, 1)
                    nc.gpsimd.tensor_copy(St[:, 1, :, C - 1, N1:N1 + 1], S.vT[:, :, 0:1]).then_inc(state_set, 1)
                    values(0, 0)
                    betas(0, 0)
                    keys_over_beta(0, 0)
                values(turn, 1)
                betas(turn, 1)
                if not first(turn):
                    place_sums(turn - 1, 0)
                    times_queries(turn - 1, 1)
                keys_over_beta(turn, 1)
                hidden(turn, 0)
                hidden(turn, 1)
                if not last(turn):
                    values(turn, 2)
                    betas(turn, 2)
                if not first(turn):
                    place_sums(turn - 1, 1)
                times_queries(turn, 0)
                hidden(turn, 2)
                hidden(turn, 3)
                if not last(turn):
                    keys_over_beta(turn, 2)
            over_turns(pool, emit)
            place_sums(TURNS - 1, 0)
            times_queries(TURNS - 1, 1)
            place_sums(TURNS - 1, 1)
            pool.wait_ge(sq_placed, 2 * TURNS)
            for c in range(4):
                hidden(TURNS, c)

        @block.tensor
        def _(pe):
            def ups(turn, c):
                if c == 0:
                    wait(pe, w_loaded, turn, 48, 48)
                for k, read, each in ((1, taken, TAKES), (0, gate_made, GATES)):
                    wait(pe, read, turn, 4 * each, each * c)
                    nc.tensor.matmul(ps[:, k, :], W[:, P * k:P * k + P], S.mT[:, QT * c:QT * c + QT], start=True, stop=True).then_inc(up_done, 1)

            def downs(turn, c):
                wait(pe, h_ready, turn, 4, c + 1)
                nc.tensor.matmul(ps[:, DOWN_BANK + c, :], W[:, 2 * P:3 * P], h[:, c % 2, :], start=first(turn),
                                 stop=isinstance(turn, int) and turn == TURNS).then_inc(down_done, 1)

            def emit(turn):
                for c in range(4):
                    ups(turn, c)
                    if c:
                        downs(turn, c - 1)
                downs(turn, 3)
            over_turns(pe, emit)
            emit(TURNS)


def finish(nc, S, dram, out):
    with ExitStack() as ctx:
        R = Room(nc, ctx, "f")
        sg, WoutT = R.sb("sg", [P, 2, T]), R.sb("WoutT", [P, 2, D])
        gate, y = R.sb("gate", [P, NT, D]), R.sb("y", [P, NT, D])
        ps = R.psum()
        loaded, sig, out_made, turned, residual, silu, projected, times, result, stored = (
            R.sem(n) for n in ("loaded", "sig", "out_made", "turned", "residual", "silu", "projected", "times", "result", "stored"))
        squared = R.sem("squared")
        block = ctx.enter_context(nc.Block())

        @block.sync
        def _(sp):
            for g in range(2):
                sp.dma_start(WoutT[:, g, :], dram["WoutT"][g, :, :]).then_inc(loaded, 16)
            for n in range(4):
                sp.wait_ge(result, n + 1)
                for t in range(4 * n, 4 * n + 4):
                    sp.dma_start(out[t * P:(t + 1) * P, :], y[:, t, :]).then_inc(stored, 16)
            sp.wait_ge(stored, 16 * NT)

        @block.scalar
        def _(act):
            for g in range(2):
                nc.scalar.activation(sg[:, g, :], S.SQ[:, g, :], ACT.Silu).then_inc(sig, 1)
            for n in range(4):
                act.wait_ge(residual, n + 1)
                nc.scalar.activation(gate[:, 4 * n:4 * n + 4, :], gate[:, 4 * n:4 * n + 4, :], ACT.Silu).then_inc(silu, 1)

        @block.tensor
        def _(pe):
            for n in range(4):
                for j in range(4):
                    ins = nc.tensor.transpose(ps[:, n, j * P:(j + 1) * P], S.mixT[:, (4 * n + j) * P:(4 * n + j + 1) * P], S.ident[:, :])
                ins.then_inc(turned, 1)
            pe.wait_ge(loaded, 32)
            pe.wait_ge(out_made, 2)
            for n in range(4):
                for j in range(4):
                    t = 4 * n + j
                    for g in range(2):
                        ins = nc.tensor.matmul(ps[:, 4 + n, j * P:(j + 1) * P], sg[:, g, t * P:(t + 1) * P], WoutT[:, g, :], start=g == 0, stop=g == 1)
                ins.then_inc(projected, 1)

        @block.vector
        def _(dve):
            for g in range(2):
                dve.wait_ge(sig, g + 1)
                nc.vector.tensor_tensor(sg[:, g, :], sg[:, g, :], S.SQ[:, g, :], ALU.mult).then_inc(out_made, 1)
            for n in range(4):
                dve.wait_ge(turned, n + 1)
                nc.vector.tensor_tensor(gate[:, 4 * n:4 * n + 4, :], ps[:, n, :].rearrange("p (j d) -> p j d", d=D), S.xn[:, 4 * n:4 * n + 4, :], ALU.add).then_inc(residual, 1)
            for n in range(4):
                part = slice(4 * n, 4 * n + 4)
                dve.wait_ge(silu, n + 1)
                dve.wait_ge(projected, n + 1)
                nc.vector.tensor_tensor(y[:, part, :], ps[:, 4 + n, :].rearrange("p (j d) -> p j d", d=D), gate[:, part, :], ALU.mult).then_inc(times, 1)
                dve.wait_ge(times, n + 1)
                nc.vector.tensor_tensor(y[:, part, :], y[:, part, :], S.x1[:, part, :], ALU.add).then_inc(result, 1)


def build_program(nc, dram, out, upto=99):
    ctx = ExitStack()
    with ctx:
        R = Room(nc, ctx, "s")
        S = Shared()
        S.scale_f = float(np.float32(1.0) / np.sqrt(np.float32(32.0)))
        S.KD, S.QD = nc.dram_tensor("KD", [NQ, 3, 2 * P, T], BF16).ap(), nc.dram_tensor("QD", [3, 3, 2 * P, T], BF16).ap()
        S.KDF, S.QDF = nc.dram_tensor("KDF", [3, 32, T], BF16).ap(), nc.dram_tensor("QDF", [3, P, T], BF16).ap()
        S.GD = nc.dram_tensor("GD", [16, P, GW], F32).ap()
        S.scale = float(np.float32(1.0) / np.sqrt(np.float32(8.0)))
        S.ident, S.bv, S.bo = R.sb("ident", [P, P]), R.sb("bv", [P, D]), R.sb("bo", [P, D])
        S.selo = R.sb("selo", [P, 32])
        S.spread = R.sb("spread", [P, P], BF16)
        S.rbias = R.sb("rbias", [P, 8])
        S.g, S.cols, S.dwb = R.sb("g", [P, 3]), R.sb("cols", [P, 10]), R.sb("dwb", [P, 2, 32])
        S.xn, S.xnT = R.sb("xn", [P, NT, D]), R.sb("xnT", [P, T])
        S.x1 = S.xnT[:, :].rearrange("p (t d) -> p t d", d=D)
        constants(nc, S, dram)
        with ExitStack() as attn:
            A = Room(nc, attn, "a")
            S.Vp, S.Vcp = A.sb("Vp", [P, NT, 16, 32]), A.sb("Vcp", [P, NT, 33])
            with ExitStack() as proj:
                B = Room(nc, proj, "q")
                S.Q2, S.K2 = B.sb("Q2", [P, 2, T]), B.sb("K2", [P, 2, T])
                S.QF, S.KF = B.sb("QF", [P, T]), B.sb("KF", [P, T])
                prepare(nc, S, dram)
                if upto < 2: return
                pieces(nc, S)
            S.AO, S.AOF = A.sb("AO", [P, NT, D]), A.sb("AOF", [P, NT, D])
            if upto < 3: return
            if upto != 4: attention(nc, S, Attention(16, 8, 32, True))
            attention(nc, S, Attention(4, 32, 32, False))
            if upto < 5: return
            mixture0(nc, S, dram)
        if upto < 6: return
        S.KN, S.QN = nc.dram_tensor("KN", [H1, T, N1 + 1], F32).ap(), nc.dram_tensor("QN", [H1, T, N1], F32).ap()
        S.ST = nc.dram_tensor("ST", [E1 + 2, T], F32).ap()
        S.vT, S.beta, S.rb = R.sb("vT", [P, 2, T + 1]), R.sb("beta", [P, 2, T]), R.sb("rb", [P, 2, T])
        S.mT = R.sb("mT", [P, T])
        prepare1(nc, S, dram)
        if upto < 7: return
        S.SQ = R.sb("SQ", [P, 2, T])
        S.mixT = S.mT
        recurrence(nc, S, dram)
        finish(nc, S, dram, out)


def layout(i):
    a = {}
    a["x"] = i["L0_attn_x"][0]
    for n in ("Wq", "Wk", "Wv", "Wo"):
        a[n + "T"] = i[f"L0_attn_{n}"].T
    for n in ("bq", "bk", "bv", "bo"):
        a[n] = i[f"L0_attn_{n}"]
    a["decay"], a["mix"] = i["L0_attn_decay_params"].reshape(-1), i["L0_attn_mix_weights"].reshape(-1)
    a["fWqT"], a["WkcT"], a["WvcT"], a["fWoT"] = (i[f"L0_ffn_{n}"].T for n in ("Wq", "Wkc", "Wvc", "Wo"))
    a["g"] = np.stack([i["L0_ffn_g1"], i["L0_ffn_g2"], i["L1_ffn_rms_w"]], axis=1)
    a["WrT"], a["rb"] = i["L0_ffn_Wr"].T, i["L0_ffn_expert_bias"]
    for n in ("W1", "W3", "W2"):
        a["e" + n] = np.concatenate([i[f"L0_ffn_e{n}"], i[f"L0_ffn_s{n}"][None]]).transpose(0, 2, 1)
    a["WinT"] = i["L1_attn_W_in"].T
    for n in ("k", "q", "v"):
        a[f"rW{n}T"] = i[f"L1_attn_W_{n}"].T
    a["rWbT"], a["bbeta"] = i["L1_attn_W_beta"].T, i["L1_attn_b_beta"].reshape(2, P).T
    a["WoutT"] = i["L1_attn_W_out"].T.reshape(2, P, D)
    a["gateT"] = i["L1_ffn_gate_w"].T
    w13, empty = i["L1_ffn_w13"].reshape(E1 // 2, 2, D, 2, I1), np.zeros((D, I1), i["L1_ffn_w13"].dtype)
    halves = [np.concatenate([w13[:, 0, :, k], w13[:, 1, :, k]], axis=2) for k in range(2)]
    pairs = np.concatenate(halves + [i["L1_ffn_w2"].reshape(E1 // 2, P, D)], axis=2)
    last = np.concatenate([i["L1_ffn_sw_gate"], empty, i["L1_ffn_sw_up"], empty,
                           np.concatenate([i["L1_ffn_sw_down"], empty.T], axis=0)], axis=1)
    a["experts"] = np.concatenate([pairs, last[None]])
    return {k: np.ascontiguousarray(v) for k, v in a.items()}


def kernel(**inputs):
    import concourse.bacc as bacc
    from concourse.bass_utils import run_bass_kernel_spmd

    arrays = layout({k: np.asarray(v) for k, v in inputs.items()})
    nc = bacc.Bacc("TRN2", target_bir_lowering=False, num_devices=1)
    dram = {n: nc.dram_tensor(f"in_{n}", a.shape, mybir.dt.from_np(a.dtype), kind="ExternalInput").ap() for n, a in arrays.items()}
    shape = inputs["L0_attn_x"].shape
    out = nc.dram_tensor("out", shape, F32, kind="ExternalOutput").ap()
    build_program(nc, dram, out[0])
    r = run_bass_kernel_spmd(nc, [{f"in_{n}": a for n, a in arrays.items()}], core_ids=[0])
    return r.results[0]["out"]
```
